# Optimizing a Trainium2 kernel written in Bass

```python
import numpy as np
import jax
import jax.numpy as jnp

def _softmax(x, axis=-1):
    return jax.nn.softmax(x, axis=axis)
def _gelu(x):
    return jax.nn.gelu(x, approximate=True)
def _silu(x):
    return jax.nn.silu(x)
def _sigmoid(x):
    return jax.nn.sigmoid(x)
def _layernorm(x, axis=-1, eps=1e-5):
    m = jnp.mean(x, axis=axis, keepdims=True)
    v = jnp.var(x, axis=axis, keepdims=True)
    return (x - m) / jnp.sqrt(v + eps)
def _scatter_add(tgt, idx, src, axis=0):
    return tgt.at[idx].add(src)
def _segment_sum(src, seg, n):
    return jax.ops.segment_sum(src, seg, n)

kernel_name = 'mk_conv_seq_d2_conv_nchw64_5e7817'

def setup_inputs(seed: int = 0):
    np.random.seed(seed)
    _w = jnp.asarray
    def _rec_inputs():
        import jax
        import jax.numpy as jnp
        _gk = jax.random.key(seed)
        x = -0.0003929 + 0.9999 * jax.random.normal(jax.random.fold_in(_gk, 1), (4, 64, 256, 256), jnp.float32)
        return x
    x = _rec_inputs()
    def _L0_conv_setup():
        import jax, jax.numpy as jnp
        import numpy as np
        B, DIM, H, W = (4, 64, 256, 256)
        HEADS = 4
        P = 8

        def _conv1x1(x, w, b=None):
            y = jnp.einsum('bchw,oc->bohw', x, w)
            return y if b is None else y + b[None, :, None, None]

        def _dwconv(x, k):
            return jax.lax.conv_general_dilated(x, k, (1, 1), 'SAME', feature_group_count=x.shape[1], dimension_numbers=('NCHW', 'OIHW', 'NCHW'))

        def _layernorm(x, w, b):
            mu = x.mean(axis=1, keepdims=True)
            var = x.var(axis=1, keepdims=True)
            return (x - mu) / jnp.sqrt(var + 1e-05) * w[None, :, None, None] + b[None, :, None, None]

        def _lgce(x, pre_w, pre_b, post_w, post_b, m1w, m1b, m2w, m2b, spw, spb):
            res = x
            x = _conv1x1(x, pre_w, pre_b)
            b, C, Hh, Ww = x.shape
            G = m1w.shape[0]
            cg = C // G
            xg = x.reshape(b, G, cg, Hh, Ww)
            pooled = xg.mean(axis=(3, 4))
            h1 = jax.nn.relu(jnp.einsum('bgc,ghc->bgh', pooled, m1w) + m1b[None])
            cw = jax.nn.sigmoid(jnp.einsum('bgh,gch->bgc', h1, m2w) + m2b[None])
            xa = xg * cw[:, :, :, None, None]
            sw = jax.nn.sigmoid(jnp.einsum('bgchw,goc->bgohw', xa, spw) + spb[None, :, :, None, None])
            resp = jax.nn.sigmoid(xa * sw)
            thr = resp.mean(axis=(2, 3, 4), keepdims=True)
            mask = jnp.where(resp > thr, jnp.ones_like(resp), resp)
            x = (xg * mask).reshape(b, C, Hh, Ww)
            x = _conv1x1(x, post_w, post_b)
            return x + res

        def _sgsa(x, in_proj_w, qkv_w, qkv_dw, out_proj_w, temperature, attn_scales, gate_w1, gate_b1, gate_w2, gate_b2, lgce_pre_w, lgce_pre_b, lgce_post_w, lgce_post_b, cbam_m1w, cbam_m1b, cbam_m2w, cbam_m2b, cbam_spw, cbam_spb):
            b, C, Hh, Ww = x.shape
            proj = _conv1x1(x, in_proj_w)
            local, glob = jnp.split(proj, 2, axis=1)
            local = _lgce(local, lgce_pre_w, lgce_pre_b, lgce_post_w, lgce_post_b, cbam_m1w, cbam_m1b, cbam_m2w, cbam_m2b, cbam_spw, cbam_spb)
            qkv = _dwconv(_conv1x1(glob, qkv_w), qkv_dw)
            q, k, v = jnp.split(qkv, 3, axis=1)
            hd = lambda t: t.reshape(b, HEADS, -1, Hh * Ww)
            q, k, v = (hd(q), hd(k), hd(v))
            l2n = lambda t: t / jnp.maximum(jnp.linalg.norm(t, axis=-1, keepdims=True), 1e-12)
            q, k = (l2n(q), l2n(k))
            c = q.shape[2]
            g = jax.nn.sigmoid(_conv1x1(jax.nn.relu(_conv1x1(glob, gate_w1, gate_b1)), gate_w2, gate_b2))
            dk = jnp.clip(jnp.floor(c * g.mean()), 1, c).astype(jnp.int32)
            attn = jnp.einsum('bhcn,bhdn->bhcd', q, k) * temperature[None]
            sorted_desc = -jnp.sort(-attn, axis=-1)
            kth = jnp.take(sorted_desc, dk - 1, axis=-1)
            attn = jnp.where(attn >= kth[..., None], attn, -jnp.inf)
            attn = jax.nn.softmax(attn, axis=-1)
            out = jnp.einsum('bhcd,bhdn->bhcn', attn, v) * attn_scales.sum()
            out = out.reshape(b, C // 2, Hh, Ww)
            fused = jnp.concatenate([out, local], axis=1)
            return _conv1x1(fused, out_proj_w)

        def _mffn(x, in_w, dw3, dw5, out_w, fW):
            t = _conv1x1(x, in_w)
            x1, x2 = (t[:, :192], t[:, 192:])
            d1 = _dwconv(x1, dw3)
            x_gate, x1_2 = (d1[:, :128], d1[:, 128:])
            x2 = _dwconv(x2, dw5)
            y = jax.nn.gelu(x_gate, approximate=False) * jnp.concatenate([x1_2, x2], axis=1)
            y = _conv1x1(y, out_w)
            b, c, Hh, Ww = y.shape
            p = y.reshape(b, c, Hh // P, P, Ww // P, P).transpose(0, 1, 2, 4, 3, 5)
            f = jnp.fft.rfft2(p) * fW
            p = jnp.fft.irfft2(f, s=(P, P))
            return p.transpose(0, 1, 2, 4, 3, 5).reshape(b, c, Hh, Ww)

        def _forward(x, ln1_w, ln1_b, in_proj_w, qkv_w, qkv_dw, out_proj_w, temperature, attn_scales, gate_w1, gate_b1, gate_w2, gate_b2, lgce_pre_w, lgce_pre_b, lgce_post_w, lgce_post_b, cbam_m1w, cbam_m1b, cbam_m2w, cbam_m2b, cbam_spw, cbam_spb, ln2_w, ln2_b, ffn_in_w, dw3_w, dw5_w, ffn_out_w, fft_W):
            x = x + _sgsa(_layernorm(x, ln1_w, ln1_b), in_proj_w, qkv_w, qkv_dw, out_proj_w, temperature, attn_scales, gate_w1, gate_b1, gate_w2, gate_b2, lgce_pre_w, lgce_pre_b, lgce_post_w, lgce_post_b, cbam_m1w, cbam_m1b, cbam_m2w, cbam_m2b, cbam_spw, cbam_spb)
            x = x + _mffn(_layernorm(x, ln2_w, ln2_b), ffn_in_w, dw3_w, dw5_w, ffn_out_w, fft_W)
            return x
        key = jax.random.key(seed)
        ks = jax.random.split(key, 20)
        r = lambda k, s: jax.random.normal(k, s, dtype=jnp.float32) * 0.02
        return {'x': jax.random.normal(ks[0], (B, DIM, H, W), dtype=jnp.float32), 'ln1_w': jnp.ones((DIM,), jnp.float32), 'ln1_b': jnp.zeros((DIM,), jnp.float32), 'in_proj_w': r(ks[1], (DIM, DIM)), 'qkv_w': r(ks[2], (DIM // 2 * 3, DIM // 2)), 'qkv_dw': r(ks[3], (DIM // 2 * 3, 1, 3, 3)), 'out_proj_w': r(ks[4], (DIM, DIM)), 'temperature': jnp.ones((HEADS, 1, 1), jnp.float32), 'attn_scales': jnp.full((4,), 0.2, jnp.float32), 'gate_w1': r(ks[5], (DIM // 4, DIM // 2)), 'gate_b1': jnp.zeros((DIM // 4,), jnp.float32), 'gate_w2': r(ks[6], (1, DIM // 4)), 'gate_b2': jnp.zeros((1,), jnp.float32), 'lgce_pre_w': r(ks[7], (DIM // 2, DIM // 2)), 'lgce_pre_b': jnp.zeros((DIM // 2,), jnp.float32), 'lgce_post_w': r(ks[8], (DIM // 2, DIM // 2)), 'lgce_post_b': jnp.zeros((DIM // 2,), jnp.float32), 'cbam_m1w': r(ks[9], (8, 1, 4)), 'cbam_m1b': jnp.zeros((8, 1), jnp.float32), 'cbam_m2w': r(ks[10], (8, 4, 1)), 'cbam_m2b': jnp.zeros((8, 4), jnp.float32), 'cbam_spw': r(ks[11], (8, 1, 4)), 'cbam_spb': jnp.zeros((8, 1), jnp.float32), 'ln2_w': jnp.ones((DIM,), jnp.float32), 'ln2_b': jnp.zeros((DIM,), jnp.float32), 'ffn_in_w': r(ks[12], (256, DIM)), 'dw3_w': r(ks[13], (192, 1, 3, 3)), 'dw5_w': r(ks[14], (64, 1, 5, 5)), 'ffn_out_w': r(ks[15], (DIM, 128)), 'fft_W': jnp.ones((DIM, 1, 1, P, P // 2 + 1), jnp.float32)}
    _L0_conv_all = _L0_conv_setup()
    _L0_conv_in = {k: v for k, v in _L0_conv_all.items() if k in ('ln1_w', 'ln1_b', 'in_proj_w', 'qkv_w', 'qkv_dw', 'out_proj_w', 'temperature', 'attn_scales', 'gate_w1', 'gate_b1', 'gate_w2', 'gate_b2', 'lgce_pre_w', 'lgce_pre_b', 'lgce_post_w', 'lgce_post_b', 'cbam_m1w', 'cbam_m1b', 'cbam_m2w', 'cbam_m2b', 'cbam_spw', 'cbam_spb', 'ln2_w', 'ln2_b', 'ffn_in_w', 'dw3_w', 'dw5_w', 'ffn_out_w', 'fft_W', )}
    del _L0_conv_all

    def _L1_conv_setup():
        import jax, jax.numpy as jnp
        import numpy as np
        E = 64
        H = 4
        DQK = 1
        B = 2
        R = 1225
        C = 512
        EPS_LN = 1e-05

        def _ln(x, g, b):
            m = x.mean(-1, keepdims=True)
            v = jnp.mean((x - m) ** 2, -1, keepdims=True)
            return (x - m) / jnp.sqrt(v + EPS_LN) * g + b

        def _lin_attn(x, wq, bq, wk, bk, wv, bv, wo, bo):
            b_, r_, c_, e_ = x.shape
            dv = e_ // H
            q = (x @ wq.T + bq).reshape(b_, r_, c_, H, DQK).swapaxes(2, 3)
            k = (x @ wk.T + bk).reshape(b_, r_, c_, H, DQK).swapaxes(2, 3)
            v = (x @ wv.T + bv).reshape(b_, r_, c_, H, dv).swapaxes(2, 3)
            q = jax.nn.elu(q) + 1.0
            k = jax.nn.elu(k) + 1.0
            q = q / q.mean(axis=3, keepdims=True)
            k = k / k.sum(axis=3, keepdims=True)
            ktv = jnp.einsum('brhcd,brhce->brhde', k, v)
            o = jnp.einsum('brhcd,brhde->brhce', q, ktv)
            o = o.swapaxes(2, 3).reshape(b_, r_, c_, e_)
            return o @ wo.T + bo
        key = jax.random.key(seed)
        ks = iter(jax.random.split(key, 32))

        def w(shape, s=0.05):
            return jax.random.normal(next(ks), shape, jnp.float32) * s
        inp = {'x': jax.random.normal(next(ks), (B, E, R, C), jnp.float32)}
        for p in ('row', 'col'):
            inp[p + '_wq'] = w((H, E))
            inp[p + '_bq'] = jnp.zeros((H,), jnp.float32)
            inp[p + '_wk'] = w((H, E))
            inp[p + '_bk'] = jnp.zeros((H,), jnp.float32)
            inp[p + '_wv'] = w((E, E))
            inp[p + '_bv'] = jnp.zeros((E,), jnp.float32)
            inp[p + '_wo'] = w((E, E))
            inp[p + '_bo'] = jnp.zeros((E,), jnp.float32)
        for p in ('rn', 'cn', 'fn'):
            inp[p + '_g'] = jnp.ones((E,), jnp.float32)
            inp[p + '_b'] = jnp.zeros((E,), jnp.float32)
        inp['w1'] = w((4 * E, E))
        inp['b1'] = jnp.zeros((4 * E,), jnp.float32)
        inp['w2'] = w((E, 4 * E))
        inp['b2'] = jnp.zeros((E,), jnp.float32)
        return inp
    _L1_conv_all = _L1_conv_setup()
    _L1_conv_in = {k: v for k, v in _L1_conv_all.items() if k in ('row_wq', 'row_bq', 'row_wk', 'row_bk', 'row_wv', 'row_bv', 'row_wo', 'row_bo', 'col_wq', 'col_bq', 'col_wk', 'col_bk', 'col_wv', 'col_bv', 'col_wo', 'col_bo', 'rn_g', 'rn_b', 'cn_g', 'cn_b', 'fn_g', 'fn_b', 'w1', 'b1', 'w2', 'b2', )}
    del _L1_conv_all

    return {
        "x": x,
        "L0_conv_ln1_w": _L0_conv_in["ln1_w"],
        "L0_conv_ln1_b": _L0_conv_in["ln1_b"],
        "L0_conv_in_proj_w": _L0_conv_in["in_proj_w"],
        "L0_conv_qkv_w": _L0_conv_in["qkv_w"],
        "L0_conv_qkv_dw": _L0_conv_in["qkv_dw"],
        "L0_conv_out_proj_w": _L0_conv_in["out_proj_w"],
        "L0_conv_temperature": _L0_conv_in["temperature"],
        "L0_conv_attn_scales": _L0_conv_in["attn_scales"],
        "L0_conv_gate_w1": _L0_conv_in["gate_w1"],
        "L0_conv_gate_b1": _L0_conv_in["gate_b1"],
        "L0_conv_gate_w2": _L0_conv_in["gate_w2"],
        "L0_conv_gate_b2": _L0_conv_in["gate_b2"],
        "L0_conv_lgce_pre_w": _L0_conv_in["lgce_pre_w"],
        "L0_conv_lgce_pre_b": _L0_conv_in["lgce_pre_b"],
        "L0_conv_lgce_post_w": _L0_conv_in["lgce_post_w"],
        "L0_conv_lgce_post_b": _L0_conv_in["lgce_post_b"],
        "L0_conv_cbam_m1w": _L0_conv_in["cbam_m1w"],
        "L0_conv_cbam_m1b": _L0_conv_in["cbam_m1b"],
        "L0_conv_cbam_m2w": _L0_conv_in["cbam_m2w"],
        "L0_conv_cbam_m2b": _L0_conv_in["cbam_m2b"],
        "L0_conv_cbam_spw": _L0_conv_in["cbam_spw"],
        "L0_conv_cbam_spb": _L0_conv_in["cbam_spb"],
        "L0_conv_ln2_w": _L0_conv_in["ln2_w"],
        "L0_conv_ln2_b": _L0_conv_in["ln2_b"],
        "L0_conv_ffn_in_w": _L0_conv_in["ffn_in_w"],
        "L0_conv_dw3_w": _L0_conv_in["dw3_w"],
        "L0_conv_dw5_w": _L0_conv_in["dw5_w"],
        "L0_conv_ffn_out_w": _L0_conv_in["ffn_out_w"],
        "L0_conv_fft_W": _L0_conv_in["fft_W"],
        "L1_conv_row_wq": _L1_conv_in["row_wq"],
        "L1_conv_row_bq": _L1_conv_in["row_bq"],
        "L1_conv_row_wk": _L1_conv_in["row_wk"],
        "L1_conv_row_bk": _L1_conv_in["row_bk"],
        "L1_conv_row_wv": _L1_conv_in["row_wv"],
        "L1_conv_row_bv": _L1_conv_in["row_bv"],
        "L1_conv_row_wo": _L1_conv_in["row_wo"],
        "L1_conv_row_bo": _L1_conv_in["row_bo"],
        "L1_conv_col_wq": _L1_conv_in["col_wq"],
        "L1_conv_col_bq": _L1_conv_in["col_bq"],
        "L1_conv_col_wk": _L1_conv_in["col_wk"],
        "L1_conv_col_bk": _L1_conv_in["col_bk"],
        "L1_conv_col_wv": _L1_conv_in["col_wv"],
        "L1_conv_col_bv": _L1_conv_in["col_bv"],
        "L1_conv_col_wo": _L1_conv_in["col_wo"],
        "L1_conv_col_bo": _L1_conv_in["col_bo"],
        "L1_conv_rn_g": _L1_conv_in["rn_g"],
        "L1_conv_rn_b": _L1_conv_in["rn_b"],
        "L1_conv_cn_g": _L1_conv_in["cn_g"],
        "L1_conv_cn_b": _L1_conv_in["cn_b"],
        "L1_conv_fn_g": _L1_conv_in["fn_g"],
        "L1_conv_fn_b": _L1_conv_in["fn_b"],
        "L1_conv_w1": _L1_conv_in["w1"],
        "L1_conv_b1": _L1_conv_in["b1"],
        "L1_conv_w2": _L1_conv_in["w2"],
        "L1_conv_b2": _L1_conv_in["b2"],
    }

def reference(x, L0_conv_ln1_w, L0_conv_ln1_b, L0_conv_in_proj_w, L0_conv_qkv_w, L0_conv_qkv_dw, L0_conv_out_proj_w, L0_conv_temperature, L0_conv_attn_scales, L0_conv_gate_w1, L0_conv_gate_b1, L0_conv_gate_w2, L0_conv_gate_b2, L0_conv_lgce_pre_w, L0_conv_lgce_pre_b, L0_conv_lgce_post_w, L0_conv_lgce_post_b, L0_conv_cbam_m1w, L0_conv_cbam_m1b, L0_conv_cbam_m2w, L0_conv_cbam_m2b, L0_conv_cbam_spw, L0_conv_cbam_spb, L0_conv_ln2_w, L0_conv_ln2_b, L0_conv_ffn_in_w, L0_conv_dw3_w, L0_conv_dw5_w, L0_conv_ffn_out_w, L0_conv_fft_W, L1_conv_row_wq, L1_conv_row_bq, L1_conv_row_wk, L1_conv_row_bk, L1_conv_row_wv, L1_conv_row_bv, L1_conv_row_wo, L1_conv_row_bo, L1_conv_col_wq, L1_conv_col_bq, L1_conv_col_wk, L1_conv_col_bk, L1_conv_col_wv, L1_conv_col_bv, L1_conv_col_wo, L1_conv_col_bo, L1_conv_rn_g, L1_conv_rn_b, L1_conv_cn_g, L1_conv_cn_b, L1_conv_fn_g, L1_conv_fn_b, L1_conv_w1, L1_conv_b1, L1_conv_w2, L1_conv_b2):
    import jax
    import jax.numpy as jnp
    def _L0_conv_ref(x, ln1_w, ln1_b, in_proj_w, qkv_w, qkv_dw, out_proj_w, temperature, attn_scales, gate_w1, gate_b1, gate_w2, gate_b2, lgce_pre_w, lgce_pre_b, lgce_post_w, lgce_post_b, cbam_m1w, cbam_m1b, cbam_m2w, cbam_m2b, cbam_spw, cbam_spb, ln2_w, ln2_b, ffn_in_w, dw3_w, dw5_w, ffn_out_w, fft_W):
        import jax, jax.numpy as jnp
        import numpy as np
        B, DIM, H, W = (4, 64, 256, 256)
        HEADS = 4
        P = 8

        def _conv1x1(x, w, b=None):
            y = jnp.einsum('bchw,oc->bohw', x, w)
            return y if b is None else y + b[None, :, None, None]

        def _dwconv(x, k):
            return jax.lax.conv_general_dilated(x, k, (1, 1), 'SAME', feature_group_count=x.shape[1], dimension_numbers=('NCHW', 'OIHW', 'NCHW'))

        def _layernorm(x, w, b):
            mu = x.mean(axis=1, keepdims=True)
            var = x.var(axis=1, keepdims=True)
            return (x - mu) / jnp.sqrt(var + 1e-05) * w[None, :, None, None] + b[None, :, None, None]

        def _lgce(x, pre_w, pre_b, post_w, post_b, m1w, m1b, m2w, m2b, spw, spb):
            res = x
            x = _conv1x1(x, pre_w, pre_b)
            b, C, Hh, Ww = x.shape
            G = m1w.shape[0]
            cg = C // G
            xg = x.reshape(b, G, cg, Hh, Ww)
            pooled = xg.mean(axis=(3, 4))
            h1 = jax.nn.relu(jnp.einsum('bgc,ghc->bgh', pooled, m1w) + m1b[None])
            cw = jax.nn.sigmoid(jnp.einsum('bgh,gch->bgc', h1, m2w) + m2b[None])
            xa = xg * cw[:, :, :, None, None]
            sw = jax.nn.sigmoid(jnp.einsum('bgchw,goc->bgohw', xa, spw) + spb[None, :, :, None, None])
            resp = jax.nn.sigmoid(xa * sw)
            thr = resp.mean(axis=(2, 3, 4), keepdims=True)
            mask = jnp.where(resp > thr, jnp.ones_like(resp), resp)
            x = (xg * mask).reshape(b, C, Hh, Ww)
            x = _conv1x1(x, post_w, post_b)
            return x + res

        def _sgsa(x, in_proj_w, qkv_w, qkv_dw, out_proj_w, temperature, attn_scales, gate_w1, gate_b1, gate_w2, gate_b2, lgce_pre_w, lgce_pre_b, lgce_post_w, lgce_post_b, cbam_m1w, cbam_m1b, cbam_m2w, cbam_m2b, cbam_spw, cbam_spb):
            b, C, Hh, Ww = x.shape
            proj = _conv1x1(x, in_proj_w)
            local, glob = jnp.split(proj, 2, axis=1)
            local = _lgce(local, lgce_pre_w, lgce_pre_b, lgce_post_w, lgce_post_b, cbam_m1w, cbam_m1b, cbam_m2w, cbam_m2b, cbam_spw, cbam_spb)
            qkv = _dwconv(_conv1x1(glob, qkv_w), qkv_dw)
            q, k, v = jnp.split(qkv, 3, axis=1)
            hd = lambda t: t.reshape(b, HEADS, -1, Hh * Ww)
            q, k, v = (hd(q), hd(k), hd(v))
            l2n = lambda t: t / jnp.maximum(jnp.linalg.norm(t, axis=-1, keepdims=True), 1e-12)
            q, k = (l2n(q), l2n(k))
            c = q.shape[2]
            g = jax.nn.sigmoid(_conv1x1(jax.nn.relu(_conv1x1(glob, gate_w1, gate_b1)), gate_w2, gate_b2))
            dk = jnp.clip(jnp.floor(c * g.mean()), 1, c).astype(jnp.int32)
            attn = jnp.einsum('bhcn,bhdn->bhcd', q, k) * temperature[None]
            sorted_desc = -jnp.sort(-attn, axis=-1)
            kth = jnp.take(sorted_desc, dk - 1, axis=-1)
            attn = jnp.where(attn >= kth[..., None], attn, -jnp.inf)
            attn = jax.nn.softmax(attn, axis=-1)
            out = jnp.einsum('bhcd,bhdn->bhcn', attn, v) * attn_scales.sum()
            out = out.reshape(b, C // 2, Hh, Ww)
            fused = jnp.concatenate([out, local], axis=1)
            return _conv1x1(fused, out_proj_w)

        def _mffn(x, in_w, dw3, dw5, out_w, fW):
            t = _conv1x1(x, in_w)
            x1, x2 = (t[:, :192], t[:, 192:])
            d1 = _dwconv(x1, dw3)
            x_gate, x1_2 = (d1[:, :128], d1[:, 128:])
            x2 = _dwconv(x2, dw5)
            y = jax.nn.gelu(x_gate, approximate=False) * jnp.concatenate([x1_2, x2], axis=1)
            y = _conv1x1(y, out_w)
            b, c, Hh, Ww = y.shape
            p = y.reshape(b, c, Hh // P, P, Ww // P, P).transpose(0, 1, 2, 4, 3, 5)
            f = jnp.fft.rfft2(p) * fW
            p = jnp.fft.irfft2(f, s=(P, P))
            return p.transpose(0, 1, 2, 4, 3, 5).reshape(b, c, Hh, Ww)

        def _forward(x, ln1_w, ln1_b, in_proj_w, qkv_w, qkv_dw, out_proj_w, temperature, attn_scales, gate_w1, gate_b1, gate_w2, gate_b2, lgce_pre_w, lgce_pre_b, lgce_post_w, lgce_post_b, cbam_m1w, cbam_m1b, cbam_m2w, cbam_m2b, cbam_spw, cbam_spb, ln2_w, ln2_b, ffn_in_w, dw3_w, dw5_w, ffn_out_w, fft_W):
            x = x + _sgsa(_layernorm(x, ln1_w, ln1_b), in_proj_w, qkv_w, qkv_dw, out_proj_w, temperature, attn_scales, gate_w1, gate_b1, gate_w2, gate_b2, lgce_pre_w, lgce_pre_b, lgce_post_w, lgce_post_b, cbam_m1w, cbam_m1b, cbam_m2w, cbam_m2b, cbam_spw, cbam_spb)
            x = x + _mffn(_layernorm(x, ln2_w, ln2_b), ffn_in_w, dw3_w, dw5_w, ffn_out_w, fft_W)
            return x
        return _forward(x, ln1_w, ln1_b, in_proj_w, qkv_w, qkv_dw, out_proj_w, temperature, attn_scales, gate_w1, gate_b1, gate_w2, gate_b2, lgce_pre_w, lgce_pre_b, lgce_post_w, lgce_post_b, cbam_m1w, cbam_m1b, cbam_m2w, cbam_m2b, cbam_spw, cbam_spb, ln2_w, ln2_b, ffn_in_w, dw3_w, dw5_w, ffn_out_w, fft_W)

    def _L1_conv_ref(x, row_wq, row_bq, row_wk, row_bk, row_wv, row_bv, row_wo, row_bo, col_wq, col_bq, col_wk, col_bk, col_wv, col_bv, col_wo, col_bo, rn_g, rn_b, cn_g, cn_b, fn_g, fn_b, w1, b1, w2, b2):
        import jax, jax.numpy as jnp
        import numpy as np
        E = 64
        H = 4
        DQK = 1
        B = 2
        R = 1225
        C = 512
        EPS_LN = 1e-05

        def _ln(x, g, b):
            m = x.mean(-1, keepdims=True)
            v = jnp.mean((x - m) ** 2, -1, keepdims=True)
            return (x - m) / jnp.sqrt(v + EPS_LN) * g + b

        def _lin_attn(x, wq, bq, wk, bk, wv, bv, wo, bo):
            b_, r_, c_, e_ = x.shape
            dv = e_ // H
            q = (x @ wq.T + bq).reshape(b_, r_, c_, H, DQK).swapaxes(2, 3)
            k = (x @ wk.T + bk).reshape(b_, r_, c_, H, DQK).swapaxes(2, 3)
            v = (x @ wv.T + bv).reshape(b_, r_, c_, H, dv).swapaxes(2, 3)
            q = jax.nn.elu(q) + 1.0
            k = jax.nn.elu(k) + 1.0
            q = q / q.mean(axis=3, keepdims=True)
            k = k / k.sum(axis=3, keepdims=True)
            ktv = jnp.einsum('brhcd,brhce->brhde', k, v)
            o = jnp.einsum('brhcd,brhde->brhce', q, ktv)
            o = o.swapaxes(2, 3).reshape(b_, r_, c_, e_)
            return o @ wo.T + bo
        xe = jnp.moveaxis(x, 1, -1)
        h = xe + _lin_attn(_ln(xe, rn_g, rn_b), row_wq, row_bq, row_wk, row_bk, row_wv, row_bv, row_wo, row_bo)
        hc = _ln(h.swapaxes(1, 2), cn_g, cn_b)
        h = h + _lin_attn(hc, col_wq, col_bq, col_wk, col_bk, col_wv, col_bv, col_wo, col_bo).swapaxes(1, 2)
        f = _ln(h, fn_g, fn_b)
        f = jax.nn.gelu(f @ w1.T + b1, approximate=False) @ w2.T + b2
        return jnp.moveaxis(h + f, -1, 1)

    def _gn(v, G=32, eps=1e-5):
        B_, C_, H_, W_ = v.shape
        g = v.reshape(B_, G, C_ // G, H_, W_)
        m = jnp.mean(g, axis=(2, 3, 4), keepdims=True)
        s = jnp.var(g, axis=(2, 3, 4), keepdims=True)
        return ((g - m) / jnp.sqrt(s + eps)).reshape(v.shape)

    def _ln_c(v, eps=1e-6):
        m = jnp.mean(v, axis=1, keepdims=True)
        s = jnp.var(v, axis=1, keepdims=True)
        return (v - m) / jnp.sqrt(s + eps)

    def _ln_t(v, eps=1e-5):
        m = jnp.mean(v, axis=-1, keepdims=True)
        s = jnp.var(v, axis=-1, keepdims=True)
        return (v - m) / jnp.sqrt(s + eps)

    def _to_tokens(v):
        B_, C_, H_, W_ = v.shape
        return v.reshape(B_, C_, H_ * W_).transpose(0, 2, 1)
    def _from_tokens(t, like):
        B_, C_, H_, W_ = like.shape
        return t.transpose(0, 2, 1).reshape(B_, C_, H_, W_)

    x = _L0_conv_ref(x, L0_conv_ln1_w, L0_conv_ln1_b, L0_conv_in_proj_w, L0_conv_qkv_w, L0_conv_qkv_dw, L0_conv_out_proj_w, L0_conv_temperature, L0_conv_attn_scales, L0_conv_gate_w1, L0_conv_gate_b1, L0_conv_gate_w2, L0_conv_gate_b2, L0_conv_lgce_pre_w, L0_conv_lgce_pre_b, L0_conv_lgce_post_w, L0_conv_lgce_post_b, L0_conv_cbam_m1w, L0_conv_cbam_m1b, L0_conv_cbam_m2w, L0_conv_cbam_m2b, L0_conv_cbam_spw, L0_conv_cbam_spb, L0_conv_ln2_w, L0_conv_ln2_b, L0_conv_ffn_in_w, L0_conv_dw3_w, L0_conv_dw5_w, L0_conv_ffn_out_w, L0_conv_fft_W)
    x = _L1_conv_ref(x, L1_conv_row_wq, L1_conv_row_bq, L1_conv_row_wk, L1_conv_row_bk, L1_conv_row_wv, L1_conv_row_bv, L1_conv_row_wo, L1_conv_row_bo, L1_conv_col_wq, L1_conv_col_bq, L1_conv_col_wk, L1_conv_col_bk, L1_conv_col_wv, L1_conv_col_bv, L1_conv_col_wo, L1_conv_col_bo, L1_conv_rn_g, L1_conv_rn_b, L1_conv_cn_g, L1_conv_cn_b, L1_conv_fn_g, L1_conv_fn_b, L1_conv_w1, L1_conv_b1, L1_conv_w2, L1_conv_b2)
    return x


_drawn_inputs = setup_inputs


def setup_inputs(seed=0):
    import zlib

    import numpy as np

    out = dict(_drawn_inputs(seed))
    spreads = {'L0_conv_ln1_w': (1.0, 0.6),
     'L0_conv_ln1_b': (0.0, 0.8),
     'L0_conv_temperature': (1.0, 0.6),
     'L0_conv_attn_scales': (0.20000000298023224, 0.6),
     'L0_conv_gate_b1': (0.0, 0.1),
     'L0_conv_lgce_pre_b': (0.0, 0.8),
     'L0_conv_lgce_post_b': (0.0, 0.586),
     'L0_conv_cbam_m1b': (0.0, 2.0),
     'L0_conv_cbam_m2b': (0.0, 2.0),
     'L0_conv_cbam_spb': (0.0, 2.0),
     'L0_conv_ln2_w': (1.0, 0.6),
     'L0_conv_ln2_b': (0.0, 0.8),
     'L0_conv_fft_W': (1.0, 0.6),
     'L1_conv_row_bq': (0.0, 2.0),
     'L1_conv_row_bk': (0.0, 2.0),
     'L1_conv_row_bv': (0.0, 0.31),
     'L1_conv_row_bo': (0.0, 0.1),
     'L1_conv_col_bq': (0.0, 2.0),
     'L1_conv_col_bk': (0.0, 2.0),
     'L1_conv_col_bv': (0.0, 0.316),
     'L1_conv_col_bo': (0.0, 0.1),
     'L1_conv_rn_g': (1.0, 0.6),
     'L1_conv_rn_b': (0.0, 0.489),
     'L1_conv_cn_g': (1.0, 0.6),
     'L1_conv_cn_b': (0.0, 0.443),
     'L1_conv_fn_g': (1.0, 0.6),
     'L1_conv_fn_b': (0.0, 0.488),
     'L1_conv_b1': (0.0, 0.406),
     'L1_conv_b2': (0.0, 0.1)}
    factors = {'L0_conv_in_proj_w': 3.01,
     'L0_conv_qkv_w': 28.976,
     'L0_conv_qkv_dw': 30.007,
     'L0_conv_lgce_pre_w': 8.0,
     'L0_conv_lgce_post_w': 8.0,
     'L0_conv_cbam_m1w': 200.0,
     'L0_conv_cbam_m2w': 200.0,
     'L0_conv_cbam_spw': 200.0,
     'L0_conv_ffn_in_w': 8.0,
     'L0_conv_dw3_w': 8.0,
     'L0_conv_dw5_w': 8.0,
     'L0_conv_ffn_out_w': 8.0,
     'L1_conv_row_wq': 3.699,
     'L1_conv_row_wk': 7.266,
     'L1_conv_col_wq': 2.948,
     'L1_conv_col_wk': 6.558}
    for name, (base, spread) in spreads.items():
        noise = np.random.default_rng([zlib.crc32(name.encode()), seed]).standard_normal(out[name].shape)
        drawn = base * np.exp(spread * noise) if base else spread * noise
        out[name] = jnp.asarray(drawn.astype(out[name].dtype))
    for name, factor in factors.items():
        out[name] = (out[name] * factor).astype(out[name].dtype)
    return out
```

```python
from contextlib import ExitStack

import numpy as np
import concourse.bass as bass
import concourse.mybir as mybir

F32 = mybir.dt.float32
ALU = mybir.AluOpType
ACT = mybir.ActivationFunctionType
AX = mybir.AxisListType

B, C, H, W = 4, 64, 256, 256
HALF = C // 2
NPIX = H * W
P = 128
TILE = 512
ROWS = TILE // W
EPS = 1e-5
HEADS = 4
PATCH = 8
OUT_SLOTS = 2
LOG_EXP = "natural_log_exp_and_others"
GP = W + 2
ZP = W + 4
GROWS = H + 2
ZROWS = H + 6


def after(eng, sem, n):
    if n > 0:
        eng.wait_ge(sem, n)


def skewed(n, *steps):
    for t in range(n + max(lag for lag, _ in steps)):
        for lag, step in steps:
            if 0 <= t - lag < n:
                step(t - lag)


class Slots:

    def __init__(self, sem, name, n, per=1):
        self.sems = [sem(f"{name}{k}") for k in range(n)]
        self.n, self.per = n, per

    def sem_of(self, i):
        return self.sems[i % self.n]

    def landed(self, eng, i):
        eng.wait_ge(self.sems[i % self.n], 16 * self.per * (i // self.n + 1))

    def all_landed(self, eng, total):
        for k in range(min(self.n, total)):
            eng.wait_ge(self.sems[k], 16 * self.per * ((total - 1 - k) // self.n + 1))


class Norm:

    def __init__(self, sb, sem, banks, name, w, weight, bias, x_at, x_ready, z_at, z_free, cols=TILE):
        self.ps_center, self.ps_var = banks[0:2], banks[2:]
        self.square_sb = sb(f"{name}_square", [P, 2, TILE])
        self.rstd_sb = sb(f"{name}_rstd", [P, 2, TILE])
        self.scaled_sb = sb(f"{name}_scaled", [P, 2, TILE])
        names = ("center", "square", "var", "log", "rstd", "scaled", "z")
        self.s_center, self.s_square, self.s_var, self.s_log, self.s_rstd, self.s_scaled, self.s_z = [
            sem(f"{name}_{n}") for n in names]
        self.w, self.weight, self.bias = w, weight, bias
        self.x_at, self.x_ready, self.z_at, self.z_free = x_at, x_ready, z_at, z_free

    def center(self, pe, i):
        self.x_ready(pe, i)
        after(pe, self.s_scaled, i - 1)
        pe.matmul(self.ps_center[i % 2][:, :], self.w("center"), self.x_at(i),
                  start=True, stop=True).then_inc(self.s_center, 1)

    def square(self, act, i):
        after(act, self.s_center, i + 1)
        after(act, self.s_var, i - 1)
        act.activation(self.square_sb[:, i % 2, :], self.ps_center[i % 2][:, :],
                       ACT.Square).then_inc(self.s_square, 1)

    def variance(self, pe, i):
        nb = len(self.ps_var)
        after(pe, self.s_square, i + 1)
        after(pe, self.s_log, i + 1 - nb)
        pe.matmul(self.ps_var[i % nb][:, :], self.w("average"), self.square_sb[:, i % 2, :],
                  start=True, stop=True).then_inc(self.s_var, 1)

    def rstd(self, act, i):
        nb = len(self.ps_var)
        r = self.rstd_sb[:, i % 2, :]
        after(act, self.s_var, i + 1)
        after(act, self.s_scaled, i - 1)
        act.activation(r, self.ps_var[i % nb][:, :], ACT.Ln, bias=self.w("eps")).then_inc(self.s_log, 1)
        after(act, self.s_log, i + 1)
        act.activation(r, r, ACT.Exp, scale=-0.5).then_inc(self.s_rstd, 1)

    def scale(self, dve, i):
        after(dve, self.s_rstd, i + 1)
        after(dve, self.s_z, i - 1)
        dve.tensor_tensor(self.scaled_sb[:, i % 2, :], self.ps_center[i % 2][:, :],
                          self.rstd_sb[:, i % 2, :], ALU.mult).then_inc(self.s_scaled, 1)

    def affine(self, pool, i):
        after(pool, self.s_scaled, i + 1)
        self.z_free(pool, i)
        pool.tensor_scalar(self.z_at(i), self.scaled_sb[:, i % 2, :], self.w(self.weight),
                           self.w(self.bias), ALU.mult, ALU.add).then_inc(self.s_z, 1)



def laid_out(a):
    f = np.float32
    out = {}

    def put(name, x, row=0):
        x = np.asarray(x)
        x = x.reshape(x.shape[0], -1)
        full = np.zeros((P, x.shape[1]), f)
        full[row:row + x.shape[0]] = x
        out[name] = full

    def blocks(n, *m):
        r = m[0].shape[0]
        parts = []
        for x in m:
            y = np.zeros((n * r, n * x.shape[1]), f)
            for k in range(n):
                y[k * r:(k + 1) * r, k * x.shape[1]:(k + 1) * x.shape[1]] = x
            parts.append(y)
        return np.concatenate(parts, 1)

    def column(x, n):
        return np.tile(np.asarray(x).reshape(-1, 1), (n, 1))

    eye, one = np.eye(C, dtype=f), np.ones((C, C), f)
    put("center", blocks(2, eye - one / C))
    put("average", blocks(2, one / C))
    put("ident", np.eye(P, dtype=f))
    put("ones", np.ones((P, P), f))
    put("group4", blocks(P // 4, np.ones((4, 4), f)))
    put("head8", blocks(HEADS, np.ones((8, 8), f)))
    put("eps", np.full((P, 1), EPS, f))
    hm = np.zeros((P, 8), f)
    for m in range(2):
        for h in range(HEADS):
            hm[m * C + 16 * h:m * C + 16 * h + 16, m * HEADS + h] = W
    put("head_w", hm)
    fwd, inv, sel = patch_transform()
    put("dft", fwd)
    put("idft", inv)
    put("pick_w", sel)

    for name, key in (("ln1_w", "L0_conv_ln1_w"), ("ln1_b", "L0_conv_ln1_b"), ("ln2_w", "L0_conv_ln2_w"),
                      ("ln2_b", "L0_conv_ln2_b"), ("rn_g", "L1_conv_rn_g"), ("rn_b", "L1_conv_rn_b"),
                      ("cn_g", "L1_conv_cn_g"), ("cn_b", "L1_conv_cn_b"), ("fn_g", "L1_conv_fn_g"),
                      ("fn_b", "L1_conv_fn_b"), ("b2", "L1_conv_b2")):
        put(name, column(a[key], 2))
    wi = a["L0_conv_in_proj_w"]
    put("in_projT", blocks(2, wi[:HALF].T, wi[HALF:].T))
    put("gate1T", blocks(2, a["L0_conv_gate_w1"].T), row=2 * HALF)
    put("gate1_b", column(a["L0_conv_gate_b1"], 2))
    wide = np.zeros((32, 254), f)
    for m in range(2):
        wide[16 * m:16 * m + 16, 126 + m] = a["L0_conv_gate_w2"][0]
    put("gate2_wide", wide)
    put("gate2_b", column(a["L0_conv_gate_b2"], P))
    for s in ("pre", "post"):
        put(f"{s}T", blocks(4, a[f"L0_conv_lgce_{s}_w"].T))
        put(f"{s}_b", column(a[f"L0_conv_lgce_{s}_b"], 4))
    put("m1w", column(a["L0_conv_cbam_m1w"], 4))
    put("m1b", column(np.repeat(a["L0_conv_cbam_m1b"].reshape(-1), 4), 4))
    put("m2w", column(a["L0_conv_cbam_m2w"], 4))
    put("m2b", column(a["L0_conv_cbam_m2b"], 4))
    put("spw", column(a["L0_conv_cbam_spw"], 4))
    put("spb", column(np.repeat(a["L0_conv_cbam_spb"].reshape(-1), 4), 4))
    qkv, dw = a["L0_conv_qkv_w"], a["L0_conv_qkv_dw"].reshape(96, 9)
    put("qk_w", np.tile(qkv[:64], (2, 1)))
    put("qk_dw", np.tile(dw[:64], (2, 1)))
    put("v_w", qkv[64:])
    put("v_dw", dw[64:])
    wo = a["L0_conv_out_proj_w"]
    put("outA_T", wo[:, :HALF].T)
    put("outL_T", blocks(2, wo[:, HALF:].T))
    put("temp", np.repeat(a["L0_conv_temperature"].reshape(-1), 8).reshape(-1, 1))
    put("scales", np.tile(a["L0_conv_attn_scales"].reshape(1, 4), (32, 1)))
    fi = a["L0_conv_ffn_in_w"]
    put("ffn_gate", fi[:P])
    put("ffn_val", fi[P:])
    dw3, dw5 = a["L0_conv_dw3_w"][:, 0], a["L0_conv_dw5_w"][:, 0]
    put("dw_gate", dw3[:P])
    val = np.zeros((P, 5, 5), f)
    val[:C, 1:4, 1:4] = dw3[P:]
    val[C:] = dw5
    put("dw_val", val)
    put("ffn_outT", a["L0_conv_ffn_out_w"].T)
    put("fftT", a["L0_conv_fft_W"].reshape(C, 40).T)
    for s in ("row", "col"):
        g = {k: a[f"L1_conv_{s}_{k}"] for k in ("wq", "bq", "wk", "bk", "wv", "bv", "wo", "bo")}
        put(f"{s}_kqT", blocks(2, g["wk"].T, g["wq"].T))
        kq = np.concatenate([g["bk"], g["bk"], g["bq"], g["bq"]])
        put(f"{s}_kqb", np.tile(kq.reshape(1, 16), (P, 1)))
        put(f"{s}_vT", blocks(2, g["wv"].T))
        put(f"{s}_oT", blocks(2, g["wo"].T))
        put(f"{s}_bv", column(g["bv"], 2))
        put(f"{s}_bo", column(g["bo"], 2))
    put("w1T", np.tile(a["L1_conv_w1"].T, (2, 1)))
    put("b1", a["L1_conv_b1"].reshape(2, P).T)
    put("w2T", a["L1_conv_w2"].T.reshape(2, P, C).transpose(1, 0, 2))
    return out


def patch_transform():
    n = PATCH
    y, x = np.meshgrid(np.arange(n), np.arange(n), indexing="ij")
    rows_f, rows_i, picks = [], [], []
    for kx in range(n // 2 + 1):
        for ky in range(n):
            mirror = (-ky) % n
            own = kx in (0, n // 2) and ky == mirror
            if kx in (0, n // 2) and ky > mirror:
                continue
            arg = 2 * np.pi * (ky * y + kx * x) / n
            pick = np.zeros(n * (n // 2 + 1))
            if kx in (0, n // 2):
                pick[ky * 5 + kx] += 0.5
                pick[mirror * 5 + kx] += 0.5
            else:
                pick[ky * 5 + kx] = 1.0
            for fn in ((np.cos,) if own else (np.cos, np.sin)):
                rows_f.append(fn(arg).reshape(-1))
                rows_i.append(fn(arg).reshape(-1) * (1 if own else 2) / n ** 2)
                picks.append(pick)
    f, i = np.array(rows_f), np.array(rows_i)
    fwd = np.zeros((n, 2, n, 2, n * n))
    inv = np.zeros((2, n * n, n, 2, n))
    for p in range(2):
        fwd[:, p, :, p, :] = f.reshape(n * n, n, n).transpose(1, 2, 0)
        inv[p, :, :, p, :] = i.reshape(n * n, n, n)
    sel = np.concatenate([np.array(picks)] * 2).T
    return (fwd.reshape(P, P).astype(np.float32), inv.reshape(P, P).astype(np.float32),
            sel.astype(np.float32))


def pixels(t, b0, n, r0, rows):
    return t[b0:b0 + n].rearrange("b c n -> (b c) n")[:, r0 * W:(r0 + rows) * W]



class Program:

    def __init__(self, nc, ctx, where, packed, dram):
        self.nc, self.ctx, self.where, self.packed, self.dram = nc, ctx, where, packed, dram
        self.n_sem, self.sems, self.sem_ctx = 0, [], ctx.enter_context(ExitStack())
        self.out_stored = Slots(lambda name: ctx.enter_context(nc.semaphore(name)), "out_stored", OUT_SLOTS)
        self.all_w = self.keep("all_w", [P, packed.shape[1]])
        self.banks = [ctx.enter_context(nc.psum_tensor(f"bank{k}", [P, TILE], F32)) for k in range(8)]

    def layer0(self, ctx):
        keep = lambda name, shape: ctx.enter_context(self.nc.sbuf_tensor(name, shape, F32))
        self.conv_qk = keep("conv_qk", [P, 2, 3, P])
        self.v_taps = keep("v_taps", [32, 3, 96])
        self.conv_v = keep("conv_v", [96, B, 3, C])
        self.conv_gate = keep("conv_gate", [P, 2, 3, P])
        self.conv_val = keep("conv_val", [P, 3, 5, P])
        self.freq_w = keep("freq_w", [P, C])
        self.local_sum = keep("local_sum", [2 * HALF, 2, NPIX // TILE])
        self.gate_sum = keep("gate_sum", [P, 4])
        self.gram = keep("gram", [64, B, 64])
        self.cw = keep("cw", [P, 1])
        self.resp_sum = keep("resp_sum", [P, NPIX // TILE])
        self.threshold = keep("threshold", [P, 1])

    def keep(self, name, shape):
        return self.ctx.enter_context(self.nc.sbuf_tensor(name, shape, F32))

    def sem(self, name):
        self.n_sem += 1
        made = self.sem_ctx.enter_context(self.nc.semaphore(f"s{self.n_sem}_{name}"))
        self.sems.append(made)
        return made

    def reuse_semaphores(self):
        for sem in self.sems:
            self.nc.sync.sem_clear(sem)
        self.nc.all_engine_barrier()
        self.sem_ctx.close()
        self.sems = []

    def w(self, name, rows=slice(0, P)):
        a, b = self.where[name]
        return self.all_w[rows, a:b]


def phase(fn):
    def run(k, *args):
        with ExitStack() as ctx:
            def sb(name, shape):
                return ctx.enter_context(k.nc.sbuf_tensor(f"{fn.__name__}{args}_{name}".replace("'", ""), shape, F32))
            fn(k, sb, *args)
    return run


@phase
def set_up(k, sb):
    nc, w = k.nc, k.w
    n_gate, n_val = 6, 15
    s_w, s_zero, s_rows, s_prod, s_turn, s_copy = [k.sem(n) for n in ("w", "zero", "rows", "prod", "turn", "copy")]
    zeros = sb("zeros", [P, 3 * ZP])
    prod_qk = sb("prod_qk", [P, 2, 3, P])
    prod = sb("prod", [P, n_gate + n_val, P])
    glob, z2 = k.dram["glob"], k.dram["z2"]

    def turned(n):
        col = 3 if n == 20 else n % 4
        return k.banks[1 + n // 4][:, P * col:P * col + P]

    with nc.Block() as block:
        @block.sync
        def _(sp):
            sp.dma_start(k.all_w[:, :], k.packed).then_inc(s_w, 16)
            after(sp, s_zero, 3)
            g = glob.rearrange("b c (r x) -> (b c) r x", x=GP)
            sp.dma_start(g[:, 0, :], zeros[:, 0:GP]).then_inc(s_rows, 16)
            sp.dma_start(g[:, GROWS - 1, :], zeros[:, 0:GP]).then_inc(s_rows, 16)
            n = 2
            for p in range(2):
                z = z2[2 * p:2 * p + 2].rearrange("b c n -> (b c) n")
                sp.dma_start(z[:, 0:2 * ZP], zeros[:, 0:2 * ZP]).then_inc(s_rows, 16)
                sp.dma_start(z[:, (H + 2) * ZP:ZROWS * ZP][:, 0:3 * ZP], zeros[:, 0:3 * ZP]).then_inc(s_rows, 16)
                sp.dma_start(z[:, (H + 5) * ZP:ZROWS * ZP], zeros[:, 0:ZP]).then_inc(s_rows, 16)
                n += 3
            sp.wait_ge(s_rows, 16 * n)

        @block.vector
        def _(dve):
            dve.memset(zeros[:, :], 0.0).then_inc(s_zero, 1)
            dve.memset(prod[:, :, :], 0.0).then_inc(s_zero, 1)
            dve.memset(prod_qk[:, :, :, :], 0.0).then_inc(s_zero, 1)
            dve.wait_ge(s_w, 16)
            dve.wait_ge(s_zero, 3)
            for dx in range(3):
                for dy in range(3):
                    t = dy * 3 + dx
                    for m in range(2):
                        rows, c = slice(64 * m, 64 * m + 64), 64 * (dy % 2) + 32 * m
                        dve.tensor_scalar(prod_qk[rows, dy // 2, dx, c:c + 32], w("qk_w", rows),
                                          w("qk_dw", rows)[:, t:t + 1], None, ALU.mult)
                    dve.tensor_scalar(k.v_taps[:, dx, 32 * dy:32 * dy + 32], w("v_w", slice(0, 32)),
                                      w("v_dw", slice(0, 32))[:, t:t + 1], None, ALU.mult)
            for n, (weight, taps, tap) in enumerate(conv_taps()):
                for s, t in enumerate(tap):
                    last = dve.tensor_scalar(prod[:, n, C * s:C * s + C], w(weight), w(taps)[:, t:t + 1],
                                             None, ALU.mult)
            last.then_inc(s_prod, 1)
            dve.wait_ge(s_turn, 1)
            for n in range(2):
                dve.tensor_copy(k.conv_qk[:, n, :, :], k.banks[6 * n][:, 0:3 * P].rearrange("p (d m) -> p d m", d=3))
            dve.tensor_copy(k.freq_w[:, :], k.banks[7][:, 0:C])
            for n in range(n_gate + n_val):
                dst = (k.conv_gate[:, n // 3, n % 3, :] if n < n_gate
                       else k.conv_val[:, (n - n_gate) // 5, (n - n_gate) % 5, :])
                last = dve.tensor_copy(dst, turned(n))
            last.then_inc(s_copy, 1)

        @block.tensor
        def _(pe):
            pe.wait_ge(s_prod, 1)
            pe.wait_ge(s_w, 16)
            for n in range(2):
                for dx in range(3):
                    pe.matmul(k.banks[6 * n][:, P * dx:P * dx + P], prod_qk[:, n, dx, :], w("ident"),
                              start=True, stop=True)
            pe.matmul(k.banks[7][:, 0:C], w("pick_w", slice(0, 40)), w("fftT", slice(0, 40)),
                      start=True, stop=True)
            for n in range(n_gate + n_val):
                last = pe.matmul(turned(n), prod[:, n, :], w("ident"),
                                 start=True, stop=True)
            last.then_inc(s_turn, 1)


def conv_taps():
    for dy in (0, 2):
        for dx in range(3):
            yield "ffn_gate", "dw_gate", [3 * d + dx for d in (dy, dy + 1) if d < 3]
    for dy in (0, 2, 4):
        for dx in range(5):
            yield "ffn_val", "dw_val", [5 * d + dx for d in (dy, dy + 1) if d < 5]


@phase
def project_in(k, sb):
    nc, w = k.nc, k.w
    n_tiles = 2 * NPIX // TILE
    per_pair = NPIX // TILE
    NX, NZ = 6, 2
    x_sb = sb("x", [P, NX, TILE])
    z_sb = sb("z", [P, NZ, TILE])
    NO = 4
    proj_sb = sb("proj", [P, NO, ROWS, GP])
    hid_sb = sb("hid", [32, 2, TILE])
    g_sb = sb("g", [P, 2, TILE])
    neg_b2 = sb("neg_b2", [P, 1])
    x_in = Slots(k.sem, "x", NX)
    stored = Slots(k.sem, "stored", NO, per=2)
    s_pad, s_proj, s_projc, s_hid, s_hidc, s_gate, s_g1, s_g2, s_g3, s_g4 = [
        k.sem(n) for n in ("pad", "proj", "projc", "hid", "hidc", "gate", "g1", "g2", "g3", "g4")]
    ps_proj, ps_hid, ps_gate = k.banks[4], k.banks[5], k.banks[6:8]
    x, local, glob = k.dram["x"], k.dram["local"], k.dram["glob"]

    ln = Norm(sb, k.sem, k.banks[0:4], "ln", w, "ln1_w", "ln1_b",
              x_at=lambda i: x_sb[:, i % NX, :], x_ready=lambda e, i: x_in.landed(e, i),
              z_at=lambda i: z_sb[:, i % NZ, :], z_free=lambda e, i: after(e, s_proj, i - NZ + 1))

    with nc.Block() as block:
        @block.sync
        def _(sp):
            def load(i):
                after(sp, ln.s_center, i - NX + 1)
                sp.dma_start(x_sb[:, i % NX, :],
                             pixels(x, 2 * (i // per_pair), 2, ROWS * (i % per_pair), ROWS)).then_inc(x_in.sem_of(i), 16)

            def store(i):
                p, r = i // per_pair, ROWS * (i % per_pair)
                after(sp, s_projc, i + 1)
                sp.dma_start(pixels(local, 2 * p, 2, r, ROWS).rearrange("p (r x) -> p r x", x=W),
                             proj_sb[0:64, i % NO, :, 1:1 + W]).then_inc(stored.sem_of(i), 16)
                sp.dma_start(glob[2 * p:2 * p + 2].rearrange("b c n -> (b c) n")[:, (r + 1) * GP:(r + 1 + ROWS) * GP]
                             .rearrange("p (r x) -> p r x", x=GP),
                             proj_sb[64:128, i % NO, :, :]).then_inc(stored.sem_of(i), 16)
            skewed(n_tiles, (0, load), (NX, store))
            stored.all_landed(sp, n_tiles)

        @block.tensor
        def _(pe):
            def proj(i):
                after(pe, ln.s_z, i + 1)
                after(pe, s_projc, i)
                pe.matmul(ps_proj[:, :], w("in_projT"), z_sb[:, i % NZ, :], start=True, stop=True).then_inc(s_proj, 1)

            def hidden(i):
                after(pe, s_projc, i + 1)
                after(pe, s_hidc, i)
                pe.matmul(ps_hid[0:32, :].rearrange("p (r x) -> p r x", x=W), w("gate1T", slice(64, P)),
                          proj_sb[64:P, i % NO, :, 1:1 + W], start=True, stop=True).then_inc(s_hid, 1)

            def gate(i):
                j = i % 64
                after(pe, s_hidc, i + 1)
                if j == 0:
                    after(pe, s_g1, i // 64 - 1)
                pe.matmul(ps_gate[i // 64 % 2][:, :], w("gate2_wide", slice(0, 32))[:, 126 - 2 * j:254 - 2 * j],
                          hid_sb[:, i % 2, :], start=(j == 0), stop=(j == 63)).then_inc(s_gate, 1)
            skewed(n_tiles, (5, gate), (4, hidden), (3, proj), (1, lambda i: ln.variance(pe, i)),
                   (0, lambda i: ln.center(pe, i)))

        @block.scalar
        def _(act):
            act.preload_act_table_set(LOG_EXP)

            def gate_exp(i):
                n = i // 64
                if i % 64 == 63:
                    after(act, s_gate, i + 1)
                    after(act, s_pad, 2)
                    after(act, s_g4, n - 1)
                    act.activation(g_sb[:, n % 2, :], ps_gate[n % 2][:, :], ACT.Exp, bias=neg_b2[:, :],
                                   scale=-1.0).then_inc(s_g1, 1)
            skewed(n_tiles, (1, lambda i: ln.rstd(act, i)), (0, lambda i: ln.square(act, i)), (6, gate_exp))

        @block.gpsimd
        def _(pool):
            skewed(n_tiles, (0, lambda i: ln.affine(pool, i)))

        @block.vector
        def _(dve):
            dve.memset(proj_sb[:, :, :, :], 0.0).then_inc(s_pad, 1)
            dve.tensor_scalar(neg_b2[:, :], w("gate2_b"), -1.0, None, ALU.mult).then_inc(s_pad, 1)
            dve.wait_ge(s_pad, 2)

            def copy(i):
                p, t = i // per_pair, i % per_pair
                after(dve, s_proj, i + 1)
                if i >= NO:
                    stored.landed(dve, i - NO)
                after(dve, s_hid, i - NO + 1)
                for rows, acc in ((slice(0, 64), k.local_sum[:, p, t:t + 1]), (slice(64, P), None)):
                    src = ps_proj[rows, :].rearrange("p (r x) -> p r x", x=W)
                    dst = proj_sb[rows, i % NO, :, 1:1 + W]
                    if acc is not None:
                        dve.tensor_scalar(dst, src, 0.0, 0.0, ALU.add, ALU.add, accum_out=acc)
                    else:
                        dve.tensor_copy(dst, src).then_inc(s_projc, 1)

            def relu(i):
                after(dve, s_hid, i + 1)
                after(dve, s_gate, i - 1)
                dve.tensor_scalar(hid_sb[:, i % 2, :], ps_hid[0:32, :], w("gate1_b", slice(0, 32)), 0.0,
                                  ALU.add, ALU.max).then_inc(s_hidc, 1)

            def gate_sum(i):
                n = i // 64
                if i % 64 == 63:
                    g = g_sb[:, n % 2, :]
                    after(dve, s_g1, n + 1)
                    dve.tensor_scalar(g, g, 1.0, None, ALU.add).then_inc(s_g2, 1)
                    after(dve, s_g2, n + 1)
                    dve.reciprocal(g, g).then_inc(s_g3, 1)
                    after(dve, s_g3, n + 1)
                    dve.tensor_reduce(k.gate_sum[:, n:n + 1], g, AX.X, ALU.add).then_inc(s_g4, 1)
            skewed(n_tiles, (3, relu), (2, copy), (0, lambda i: ln.scale(dve, i)), (6, gate_sum))


@phase
def gram(k, sb):
    nc = k.nc
    GR = 8
    NG, NB = 3, 6
    groups = GR * W // P
    n_bank = groups // 4
    n_loads = 2 * H // GR
    n_units = n_loads * n_bank
    per_pair = n_units // 2
    g_sb = sb("g", [P, NG, GR + 2, GP])
    qk_sb = sb("qk", [P, 3, 4, P])
    g_in = Slots(k.sem, "g", NG, per=2)
    s_qk, s_qkc, s_gram, s_gramc = [k.sem(n) for n in ("qk", "qkc", "gram", "gramc")]
    glob = k.dram["glob"]
    ps_gram = k.banks[NB:8]

    with nc.Block() as block:
        @block.sync
        def _(sp):
            for i in range(n_loads):
                p, r = i * GR // H, i * GR % H
                images = glob[2 * p:2 * p + 2].rearrange("b c n -> (b c) n")
                after(sp, s_qk, n_bank * (i - NG + 1))
                for copy, rows in ((0, GR + 2), (1, GR + 1)):
                    sp.dma_start(g_sb[64 * copy:64 * copy + 64, i % NG, 0:rows, :].rearrange("p r x -> p (r x)"),
                                 images[:, (r + copy) * GP:(r + copy + rows) * GP]).then_inc(g_in.sem_of(i), 16)

        @block.tensor
        def _(pe):
            def conv(u):
                i = u // n_bank
                g_in.landed(pe, i)
                after(pe, s_qkc, u - NB + 1)
                for g in range(4):
                    px = (u % n_bank) * 4 + g
                    row, col = px * P // W, px * P % W
                    for n in range(6):
                        pair, dx = n // 3, n % 3
                        rows = slice(0, P) if pair == 0 else slice(0, 64)
                        last = pe.matmul(k.banks[u % NB][:, P * g:P * g + P],
                                         g_sb[rows, i % NG, row + 2 * pair, col + dx:col + dx + P],
                                         k.conv_qk[rows, pair, dx, :], start=(n == 0), stop=(n == 5))
                last.then_inc(s_qk, 1)

            def products(u):
                p, v = u // per_pair, u % per_pair
                after(pe, s_qkc, u + 1)
                for g in range(4):
                    last = pe.matmul(ps_gram[p][:, 0:P], qk_sb[:, u % 3, g, :], qk_sb[:, u % 3, g, :],
                                     start=(v == 0 and g == 0), stop=(v == per_pair - 1 and g == 3))
                last.then_inc(s_gram, 1)
            skewed(n_units, (2, products), (0, conv))

        @block.vector
        def _(dve):
            def copy(u):
                after(dve, s_qk, u + 1)
                after(dve, s_gram, u - 2)
                dve.tensor_copy(qk_sb[:, u % 3, :, :], k.banks[u % NB][:, :].rearrange("p (g c) -> p g c", g=4)
                                ).then_inc(s_qkc, 1)

            def keep(u):
                if (u + 1) % per_pair == 0:
                    p = u // per_pair
                    after(dve, s_gram, u + 1)
                    for m in range(2):
                        dve.tensor_copy(k.gram[:, 2 * p + m, :], ps_gram[p][64 * m:64 * m + 64, 64 * m:64 * m + 64])
            skewed(n_units, (3, keep), (0, copy))


@phase
def attention_weights(k, sb):
    nc, w = k.nc, k.w
    s_dve, s_pe, s_act, s_dma = [k.sem(n) for n in ("dve", "pe", "act", "dma")]
    v3 = lambda n, *shape: sb(n, [32, B] + list(shape))
    kdiag = sb("kdiag", [64, B, 32])
    qdiag, kn = v3("qdiag", 32), v3("kn", 32)
    qn, full, scores, bigger, cmp, keep, expo, rowv, prob = (
        v3("qn", 1), v3("full", 32), v3("scores", 8), v3("bigger", 8), v3("cmp", 8), v3("keep", 8),
        v3("expo", 8), v3("rowv", 1), v3("prob", 32))
    gsum, gmean, ssum, rv_sb = sb("gsum", [P, 1]), sb("gmean", [32, 1]), sb("ssum", [32, 1]), sb("rv", [32, B, C])
    m_pair, m_all = sb("m_pair", [64, 2]), sb("m_all", [P, 1])
    pooled, h1, m1 = sb("pooled", [P, 1]), sb("h1", [P, 1]), sb("m1", [P, P])
    count = {"dve": 0, "pe": 0, "act": 0}

    steps = []

    def step(engine, fn):
        steps.append((engine, fn))

    def run(eng, name):
        sems = {"dve": s_dve, "pe": s_pe, "act": s_act, "dma": s_dma}
        done = {"dve": 0, "pe": 0, "act": 0, "dma": 0}
        for n, (engine, fn) in enumerate(steps):
            if engine == name:
                if n:
                    before = steps[n - 1][0]
                    eng.wait_ge(sems[before], done[before])
                fn(eng).then_inc(sems[name], 16 if name == "dma" else 1)
            done[engine] += 16 if engine == "dma" else 1

    r32 = slice(0, 32)
    bank = k.banks[0]
    step("dve", lambda e: e.tensor_reduce(m_pair[:, :], k.local_sum[:, :, :], AX.X, ALU.add))
    step("dve", lambda e: e.tensor_copy(m_all[0:64, :], m_pair[:, 0:1]))
    step("dma", lambda e: e.dma_start(m_all[64:P, :], m_pair[:, 1:2]))
    step("pe", lambda e: e.matmul(bank[:, 0:1], w("preT"), m_all[:, :], start=True, stop=True))
    step("dve", lambda e: e.tensor_scalar(pooled[:, :], bank[:, 0:1], 1.0 / NPIX, w("pre_b"), ALU.mult, ALU.add))
    step("dve", lambda e: e.tensor_scalar(m1[:, :], w("group4"), w("m1w"), None, ALU.mult))
    step("pe", lambda e: e.matmul(bank[:, 0:1], m1[:, :], pooled[:, :], start=True, stop=True))
    step("dve", lambda e: e.tensor_scalar(h1[:, :], bank[:, 0:1], w("m1b"), 0.0, ALU.add, ALU.max))
    step("dve", lambda e: e.tensor_tensor(h1[:, :], h1[:, :], w("m2w"), ALU.mult))
    step("act", lambda e: e.activation(k.cw[:, :], h1[:, :], ACT.Sigmoid, bias=w("m2b")))
    step("dve", lambda e: e.tensor_reduce(gsum[:, :], k.gate_sum[:, :], AX.X, ALU.add))
    step("pe", lambda e: e.matmul(bank[0:32, 0:1], w("ones")[:, 0:32], gsum[:, :], start=True, stop=True))
    step("dve", lambda e: e.tensor_scalar(gmean[:, :], bank[0:32, 0:1], 8.0 / (B * NPIX), 1.0, ALU.mult, ALU.max))
    for b in range(B):
        step("dve", lambda e, b=b: e.tensor_tensor(qdiag[:, b, :], k.gram[0:32, b, 0:32], w("ident", r32)[:, 0:32], ALU.mult))
        step("dve", lambda e, b=b: e.tensor_tensor(kdiag[32:64, b, :], k.gram[32:64, b, 32:64],
                                                   w("ident", slice(32, 64))[:, 32:64], ALU.mult))
    step("dve", lambda e: e.tensor_reduce(qn[:, :, :].rearrange("p b o -> p (b o)"), qdiag[:, :, :], AX.X, ALU.add))
    step("pe", lambda e: e.matmul(bank[0:32, 0:128], w("ones", slice(32, 64))[:, 0:32],
                                  kdiag[32:64, :, :].rearrange("p b c -> p (b c)"), start=True, stop=True))
    step("act", lambda e: e.activation(kn[:, :, :].rearrange("p b c -> p (b c)"), bank[0:32, 0:128], ACT.Sqrt))
    step("act", lambda e: e.activation(qn[:, :, :], qn[:, :, :], ACT.Sqrt))
    for t in (kn, qn):
        step("dve", lambda e, t=t: e.tensor_scalar(t[:, :, :], t[:, :, :], 1e-12, None, ALU.max))
        step("dve", lambda e, t=t: e.reciprocal(t[:, :, :], t[:, :, :]))
    for b in range(B):
        step("dve", lambda e, b=b: e.scalar_tensor_tensor(full[:, b, :], k.gram[0:32, b, 32:64], qn[:, b, :],
                                                          kn[:, b, :], ALU.mult, ALU.mult))
        step("dve", lambda e, b=b: e.scalar_tensor_tensor(full[:, b, :], full[:, b, :], w("temp", r32),
                                                          w("head8", r32), ALU.mult, ALU.mult))
        step("dve", lambda e, b=b: e.tensor_reduce(scores[:, b, :], full[:, b, :].rearrange("p (h d) -> p d h", h=HEADS),
                                                   AX.X, ALU.add))
    step("dve", lambda e: e.memset(bigger[:, :, :], 1.0))
    for d in range(8):
        step("dve", lambda e, d=d: e.tensor_tensor(cmp[:, :, :], scores[:, :, d:d + 1].broadcast_to([32, B, 8]),
                                                   scores[:, :, :], ALU.is_gt))
        step("dve", lambda e: e.tensor_tensor(bigger[:, :, :], bigger[:, :, :], cmp[:, :, :], ALU.add))
    step("dve", lambda e: e.tensor_scalar(keep[:, :, :], bigger[:, :, :], gmean[:, :], None, ALU.is_le))
    step("dve", lambda e: e.tensor_reduce(rowv[:, :, :].rearrange("p b o -> p (b o)"), scores[:, :, :], AX.X, ALU.max))
    step("dve", lambda e: e.tensor_tensor(expo[:, :, :], scores[:, :, :], rowv[:, :, :].broadcast_to([32, B, 8]), ALU.subtract))
    step("act", lambda e: e.activation(expo[:, :, :], expo[:, :, :], ACT.Exp))
    step("dve", lambda e: e.tensor_tensor(expo[:, :, :], expo[:, :, :], keep[:, :, :], ALU.mult))
    step("dve", lambda e: e.tensor_reduce(rowv[:, :, :].rearrange("p b o -> p (b o)"), expo[:, :, :], AX.X, ALU.add))
    step("dve", lambda e: e.reciprocal(rowv[:, :, :], rowv[:, :, :]))
    step("dve", lambda e: e.tensor_reduce(ssum[:, :], w("scales", r32), AX.X, ALU.add))
    step("dve", lambda e: e.tensor_scalar(rowv[:, :, :], rowv[:, :, :], ssum[:, :], None, ALU.mult))
    step("dve", lambda e: e.tensor_tensor(expo[:, :, :], expo[:, :, :], rowv[:, :, :].broadcast_to([32, B, 8]), ALU.mult))
    for b in range(B):
        for h in range(HEADS):
            step("dve", lambda e, b=b, h=h: e.tensor_tensor(prob[:, b, 8 * h:8 * h + 8], expo[:, b, :],
                                                            w("head8", r32)[:, 8 * h:8 * h + 8], ALU.mult))
    for b in range(B):
        step("pe", lambda e, b=b: e.matmul(bank[0:32, C * b:C * b + C], prob[:, b, :], w("outA_T", r32), start=True, stop=True))
    step("dve", lambda e: e.tensor_copy(rv_sb[:, :, :], bank[0:32, 0:B * C].rearrange("p (b c) -> p b c", b=B)))
    for b in range(B):
        for dx in range(3):
            step("pe", lambda e, b=b, dx=dx: e.matmul(k.banks[1 + b][0:96, C * dx:C * dx + C], k.v_taps[:, dx, :], rv_sb[:, b, :],
                                                      start=True, stop=True))
        step("dve", lambda e, b=b: e.tensor_copy(k.conv_v[:, b, :, :], k.banks[1 + b][0:96, 0:3 * C].rearrange("p (d c) -> p d c", d=3)))

    with nc.Block() as block:
        @block.sync
        def _(sp):
            run(sp, "dma")

        @block.vector
        def _(dve):
            run(dve, "dve")

        @block.tensor
        def _(pe):
            run(pe, "pe")

        @block.scalar
        def _(act):
            run(act, "act")


@phase
def local_branch(k, sb, last):
    nc, w = k.nc, k.w
    n_tiles = NPIX // TILE
    NL = 6
    l_sb = sb("l", [P, NL, TILE])
    xg_sb, xa_sb, m_sb, r_sb, y_sb = [sb(n, [P, 2, TILE]) for n in ("xg", "xa", "m", "r", "y")]
    NO = 4
    o_sb = sb("o", [P, NO, TILE])
    spread = sb("spread", [P, P])
    total = sb("total", [P, 1])
    l_in = Slots(k.sem, "l", NL)
    stored = Slots(k.sem, "stored", NO)
    names = ("spread", "pre", "xg", "xa", "sw", "sig", "m", "r", "mask", "y", "post", "o", "thr")
    s_spread, s_pre, s_xg, s_xa, s_sw, s_sig, s_m, s_r, s_mask, s_y, s_post, s_o, s_thr = [k.sem(n) for n in names]
    ps_pre, ps_sw, ps_sig, ps_post = k.banks[0:2], k.banks[2], k.banks[3:5], k.banks[5:7]
    local, gated = k.dram["local"], k.dram["gated"]

    with nc.Block() as block:
        @block.sync
        def _(sp):
            def load(i):
                after(sp, s_o if last else s_pre, i - NL + 1)
                sp.dma_start(l_sb[:, i % NL, :], pixels(local, 0, B, ROWS * i, ROWS)).then_inc(l_in.sem_of(i), 16)

            def store(i):
                after(sp, s_o, i + 1)
                sp.dma_start(pixels(gated, 0, B, ROWS * i, ROWS), o_sb[:, i % NO, :]).then_inc(stored.sem_of(i), 16)
            skewed(n_tiles, (0, load), *([(NL - 1, store)] if last else []))
            if last:
                stored.all_landed(sp, n_tiles)

        @block.tensor
        def _(pe):
            after(pe, s_spread, 1)

            def pre(i):
                l_in.landed(pe, i)
                after(pe, s_xa, i - 1)
                if last:
                    after(pe, s_xg, i - 1)
                pe.matmul(ps_pre[i % 2][:, :], w("preT"), l_sb[:, i % NL, :], start=True, stop=True).then_inc(s_pre, 1)

            def sw(i):
                after(pe, s_xa, i + 1)
                after(pe, s_sig, i)
                pe.matmul(ps_sw[:, :], spread[:, :], xa_sb[:, i % 2, :], start=True, stop=True).then_inc(s_sw, 1)

            def post(i):
                after(pe, s_y, i + 1)
                after(pe, s_o, i - 1)
                pe.matmul(ps_post[i % 2][:, :], w("postT"), y_sb[:, i % 2, :], start=True, stop=True).then_inc(s_post, 1)
            skewed(n_tiles, *([(3, post)] if last else []), (1, sw), (0, pre))

            def thr(pe):
                after(pe, s_thr, 1)
                pe.matmul(k.banks[7][:, 0:1], w("group4"), total[:, :], start=True, stop=True).then_inc(s_thr, 1)
            if not last:
                thr(pe)

        @block.scalar
        def _(act):
            def xg(i):
                after(act, s_pre, i + 1)
                after(act, s_xa, i + 1)
                if last:
                    after(act, s_y, i - 1)
                    act.activation(xg_sb[:, i % 2, :], ps_pre[i % 2][:, :], ACT.Identity, bias=w("pre_b")).then_inc(s_xg, 1)

            def sig(i):
                after(act, s_sw, i + 1)
                after(act, s_m, i - 1)
                act.activation(ps_sig[i % 2][:, :], ps_sw[:, :], ACT.Sigmoid, bias=w("spb")).then_inc(s_sig, 1)

            def resp(i):
                after(act, s_m, i + 1)
                if last:
                    after(act, s_y, i - 1)
                    act.activation(r_sb[:, i % 2, :], m_sb[:, i % 2, :], ACT.Sigmoid).then_inc(s_r, 1)
                else:
                    act.activation(r_sb[:, i % 2, :], m_sb[:, i % 2, :], ACT.Sigmoid,
                                   accum_out=k.resp_sum[:, i:i + 1]).then_inc(s_r, 1)
            skewed(n_tiles, (2, resp), (1, sig), *([(0, xg)] if last else []))

        @block.vector
        def _(dve):
            dve.tensor_scalar(spread[:, :], w("group4"), w("spw"), None, ALU.mult).then_inc(s_spread, 1)

            def xa(i):
                after(dve, s_pre, i + 1)
                after(dve, s_sw, i - 1)
                after(dve, s_m, i - 1)
                dve.tensor_scalar(xa_sb[:, i % 2, :], ps_pre[i % 2][:, :], w("pre_b"), k.cw[:, :],
                                  ALU.add, ALU.mult).then_inc(s_xa, 1)

            def m(i):
                after(dve, s_sig, i + 1)
                after(dve, s_xa, i + 1)
                after(dve, s_r, i - 1)
                dve.tensor_tensor(m_sb[:, i % 2, :], ps_sig[i % 2][:, :], xa_sb[:, i % 2, :], ALU.mult).then_inc(s_m, 1)

            def mask(i):
                after(dve, s_r, i + 1)
                after(dve, s_y, i - 1)
                r = r_sb[:, i % 2, :]
                dve.scalar_tensor_tensor(r, r, k.threshold[:, :], r, ALU.is_gt, ALU.max).then_inc(s_mask, 1)

            def out(i):
                after(dve, s_post, i + 1)
                if i >= NO:
                    stored.landed(dve, i - NO)
                dve.scalar_tensor_tensor(o_sb[:, i % NO, :], ps_post[i % 2][:, :], w("post_b"), l_sb[:, i % NL, :],
                                         ALU.add, ALU.add).then_inc(s_o, 1)
            skewed(n_tiles, *([(4, out), (2, mask)] if last else []), (1, m), (0, xa))
            if not last:
                after(dve, s_r, n_tiles)
                dve.tensor_reduce(total[:, :], k.resp_sum[:, :], AX.X, ALU.add).then_inc(s_thr, 1)
                after(dve, s_thr, 2)
                dve.tensor_scalar(k.threshold[:, :], k.banks[7][:, 0:1], 1.0 / (4 * NPIX), None, ALU.mult)

        @block.gpsimd
        def _(pool):
            def y(i):
                after(pool, s_mask, i + 1)
                after(pool, s_xg, i + 1)
                after(pool, s_post, i - 1)
                pool.tensor_tensor(y_sb[:, i % 2, :], xg_sb[:, i % 2, :], r_sb[:, i % 2, :], ALU.mult).then_inc(s_y, 1)
            if last:
                skewed(n_tiles, (0, y))


@phase
def project_out(k, sb):
    nc, w = k.nc, k.w
    GR = 8
    per_load = GR // ROWS
    n_tiles = 2 * NPIX // TILE
    per_pair = NPIX // TILE
    NG, NX, NO = 2, 3, 3
    g_sb = sb("g", [96, NG, 2, GR, GP])
    l_sb = sb("l", [64, NX, TILE])
    x_sb = sb("x", [P, NX, TILE])
    x1_sb = sb("x1", [P, NO, TILE])
    z_sb = sb("z", [P, NO, ROWS, ZP])
    g_in = Slots(k.sem, "g", NG, per=3)
    xl_in = Slots(k.sem, "xl", NX, per=2)
    x1_out, z_out = Slots(k.sem, "x1o", NO), Slots(k.sem, "zo", NO)
    s_out, s_x1, s_pad = [k.sem(n) for n in ("out", "x1", "pad")]
    ps_out = k.banks[4:6]
    glob, gated, x, x1, z2 = [k.dram[n] for n in ("glob", "gated", "x", "x1", "z2")]
    rows_of = lambda i: (i // per_pair, ROWS * (i % per_pair))

    def z_free(e, i):
        after(e, s_pad, 1)
        if i >= NO:
            z_out.landed(e, i - NO)

    ln = Norm(sb, k.sem, k.banks[0:4], "ln", w, "ln2_w", "ln2_b",
              x_at=lambda i: x1_sb[:, i % NO, :], x_ready=lambda e, i: after(e, s_x1, i + 1),
              z_at=lambda i: z_sb[:, i % NO, :, 2:2 + W], z_free=z_free)

    with nc.Block() as block:
        @block.sync
        def _(sp):
            def load_g(i):
                if i % per_load == 0:
                    n = i // per_load
                    p, r = rows_of(i)
                    after(sp, s_out, (n - NG + 1) * per_load)
                    for dy in range(3):
                        sp.dma_start(g_sb[32 * dy:32 * dy + 32, n % NG, :, :, :],
                                     glob[2 * p:2 * p + 2].rearrange("b c n -> c b n")[:, :, (r + dy) * GP:(r + dy + GR) * GP]
                                     .rearrange("c b (r x) -> c b r x", x=GP)).then_inc(g_in.sem_of(n), 16)

            def load(i):
                p, r = rows_of(i)
                after(sp, s_x1, i - NX + 1)
                sp.dma_start(l_sb[:, i % NX, :], pixels(gated, 2 * p, 2, r, ROWS)).then_inc(xl_in.sem_of(i), 16)
                sp.dma_start(x_sb[:, i % NX, :], pixels(x, 2 * p, 2, r, ROWS)).then_inc(xl_in.sem_of(i), 16)

            def store_x(i):
                p, r = rows_of(i)
                after(sp, s_x1, i + 1)
                sp.dma_start(pixels(x1, 2 * p, 2, r, ROWS), x1_sb[:, i % NO, :]).then_inc(x1_out.sem_of(i), 16)

            def store_z(i):
                p, r = rows_of(i)
                after(sp, ln.s_z, i + 1)
                sp.dma_start(z2[2 * p:2 * p + 2].rearrange("b c n -> (b c) n")[:, (r + 2) * ZP:(r + 2 + ROWS) * ZP],
                             z_sb[:, i % NO, :, :].rearrange("p r x -> p (r x)")).then_inc(z_out.sem_of(i), 16)
            skewed(n_tiles, (0, load_g), (1, load), (4, store_x), (6, store_z))
            x1_out.all_landed(sp, n_tiles)
            z_out.all_landed(sp, n_tiles)

        @block.tensor
        def _(pe):
            def out(i):
                n, j = i // per_load, ROWS * (i % per_load)
                p = i // per_pair
                g_in.landed(pe, n)
                xl_in.landed(pe, i)
                after(pe, s_x1, i - 1)
                for m in range(2):
                    bank = ps_out[i % 2][C * m:C * m + C, :]
                    pe.matmul(bank, w("outL_T", slice(0, 64))[:, C * m:C * m + C], l_sb[:, i % NX, :],
                              start=True, stop=False)
                    for dx in range(3):
                        last = pe.matmul(bank.rearrange("p (r x) -> p r x", x=W), k.conv_v[:, 2 * p + m, dx, :],
                                         g_sb[:, n % NG, m, j:j + ROWS, dx:dx + W], start=False, stop=(dx == 2))
                last.then_inc(s_out, 1)
            skewed(n_tiles, (2, lambda i: ln.variance(pe, i)), (1, lambda i: ln.center(pe, i)), (0, out))

        @block.scalar
        def _(act):
            act.preload_act_table_set(LOG_EXP)
            skewed(n_tiles, (2, lambda i: ln.rstd(act, i)), (1, lambda i: ln.square(act, i)))

        @block.gpsimd
        def _(pool):
            skewed(n_tiles, (0, lambda i: ln.affine(pool, i)))

        @block.vector
        def _(dve):
            dve.memset(z_sb[:, :, :, :], 0.0).then_inc(s_pad, 1)

            def x1_tile(i):
                after(dve, s_out, i + 1)
                after(dve, ln.s_center, i - NO + 1)
                if i >= NO:
                    x1_out.landed(dve, i - NO)
                dve.tensor_tensor(x1_sb[:, i % NO, :], ps_out[i % 2][:, :], x_sb[:, i % NX, :], ALU.add).then_inc(s_x1, 1)
            skewed(n_tiles, (1, lambda i: ln.scale(dve, i)), (0, x1_tile))


@phase
def conv_ffn(k, sb):
    nc, w = k.nc, k.w
    SR = PATCH
    RH = SR + 4
    n_strips = B * H // SR
    per_image = H // SR
    n_sub = SR // ROWS
    n_tiles = n_strips * n_sub
    NZ, NX, NO = 2, 2, 2
    HW2 = W // 2
    z_sb = sb("z", [P, NZ, RH, ZP])
    gelu_sb = sb("gelu", [P, 2, TILE])
    h_sb = sb("h", [P, 2, 16, SR, 16])
    y_sb = sb("y", [P, 2, 8, C])
    f_sb = sb("f", [P, 2, 8, 2, C])
    x_sb = sb("x", [P, NX, SR, HW2])
    o_sb = sb("o", [P, NO, SR, HW2])
    z_in = Slots(k.sem, "z", NZ, per=2)
    x_in = Slots(k.sem, "x", NX, per=2)
    stored = Slots(k.sem, "stored", NO, per=2)
    s_conv, s_gelu, s_h, s_y, s_yc, s_f, s_fw, s_back, s_o = [
        k.sem(n) for n in ("conv", "gelu", "h", "y", "yc", "f", "fw", "back", "o")]
    ps_gate, ps_val, ps_y, ps_f, ps_back = k.banks[0:2], k.banks[2:4], k.banks[4], k.banks[5], k.banks[6:8]
    z2, x1, x2 = k.dram["z2"], k.dram["x1"], k.dram["x2"]
    halves = lambda t, s, m: t[s // per_image].rearrange("c (r x) -> c r x", x=W)[
        :, SR * (s % per_image):SR * (s % per_image) + SR, HW2 * m:HW2 * m + HW2]

    with nc.Block() as block:
        @block.sync
        def _(sp):
            def load_z(s):
                b, r = s // per_image, SR * (s % per_image)
                after(sp, s_conv, n_sub * (s - NZ + 1))
                for m in range(2):
                    sp.dma_start(z_sb[C * m:C * m + C, s % NZ, :, :].rearrange("p r x -> p (r x)"),
                                 z2[b][:, (r + m) * ZP:(r + m + RH) * ZP]).then_inc(z_in.sem_of(s), 16)

            def load_x(s):
                after(sp, s_o, 2 * (s - NX + 1))
                for m in range(2):
                    sp.dma_start(x_sb[C * m:C * m + C, s % NX, :, :], halves(x1, s, m)).then_inc(x_in.sem_of(s), 16)

            def store(s):
                after(sp, s_o, 2 * (s + 1))
                for m in range(2):
                    sp.dma_start(halves(x2, s, m), o_sb[C * m:C * m + C, s % NO, :, :]).then_inc(stored.sem_of(s), 16)
            skewed(n_strips, (0, load_z), (1, load_x), (3, store))
            stored.all_landed(sp, n_strips)

        @block.tensor
        def _(pe):
            def conv(i):
                s, j = i // n_sub, ROWS * (i % n_sub)
                z_in.landed(pe, s)
                after(pe, s_h, i - 1)
                z = lambda dy, dx, rows: z_sb[rows, s % NZ, j + dy:j + dy + ROWS, dx:dx + W]
                both, one = slice(0, P), slice(0, C)
                out = ps_gate[i % 2][:, :].rearrange("p (r x) -> p r x", x=W)
                for n in range(6):
                    pair, dx = n // 3, n % 3
                    rows = one if pair == 1 else both
                    pe.matmul(out, k.conv_gate[rows, pair, dx, :], z(1 + 2 * pair, 1 + dx, rows),
                              start=(n == 0), stop=(n == 5))
                out = ps_val[i % 2][:, :].rearrange("p (r x) -> p r x", x=W)
                for n in range(15):
                    pair, dx = n // 5, n % 5
                    rows = one if pair == 2 else both
                    last = pe.matmul(out, k.conv_val[rows, pair, dx, :], z(2 * pair, dx, rows),
                                     start=(n == 0), stop=(n == 14))
                last.then_inc(s_conv, 1)

            def filtered(s, half):
                u = 2 * s + half
                after(pe, s_h, n_sub * (s + 1))
                after(pe, s_yc, u)
                for g in range(8):
                    last = pe.matmul(ps_y[:, C * g:C * g + C], h_sb[:, s % 2, 8 * half + g, :, :], w("ffn_outT"),
                                     start=True, stop=True)
                last.then_inc(s_y, 1)

            def frequencies(s, half):
                u = 2 * s + half
                after(pe, s_yc, u + 1)
                after(pe, s_fw, u)
                pe.matmul(ps_f[:, :], w("dft"), y_sb[:, u % 2, :, :].rearrange("p g c -> p (g c)"),
                          start=True, stop=True).then_inc(s_f, 1)

            def back(s):
                after(pe, s_fw, 2 * (s + 1))
                for half in range(2):
                    after(pe, s_o, 2 * (s - 1) + half + 1)
                    for g in range(4):
                        last = pe.matmul(ps_back[half][:, P * g:P * g + P],
                                         f_sb[:, s % 2, 4 * half + g, :, :], w("idft"), start=True, stop=True)
                    last.then_inc(s_back, 1)

            for i in range(n_tiles + n_sub):
                if i < n_tiles:
                    conv(i)
                s, j = i // n_sub - 1, i % n_sub
                if s >= 0:
                    if j == 0:
                        filtered(s, 0)
                    elif j == 1:
                        frequencies(s, 0)
                        filtered(s, 1)
                    elif j == 2:
                        frequencies(s, 1)
                    else:
                        back(s)

        @block.scalar
        def _(act):
            for i in range(n_tiles):
                after(act, s_conv, i + 1)
                after(act, s_h, i - 1)
                act.activation(gelu_sb[:, i % 2, :], ps_gate[i % 2][:, :], ACT.Gelu).then_inc(s_gelu, 1)

        @block.vector
        def _(dve):
            def hidden(i):
                s, j = i // n_sub, ROWS * (i % n_sub)
                after(dve, s_gelu, i + 1)
                after(dve, s_y, 2 * (s - 1))
                grouped = lambda t: t.rearrange("p (r g x) -> p r g x", r=ROWS, x=16)
                dve.tensor_tensor(h_sb[:, s % 2, :, j:j + ROWS, :].rearrange("p g r x -> p r g x"),
                                  grouped(ps_val[i % 2][:, :]), grouped(gelu_sb[:, i % 2, :]), ALU.mult).then_inc(s_h, 1)

            def y_copy(u):
                after(dve, s_y, u + 1)
                after(dve, s_f, u - 1)
                dve.tensor_copy(y_sb[:, u % 2, :, :], ps_y[:, :].rearrange("p (g c) -> p g c", g=8)).then_inc(s_yc, 1)

            def weigh(u):
                s, half = u // 2, u % 2
                after(dve, s_f, u + 1)
                after(dve, s_back, 2 * (s - 1))
                dve.tensor_tensor(f_sb[:, s % 2, :, half, :], ps_f[:, :].rearrange("p (g c) -> p g c", g=8),
                                  k.freq_w[:, :].unsqueeze(1).broadcast_to([P, 8, C]), ALU.mult).then_inc(s_fw, 1)

            def out(s):
                x_in.landed(dve, s)
                if s >= NO:
                    stored.landed(dve, s - NO)
                for half in range(2):
                    after(dve, s_back, 2 * s + half + 1)
                    cols = slice(64 * half, 64 * half + 64)
                    view = lambda t: t[:, s % 2, :, cols].rearrange("p y (g x) -> p y g x", x=16)
                    dve.tensor_tensor(view(o_sb), ps_back[half][:, :].rearrange("p (g y x) -> p y g x", g=4, y=SR),
                                      view(x_sb), ALU.add).then_inc(s_o, 1)

            for i in range(n_tiles + n_sub + 1):
                s, j = i // n_sub - 1, i % n_sub
                if s >= 1 and j == 0:
                    out(s - 1)
                if 0 <= s < n_strips:
                    if j == 0:
                        y_copy(2 * s)
                    elif j == 1:
                        weigh(2 * s)
                        y_copy(2 * s + 1)
                    elif j == 2:
                        weigh(2 * s + 1)
                if i < n_tiles:
                    hidden(i)


LINES = 8
SPAN = LINES * W


@phase
def line_attention(k, sb, name):
    nc, w = k.nc, k.w
    cols = name == "col"
    n_units = 2 * H // LINES
    per_pair = H // LINES
    ln_w, ln_b = ("cn_g", "cn_b") if cols else ("rn_g", "rn_b")
    src, dst = (k.dram["h1"], k.dram["h2"]) if cols else (k.dram["x2"], k.dram["h1"])
    BX = 64 if cols else LINES
    NB = 2 if cols else 3
    per_block = BX // LINES
    n_blocks = n_units // per_block
    blk_sb = sb("x", [P, NB, BX * W])
    z_sb = sb("z", [P, 2, SPAN])
    lin_sb = sb("lin", [P, 2, 256])
    low_sb, exp_sb, kq_sb = [sb(n, [P, 256]) for n in ("low", "exp", "kq")]
    inv_sb = sb("inv", [P, LINES, 16])
    zt_sb = sb("zt", [P, 16, P])
    s_sb, g1_sb, g2_sb, g_sb = [sb(n, [P, LINES, 8]) for n in ("s", "g1", "g2", "gm")]
    u_sb = sb("u", [8, LINES, P])
    qt_sb = sb("qt", [8, 2, TILE])
    x_in = Slots(k.sem, "x", NB, per=2 if cols else 1)
    stored = Slots(k.sem, "stored", NB, per=2 if cols else 1)
    names = ("kq", "lin", "low", "exp", "elu", "sum", "inv", "zt", "ztc", "S", "Sc", "V", "g1", "g2", "g",
             "U", "Uc", "qt", "qtc", "app", "h")
    (s_kq, s_lin, s_low, s_exp, s_elu, s_sum, s_inv, s_zt, s_ztc, s_S, s_Sc, s_V, s_g1, s_g2, s_g,
     s_U, s_Uc, s_qt, s_qtc, s_app, s_h) = [k.sem(n) for n in names]
    ps_turn, ps_a, ps_b, ps_app = k.banks[3], k.banks[4], k.banks[5], k.banks[6:8]

    def lines(i):
        u = i // 4
        b = blk_sb[:, u // per_block % NB, :]
        first = u % per_block * LINES + 2 * (i % 4)
        if cols:
            return b.rearrange("p (y x) -> p x y", x=BX)[:, first:first + 2, :]
        return b[:, first * W:first * W + TILE].rearrange("p (l n) -> p l n", n=W)

    def zbuf(i):
        return z_sb[:, i // 4 % 2, i % 4 * TILE:i % 4 * TILE + TILE]

    ln = Norm(sb, k.sem, k.banks[0:3], "ln", w, ln_w, ln_b,
              x_at=lines, x_ready=lambda e, i: x_in.landed(e, i // 4 // per_block),
              z_at=zbuf, z_free=lambda e, i: (after(e, s_kq, i // 4 - 1), after(e, s_zt, 4 * (i // 4 - 1))))

    def block_dmas(t, n):
        p, first = n * BX // H, n * BX % H
        sbuf = blk_sb[:, n % NB, :]
        if not cols:
            return [(pixels(t, 2 * p, 2, first, BX), sbuf)]
        d = t[2 * p:2 * p + 2].rearrange("b c (y x) -> (b c) y x", x=W)[:, :, first:first + BX]
        s = sbuf.rearrange("p (y x) -> p y x", x=BX)
        return [(d[:, m * H // 2:(m + 1) * H // 2, :], s[:, m * H // 2:(m + 1) * H // 2, :]) for m in range(2)]

    with nc.Block() as block:
        @block.sync
        def _(sp):
            def load(n):
                if n >= NB:
                    stored.landed(sp, n - NB)
                for d, s in block_dmas(src, n):
                    sp.dma_start(s, d).then_inc(x_in.sem_of(n), 16)

            def store(n):
                after(sp, s_h, 4 * per_block * (n + 1))
                for d, s in block_dmas(dst, n):
                    sp.dma_start(d, s).then_inc(stored.sem_of(n), 16)
            skewed(n_blocks, (0, load), (NB - 1, store))
            stored.all_landed(sp, n_blocks)

        def rounds(norm, part):
            for u in range(-1, n_units):
                for j in range(4):
                    if u + 1 < n_units:
                        norm(4 * (u + 1) + j)
                    if u >= 0:
                        part(u, j)

        @block.tensor
        def _(pe):
            def norm(i):
                ln.center(pe, i)
                ln.variance(pe, i)

            def turn_z(u, q):
                after(pe, s_ztc, 4 * u + q)
                after(pe, s_qtc, 4 * u)
                for g in range(4):
                    n = 4 * q + g
                    last = pe.matmul(ps_turn[:, P * g:P * g + P], z_sb[:, u % 2, n * P:n * P + P], w("ident"),
                                     start=True, stop=True)
                last.then_inc(s_zt, 1)

            def turn_q(u, q):
                after(pe, s_qtc, 4 * u + q)
                after(pe, s_ztc, 4 * (u + 1))
                for g in range(4):
                    n = 4 * q + g
                    last = pe.matmul(ps_turn[0:8, P * g:P * g + P], kq_sb[:, 16 * n + 8:16 * n + 16], w("ident"),
                                     start=True, stop=True)
                last.then_inc(s_qt, 1)

            def apply(u, q):
                t = 4 * u + q
                after(pe, s_qtc, t + 1)
                after(pe, s_Uc, 2 * u + q // 2 + 1)
                after(pe, s_h, t - 1)
                for m in range(2):
                    last = pe.matmul(ps_app[t % 2][:, W * m:W * m + W], u_sb[:, 2 * q + m, :],
                                     qt_sb[:, t % 2, W * m:W * m + W], start=True, stop=True)
                last.then_inc(s_app, 1)

            def u_rows(u, half):
                after(pe, s_g, u + 1)
                after(pe, s_Uc, 2 * u + half)
                for m in range(4):
                    last = pe.matmul(ps_b[0:8, P * m:P * m + P], g_sb[:, 4 * half + m, :], w(f"{name}_oT"),
                                     start=True, stop=True)
                last.then_inc(s_U, 1)

            def part(u, j):
                if j == 0:
                    after(pe, ln.s_z, 4 * (u + 1))
                    after(pe, s_Sc, u)
                    for n in range(16):
                        last = pe.matmul(ps_a[:, 16 * n:16 * n + 16], z_sb[:, u % 2, n * P:n * P + P], w(f"{name}_kqT"),
                                         start=True, stop=True)
                    last.then_inc(s_kq, 1)
                    turn_z(u, 0)
                    turn_z(u, 1)
                elif j == 1:
                    turn_z(u, 2)
                    after(pe, s_elu, u + 1)
                    after(pe, s_Uc, 2 * u)
                    kq = kq_sb[:, :].rearrange("p (l h c) -> p l h c", h=2, c=16)
                    for h in range(2):
                        last = pe.matmul(ps_b[:, 0:128].rearrange("p (l c) -> p l c", c=16), w("ones"), kq[:, :, h, :],
                                         start=(h == 0), stop=(h == 1))
                    last.then_inc(s_sum, 1)
                    turn_z(u, 3)
                elif j == 2:
                    after(pe, s_ztc, 4 * (u + 1))
                    after(pe, s_lin, u + 1)
                    for l in range(LINES):
                        for h in range(2):
                            n = 2 * l + h
                            last = pe.matmul(ps_a[:, 256 + 8 * l:264 + 8 * l], zt_sb[:, n, :], kq_sb[:, 16 * n:16 * n + 8],
                                             start=(h == 0), stop=(h == 1))
                    last.then_inc(s_S, 1)
                    turn_q(u, 0)
                    after(pe, s_Sc, u + 1)
                    after(pe, s_inv, u + 1)
                    pe.matmul(ps_b[:, 256:320], w(f"{name}_vT"), s_sb[:, :, :].rearrange("p l c -> p (l c)"),
                              start=True, stop=True).then_inc(s_V, 1)
                else:
                    u_rows(u, 0)
                    turn_q(u, 1)
                    u_rows(u, 1)
                    apply(u, 0)
                    turn_q(u, 2)
                    apply(u, 1)
                    turn_q(u, 3)
                    apply(u, 2)
                    apply(u, 3)
            rounds(norm, part)

        @block.scalar
        def _(act):
            act.preload_act_table_set(LOG_EXP)

            def norm(i):
                ln.square(act, i)
                ln.rstd(act, i)

            def part(u, j):
                if j == 0:
                    after(act, s_low, u + 1)
                    after(act, s_elu, u)
                    act.activation(exp_sb[:, :], low_sb[:, :], ACT.Exp).then_inc(s_exp, 1)
                qs = {0: (0, 1), 1: (2, 3)}.get(j, ())
                for q in qs:
                    after(act, s_zt, 4 * u + q + 1)
                    after(act, s_S, u)
                    act.activation(zt_sb[:, 4 * q:4 * q + 4, :], ps_turn[:, :].rearrange("p (g c) -> p g c", g=4),
                                   ACT.Copy).then_inc(s_ztc, 1)
                if j >= 2:
                    for q in ((0,) if j == 2 else (1, 2, 3)):
                        t = 4 * u + q
                        after(act, s_qt, t + 1)
                        after(act, s_app, t - 1)
                        act.activation(qt_sb[:, t % 2, :], ps_turn[0:8, :], ACT.Copy).then_inc(s_qtc, 1)
            rounds(norm, part)

        @block.gpsimd
        def _(pool):
            for i in range(4 * n_units):
                ln.affine(pool, i)

        @block.vector
        def _(dve):
            def part(u, j):
                lin = lin_sb[:, u % 2, :]
                inv_k, inv_q = inv_sb[:, :, 0:8], inv_sb[:, :, 8:16]
                if j == 0:
                    after(dve, s_kq, u + 1)
                    dve.tensor_tensor(lin.rearrange("p (n c) -> p n c", c=16), ps_a[:, 0:256].rearrange("p (n c) -> p n c", c=16),
                                      w(f"{name}_kqb").unsqueeze(1).broadcast_to([P, 16, 16]), ALU.add).then_inc(s_lin, 1)
                    after(dve, s_lin, u + 1)
                    after(dve, s_exp, u)
                    dve.tensor_scalar(low_sb[:, :], lin, 0.0, None, ALU.min).then_inc(s_low, 1)
                    after(dve, s_exp, u + 1)
                    after(dve, s_S, u)
                    after(dve, s_qt, 4 * u)
                    dve.scalar_tensor_tensor(kq_sb[:, :], lin, 0.0, exp_sb[:, :], ALU.max, ALU.add).then_inc(s_elu, 1)
                elif j == 1:
                    after(dve, s_sum, u + 1)
                    after(dve, s_g2, u)
                    dve.reciprocal(inv_sb[:, :, :], ps_b[:, 0:128].rearrange("p (l c) -> p l c", c=16)).then_inc(s_inv, 1)
                elif j == 2:
                    after(dve, s_S, u + 1)
                    after(dve, s_V, u)
                    dve.tensor_copy(s_sb[:, :, :], ps_a[:, 256:320].rearrange("p (l c) -> p l c", c=8)).then_inc(s_Sc, 1)
                    after(dve, s_V, u + 1)
                    after(dve, s_inv, u + 1)
                    dve.tensor_tensor(g1_sb[:, :, :], ps_b[:, 256:320].rearrange("p (l c) -> p l c", c=8), inv_k,
                                      ALU.mult).then_inc(s_g1, 1)
                    after(dve, s_g1, u + 1)
                    dve.scalar_tensor_tensor(g2_sb[:, :, :], g1_sb[:, :, :], w(f"{name}_bv"), inv_q, ALU.add,
                                             ALU.mult).then_inc(s_g2, 1)
                    after(dve, s_g2, u + 1)
                    after(dve, s_U, 2 * u)
                    dve.tensor_tensor(g_sb[:, :, :], g2_sb[:, :, :], w("head_w").unsqueeze(1).broadcast_to([P, LINES, 8]),
                                      ALU.mult).then_inc(s_g, 1)
                else:
                    for half in range(2):
                        after(dve, s_U, 2 * u + half + 1)
                        after(dve, s_app, 4 * u)
                        dve.tensor_copy(u_sb[:, 4 * half:4 * half + 4, :], ps_b[0:8, :].rearrange("p (l c) -> p l c", l=4)
                                        ).then_inc(s_Uc, 1)
                    for q in range(4):
                        t = 4 * u + q
                        after(dve, s_app, t + 1)
                        dve.scalar_tensor_tensor(lines(t), ps_app[t % 2][:, :].rearrange("p (l n) -> p l n", n=W),
                                                 w(f"{name}_bo"), lines(t), ALU.add, ALU.add).then_inc(s_h, 1)
            rounds(lambda i: ln.scale(dve, i), part)


@phase
def ffn(k, sb):
    nc, w = k.nc, k.w
    n_units = 2 * NPIX // TILE // 4
    per_pair = NPIX // TILE // 4
    NX, NO = 3, OUT_SLOTS
    x_sb = sb("x", [P, NX, 4 * TILE])
    z_sb = sb("z", [P, 2, 4 * TILE])
    hid_sb = sb("hid", [P, 4, TILE])
    o_sb = sb("o", [P, NO, 4 * TILE])
    x_in, stored = Slots(k.sem, "x", NX), k.out_stored
    s_hid, s_gelu, s_out, s_o = [k.sem(n) for n in ("hid", "gelu", "out", "o")]
    ps_hid, ps_out = k.banks[3:6], k.banks[6:8]
    h2, out = k.dram["h2"], k.dram["out"]
    at = lambda t, i, n: t[:, i // 4 % n, i % 4 * TILE:i % 4 * TILE + TILE]
    ln = Norm(sb, k.sem, k.banks[0:3], "ln", w, "fn_g", "fn_b",
              x_at=lambda i: at(x_sb, i, NX), x_ready=lambda e, i: x_in.landed(e, i // 4),
              z_at=lambda i: at(z_sb, i, 2), z_free=lambda e, i: after(e, s_hid, 16 * (i // 4 - 1)))

    with nc.Block() as block:
        @block.sync
        def _(sp):
            def load(u):
                after(sp, s_o, 4 * (u - NX + 1))
                sp.dma_start(x_sb[:, u % NX, :], pixels(h2, 2 * (u // per_pair), 2, 8 * (u % per_pair), 8)
                             ).then_inc(x_in.sem_of(u), 16)

            def store(u):
                after(sp, s_o, 4 * (u + 1))
                sp.dma_start(pixels(out, 2 * (u // per_pair), 2, 8 * (u % per_pair), 8), o_sb[:, u % NO, :]
                             ).then_inc(stored.sem_of(u), 16)
            skewed(n_units, (0, load), (2, store))
            stored.all_landed(sp, n_units)

        def rounds(norm, work):
            for u in range(-1, n_units):
                if u + 1 < n_units:
                    norm(4 * (u + 1))
                if u >= 0:
                    for j in range(4):
                        work(4 * u + j)

        @block.tensor
        def _(pe):
            def first(c):
                i, n = c // 4, c % 4
                m = n // 2
                rows = slice(C * m, C * m + C)
                after(pe, ln.s_z, i + 1)
                after(pe, s_gelu, c - 2)
                pe.matmul(ps_hid[c % 3][:, :], w("w1T", rows)[:, P * (n % 2):P * (n % 2) + P], at(z_sb, i, 2)[rows, :],
                          start=True, stop=True).then_inc(s_hid, 1)

            def second(c):
                i, n = c // 4, c % 4
                m = n // 2
                after(pe, s_gelu, c + 1)
                if n == 0:
                    after(pe, s_o, i - 1)
                last = pe.matmul(ps_out[i % 2][C * m:C * m + C, :], w("w2T")[:, C * (n % 2):C * (n % 2) + C],
                                 hid_sb[:, c % 4, :], start=(n % 2 == 0), stop=(n % 2 == 1)).then_inc(s_out, 1)

            def work(i):
                for c in range(4 * i, 4 * i + 4):
                    first(c)
                    if c % 16 >= 2:
                        second(c - 2)
                if i % 4 == 3:
                    second(4 * i + 2)
                    second(4 * i + 3)

            def norm(i):
                skewed(4, (1, lambda j: ln.variance(pe, i + j)), (0, lambda j: ln.center(pe, i + j)))
            rounds(norm, work)

        @block.scalar
        def _(act):
            def gelu(c):
                n = c % 4
                after(act, s_hid, c + 1)
                after(act, s_out, c - 3)
                act.activation(hid_sb[:, c % 4, :], ps_hid[c % 3][:, :], ACT.Gelu, bias=w("b1")[:, n % 2:n % 2 + 1]
                               ).then_inc(s_gelu, 1)
            for u in range(-1, n_units):
                if u + 1 < n_units:
                    act.preload_act_table_set(LOG_EXP)
                    skewed(4, (1, lambda j: ln.rstd(act, 4 * (u + 1) + j)), (0, lambda j: ln.square(act, 4 * (u + 1) + j)))
                if u >= 0:
                    for c in range(16 * u, 16 * u + 16):
                        gelu(c)

        @block.gpsimd
        def _(pool):
            for i in range(4 * n_units):
                ln.affine(pool, i)

        @block.vector
        def _(dve):
            def work(i):
                if i % 4 == 0 and i // 4 >= NO:
                    stored.landed(dve, i // 4 - NO)
                after(dve, s_out, 4 * (i + 1))
                dve.scalar_tensor_tensor(at(o_sb, i, NO), ps_out[i % 2][:, :], w("b2"), at(x_sb, i, NX),
                                         ALU.add, ALU.add).then_inc(s_o, 1)
            rounds(lambda i: skewed(4, (0, lambda j: ln.scale(dve, i + j))), work)


SCRATCH = {
    "local": HALF * 0 + NPIX, "glob": GROWS * GP, "gated": NPIX, "x1": NPIX, "z2": ZROWS * ZP,
    "x2": NPIX, "h1": NPIX, "h2": NPIX,
}
CHANNELS = {"local": HALF, "glob": HALF, "gated": HALF}
PHASES = [(set_up,), (project_in,), (gram,), (attention_weights,), (local_branch, False), (local_branch, True),
          (project_out,), (conv_ffn,), (line_attention, "row"), (line_attention, "col"), (ffn,)]


def build(nc, x, packed, where, out, phases=PHASES, scratch_kind=None):
    with ExitStack() as ctx:
        dram = {"x": x, "out": out}
        for name, n in SCRATCH.items():
            kind = (scratch_kind or {}).get(name, "Internal")
            dram[name] = nc.dram_tensor(f"scratch_{name}", [B, CHANNELS.get(name, C), n], F32, kind=kind).ap()
        k = Program(nc, ctx, where, packed, dram)
        with ExitStack() as ctx0:
            k.layer0(ctx0)
            for fn, *args in phases:
                if fn is line_attention and args == ["row"]:
                    ctx0.close()
                    k.reuse_semaphores()
                fn(k, *args)
        return k


def lay_out(inputs):
    pieces = laid_out(inputs)
    where, at = {}, 0
    for name, piece in pieces.items():
        where[name] = (at, at + piece.shape[1])
        at += piece.shape[1]
    return where, np.ascontiguousarray(np.concatenate(list(pieces.values()), 1))


def kernel(**inputs):
    import concourse.bacc as bacc
    from concourse.bass_utils import run_bass_kernel_spmd

    inputs = {name: np.asarray(v) for name, v in inputs.items()}
    x = np.ascontiguousarray(inputs["x"]).reshape(B, C, NPIX)
    where, packed = lay_out(inputs)
    nc = bacc.Bacc("TRN2", target_bir_lowering=False, num_devices=1)
    x_d = nc.dram_tensor("x", x.shape, F32, kind="ExternalInput").ap()
    w_d = nc.dram_tensor("weights", packed.shape, F32, kind="ExternalInput").ap()
    out_d = nc.dram_tensor("out", x.shape, F32, kind="ExternalOutput").ap()
    build(nc, x_d, w_d, where, out_d)
    r = run_bass_kernel_spmd(nc, [{"x": x, "weights": packed}], core_ids=[0])
    return r.results[0]["out"].reshape(B, C, H, W)
```

```python
from contextlib import ExitStack

import numpy as np
import concourse.bass as bass
import concourse.mybir as mybir

F32 = mybir.dt.float32
F32R = mybir.dt.float32r
ALU = mybir.AluOpType
ACT = mybir.ActivationFunctionType
AX = mybir.AxisListType

B, C, H, W = 4, 64, 256, 256
HALF = C // 2
NPIX = H * W
P = 128
TILE = 512
ROWS = TILE // W
EPS = 1e-5
HEADS = 4
PATCH = 8
OUT_SLOTS = 2
LOG_EXP = "natural_log_exp_and_others"
GP = W + 2
ZP = W + 4
GPAIRS = H // 2 + 1
ZPAIRS = H // 2 + 2


def after(eng, sem, n):
    if n > 0:
        eng.wait_ge(sem, n)


def skewed(n, *steps):
    for t in range(n + max(lag for lag, _ in steps)):
        for lag, step in steps:
            if 0 <= t - lag < n:
                step(t - lag)


class Slots:

    def __init__(self, sem, name, n, per=1):
        self.sems = [sem(f"{name}{k}") for k in range(n)]
        self.n, self.per = n, per

    def sem_of(self, i):
        return self.sems[i % self.n]

    def landed(self, eng, i):
        eng.wait_ge(self.sems[i % self.n], 16 * self.per * (i // self.n + 1))

    def all_landed(self, eng, total):
        for k in range(min(self.n, total)):
            eng.wait_ge(self.sems[k], 16 * self.per * ((total - 1 - k) // self.n + 1))


class Norm:

    def __init__(self, sb, sem, banks, name, w, weight, bias, x_at, x_ready, z_at, z_free, n_center=2, average=None):
        self.ps_center, self.ps_var = banks[:n_center], banks[n_center:]
        self.square_sb = sb(f"{name}_square", [P, n_center, TILE])
        self.average = average
        if average is not None:
            self.hi_sb, self.lo_sb = [sb(f"{name}_{part}", [P, n_center, TILE], F32R) for part in ("hi", "lo")]
            self.s_lo = sem(f"{name}_lo")
        self.rstd_sb = sb(f"{name}_rstd", [P, 2, TILE])
        self.scaled_sb = sb(f"{name}_scaled", [P, 2, TILE])
        names = ("center", "square", "var", "log", "rstd", "scaled", "z")
        self.s_center, self.s_square, self.s_var, self.s_log, self.s_rstd, self.s_scaled, self.s_z = [
            sem(f"{name}_{n}") for n in names]
        self.w, self.weight, self.bias = w, weight, bias
        self.x_at, self.x_ready, self.z_at, self.z_free = x_at, x_ready, z_at, z_free

    def center(self, pe, i):
        self.x_ready(pe, i)
        nc = len(self.ps_center)
        after(pe, self.s_scaled, i + 1 - nc)
        pe.matmul(self.ps_center[i % nc][:, :], self.w("center"), self.x_at(i),
                  start=True, stop=True).then_inc(self.s_center, 1)

    def square(self, act, i):
        after(act, self.s_center, i + 1)
        nc = len(self.ps_center)
        after(act, self.s_var, i + 1 - nc)
        if self.average is not None:
            act.activation(self.hi_sb[:, i % nc, :], self.ps_center[i % nc][:, :], ACT.Square)
        act.activation(self.square_sb[:, i % nc, :], self.ps_center[i % nc][:, :],
                       ACT.Square).then_inc(self.s_square, 1)

    def square_lo(self, pool, i):
        n = i % len(self.ps_center)
        after(pool, self.s_square, i + 1)
        pool.tensor_tensor(self.lo_sb[:, n, :], self.square_sb[:, n, :], self.hi_sb[:, n, :].bitcast(F32),
                           ALU.subtract).then_inc(self.s_lo, 1)

    def variance(self, pe, i):
        nb, n = len(self.ps_var), i % len(self.ps_center)
        after(pe, self.s_square if self.average is None else self.s_lo, i + 1)
        after(pe, self.s_log, i + 1 - nb)
        bank = self.ps_var[i % nb][:, :]
        if self.average is None:
            last = pe.matmul(bank, self.w("average"), self.square_sb[:, n, :], start=True, stop=True)
        else:
            pe.matmul(bank, self.average, self.hi_sb[:, n, :], start=True, stop=False)
            last = pe.matmul(bank, self.average, self.lo_sb[:, n, :], start=False, stop=True)
        last.then_inc(self.s_var, 1)

    def rstd(self, act, i):
        nb = len(self.ps_var)
        r = self.rstd_sb[:, i % 2, :]
        after(act, self.s_var, i + 1)
        after(act, self.s_scaled, i - 1)
        act.activation(r, self.ps_var[i % nb][:, :], ACT.Ln, bias=self.w("eps")).then_inc(self.s_log, 1)
        after(act, self.s_log, i + 1)
        act.activation(r, r, ACT.Exp, scale=-0.5).then_inc(self.s_rstd, 1)

    def scale(self, dve, i):
        after(dve, self.s_rstd, i + 1)
        after(dve, self.s_z, i - 1)
        dve.tensor_tensor(self.scaled_sb[:, i % 2, :], self.ps_center[i % len(self.ps_center)][:, :],
                          self.rstd_sb[:, i % 2, :], ALU.mult).then_inc(self.s_scaled, 1)

    def affine(self, pool, i):
        after(pool, self.s_scaled, i + 1)
        self.z_free(pool, i)
        pool.tensor_scalar(self.z_at(i), self.scaled_sb[:, i % 2, :], self.w(self.weight),
                           self.w(self.bias), ALU.mult, ALU.add).then_inc(self.s_z, 1)



def conv_matrices():
    for part in range(3):
        for dx in range(3):
            yield part, SHIFTED, dx, [[3 - po for po in range(2)], [-po for po in range(2)]]
        for dx in range(3):
            yield part, 1, dx, [[1 + pi - po for po in range(2)] for pi in range(2)]
    for j in range(3):
        for dx in range(5):
            yield 3, j, dx, [[2 * j + pi - po for po in range(2)] for pi in range(2)]


STRIP_PAIRS = PATCH // 2
SHIFTED = STRIP_PAIRS + 2
CONV_MATRICES = list(conv_matrices())


def laid_out(a):
    f = np.float32
    out = {}

    def put(name, x, row=0):
        x = np.asarray(x)
        x = x.reshape(x.shape[0], -1)
        full = np.zeros((P, x.shape[1]), f)
        full[row:row + x.shape[0]] = x
        out[name] = full

    def blocks(n, *m):
        r = m[0].shape[0]
        parts = []
        for x in m:
            y = np.zeros((n * r, n * x.shape[1]), f)
            for k in range(n):
                y[k * r:(k + 1) * r, k * x.shape[1]:(k + 1) * x.shape[1]] = x
            parts.append(y)
        return np.concatenate(parts, 1)

    def column(x, n):
        return np.tile(np.asarray(x).reshape(-1, 1), (n, 1))

    eye, one = np.eye(C, dtype=f), np.ones((C, C), f)
    put("center", blocks(2, eye - one / C))
    put("average", blocks(2, one / C))
    put("ident", np.eye(P, dtype=f))
    put("ones", np.ones((P, P), f))
    put("group4", blocks(P // 4, np.ones((4, 4), f)))
    put("head8", blocks(HEADS, np.ones((8, 8), f)))
    put("eps", np.full((P, 1), EPS, f))
    hm = np.zeros((P, 8), f)
    for m in range(2):
        for h in range(HEADS):
            hm[m * C + 16 * h:m * C + 16 * h + 16, m * HEADS + h] = W
    put("head_w", hm)
    fwd, inv, sel = patch_transform()
    rows = fwd.reshape(PATCH // 2, 2, 2 * PATCH, P)
    dft = np.zeros((2, 2, PATCH // 2, 2, 2 * PATCH, P), f)
    for p in range(2):
        for q in range(2):
            dft[p, q, :, q] = rows[:, p]
    put("dft", dft.reshape(4, P, P).transpose(1, 0, 2))
    put("idft", inv)
    put("pick_w", sel)

    for name, key in (("ln1_w", "L0_conv_ln1_w"), ("ln1_b", "L0_conv_ln1_b"), ("ln2_w", "L0_conv_ln2_w"),
                      ("ln2_b", "L0_conv_ln2_b"), ("rn_g", "L1_conv_rn_g"), ("rn_b", "L1_conv_rn_b"),
                      ("cn_g", "L1_conv_cn_g"), ("cn_b", "L1_conv_cn_b"), ("fn_g", "L1_conv_fn_g"),
                      ("fn_b", "L1_conv_fn_b"), ("b2", "L1_conv_b2")):
        put(name, column(a[key], 2))
    wi = a["L0_conv_in_proj_w"]
    put("in_projT", blocks(2, wi[:HALF].T, wi[HALF:].T))
    put("gate1T", blocks(2, a["L0_conv_gate_w1"].T), row=2 * HALF)
    put("gate1_b", column(a["L0_conv_gate_b1"], 2))
    wide = np.zeros((32, 254), f)
    for m in range(2):
        wide[16 * m:16 * m + 16, 126 + m] = a["L0_conv_gate_w2"][0]
    put("gate2_wide", wide)
    put("gate2_b", column(a["L0_conv_gate_b2"], P))
    for s in ("pre", "post"):
        put(f"{s}T", blocks(4, a[f"L0_conv_lgce_{s}_w"].T))
        put(f"{s}_b", column(a[f"L0_conv_lgce_{s}_b"], 4))
    put("m1w", column(a["L0_conv_cbam_m1w"], 4))
    put("m1b", column(np.repeat(a["L0_conv_cbam_m1b"].reshape(-1), 4), 4))
    put("m2w", column(a["L0_conv_cbam_m2w"], 4))
    put("m2b", column(a["L0_conv_cbam_m2b"], 4))
    put("spw", column(a["L0_conv_cbam_spw"], 4))
    put("spb", column(np.repeat(a["L0_conv_cbam_spb"].reshape(-1), 4), 4))
    qkv, dw = a["L0_conv_qkv_w"], a["L0_conv_qkv_dw"].reshape(96, 9)
    put("qk_w", np.tile(qkv[:64], (2, 1)))
    taps = np.zeros((2, C, 3, 4), f)
    for row in range(2):
        taps[row, :, :, row:row + 3] = dw[:64].reshape(C, 3, 3).transpose(0, 2, 1)
    put("qk_taps", taps.reshape(P, -1))
    put("v_w", qkv[64:])
    put("v_dw", dw[64:])
    wo = a["L0_conv_out_proj_w"]
    put("outA_T", wo[:, :HALF].T)
    put("outL_T", np.tile(blocks(2, wo[:, HALF:].T), (2, 1)))
    put("first_half", np.repeat([[1.0], [0.0]], C, 0))
    put("last_half", np.repeat([[0.0], [1.0]], C, 0))
    put("temp", np.repeat(a["L0_conv_temperature"].reshape(-1), 8).reshape(-1, 1))
    put("scales", np.tile(a["L0_conv_attn_scales"].reshape(1, 4), (32, 1)))
    fi = a["L0_conv_ffn_in_w"]
    dw3, dw5 = a["L0_conv_dw3_w"][:, 0], a["L0_conv_dw5_w"][:, 0]
    depthwise = [dw3[:C], dw3[C:P], dw3[P:], dw5]
    taps = np.zeros((2, C, len(CONV_MATRICES), 2), f)
    for n, (part, _, dx, dys) in enumerate(CONV_MATRICES):
        for pi in range(2):
            for po in range(2):
                if 0 <= dys[pi][po] < depthwise[part].shape[1]:
                    taps[po, :, n, pi] = depthwise[part][:, dys[pi][po], dx]
    put("conv_taps", taps.reshape(P, -1))
    for part in range(4):
        put(f"ffn_in{part}", np.tile(fi[C * part:C * part + C], (2, 1)))
    for part in range(2):
        put(f"ffn_outT{part}", blocks(2, a["L0_conv_ffn_out_w"].T[C * part:C * part + C]))
    put("fftT", a["L0_conv_fft_W"].reshape(C, 40).T)
    for s in ("row", "col"):
        g = {k: a[f"L1_conv_{s}_{k}"] for k in ("wq", "bq", "wk", "bk", "wv", "bv", "wo", "bo")}
        put(f"{s}_kqT", blocks(2, g["wk"].T, g["wq"].T))
        kq = np.concatenate([g["bk"], g["bk"], g["bq"], g["bq"]])
        put(f"{s}_kqb", np.tile(kq.reshape(1, 16), (P, 1)))
        put(f"{s}_vT", blocks(2, g["wv"].T))
        put(f"{s}_oT", blocks(2, g["wo"].T))
        put(f"{s}_bv", column(g["bv"], 2))
        put(f"{s}_bo", column(g["bo"], 2))
    put("w1T", np.tile(a["L1_conv_w1"].T, (2, 1)))
    put("b1", a["L1_conv_b1"].reshape(2, P).T)
    put("w2T", a["L1_conv_w2"].T.reshape(2, P, C).transpose(1, 0, 2))
    return out


def patch_transform():
    n = PATCH
    y, x = np.meshgrid(np.arange(n), np.arange(n), indexing="ij")
    rows_f, rows_i, picks = [], [], []
    for kx in range(n // 2 + 1):
        for ky in range(n):
            mirror = (-ky) % n
            own = kx in (0, n // 2) and ky == mirror
            if kx in (0, n // 2) and ky > mirror:
                continue
            arg = 2 * np.pi * (ky * y + kx * x) / n
            pick = np.zeros(n * (n // 2 + 1))
            if kx in (0, n // 2):
                pick[ky * 5 + kx] += 0.5
                pick[mirror * 5 + kx] += 0.5
            else:
                pick[ky * 5 + kx] = 1.0
            for fn in ((np.cos,) if own else (np.cos, np.sin)):
                rows_f.append(fn(arg).reshape(-1))
                rows_i.append(fn(arg).reshape(-1) * (1 if own else 2) / n ** 2)
                picks.append(pick)
    f, i = np.array(rows_f), np.array(rows_i)
    fwd = np.zeros((n, 2, n, 2, n * n))
    inv = np.zeros((2, n * n, n, 2, n))
    for p in range(2):
        fwd[:, p, :, p, :] = f.reshape(n * n, n, n).transpose(1, 2, 0)
        inv[p, :, :, p, :] = i.reshape(n * n, n, n)
    sel = np.concatenate([np.array(picks)] * 2).T
    return (fwd.reshape(P, P).astype(np.float32), inv.reshape(P, P).astype(np.float32),
            sel.astype(np.float32))


def pixels(t, b0, n, r0, rows):
    return t[b0:b0 + n].rearrange("b c n -> (b c) n")[:, r0 * W:(r0 + rows) * W]


def by_parity(t, width):
    return t.rearrange("b c (q r x) -> b c q r x", q=2, x=width)


def row_pairs(t, s, per_image, n, width, first=0):
    at = n * (s % per_image) + first
    image = by_parity(t[s // per_image:s // per_image + 1], width)[0]
    return image[:, :, at:at + n, :].rearrange("c q r x -> q c (r x)")



class Program:

    def __init__(self, nc, ctx, where, packed, dram):
        self.nc, self.ctx, self.where, self.packed, self.dram = nc, ctx, where, packed, dram
        self.n_sem, self.sems, self.sem_ctx = 0, [], ctx.enter_context(ExitStack())
        self.out_stored = Slots(lambda name: ctx.enter_context(nc.semaphore(name)), "out_stored", OUT_SLOTS)
        self.all_w = self.keep("all_w", [P, packed.shape[1]])
        self.psum = ctx.enter_context(nc.psum_tensor("psum", [P, 8, TILE], F32))
        self.banks = [self.psum[:, n, :] for n in range(8)]

    def layer0(self, ctx):
        keep = lambda name, shape, dtype=F32: ctx.enter_context(self.nc.sbuf_tensor(name, shape, dtype))
        self.conv_qk = keep("conv_qk", [P, 3, P])
        self.v_taps = keep("v_taps", [32, 3, 160])
        self.average = keep("average", [P, P], F32R)
        self.out_hi = keep("out_hi", [P, B, 3, P], F32R)
        self.out_lo = keep("out_lo", [P, B, 3, P], F32R)
        self.out_local_hi = keep("out_local_hi", [P, P], F32R)
        self.out_local_lo = keep("out_local_lo", [P, P], F32R)
        self.conv_hi = keep("conv_hi", [P, len(CONV_MATRICES), P], F32R)
        self.conv_lo = keep("conv_lo", [P, len(CONV_MATRICES), P], F32R)
        self.freq_w = keep("freq_w", [P, C])
        self.local_sum = keep("local_sum", [2 * HALF, 2, NPIX // TILE])
        self.gate_sum = keep("gate_sum", [P, 4])
        self.gram = keep("gram", [64, B, 64])
        self.cw = keep("cw", [P, 1])
        self.resp_sum = keep("resp_sum", [P, NPIX // TILE])
        self.threshold = keep("threshold", [P, 1])

    def keep(self, name, shape):
        return self.ctx.enter_context(self.nc.sbuf_tensor(name, shape, F32))

    def sem(self, name):
        self.n_sem += 1
        made = self.sem_ctx.enter_context(self.nc.semaphore(f"s{self.n_sem}_{name}"))
        self.sems.append(made)
        return made

    def reuse_semaphores(self):
        for sem in self.sems:
            self.nc.sync.sem_clear(sem)
        self.nc.all_engine_barrier()
        self.sem_ctx.close()
        self.sems = []

    def w(self, name, rows=slice(0, P)):
        a, b = self.where[name]
        return self.all_w[rows, a:b]


def phase(fn):
    def run(k, *args):
        with ExitStack() as ctx:
            def sb(name, shape, dtype=F32):
                return ctx.enter_context(k.nc.sbuf_tensor(f"{fn.__name__}{args}_{name}".replace("'", ""), shape, dtype))
            fn(k, sb, *args)
    return run


@phase
def set_up(k, sb):
    nc, w = k.nc, k.w
    n_conv, per_bank, first_bank, n_banks = len(CONV_MATRICES), TILE // P, 1, 6
    s_w, s_zero, s_rows, s_prod_qk, s_prod, s_turn, s_hi, s_split, s_copy = [k.sem(n) for n in (
        "w", "zero", "rows", "prod_qk", "prod", "turn", "hi", "split", "copy")]
    zeros = sb("zeros", [P, 2, ZP])
    prod_qk = sb("prod_qk", [P, 3, P])
    prod = sb("prod", [P, n_conv, P])
    glob, z2 = k.dram["glob"], k.dram["z2"]
    groups = [list(range(n, min(n + per_bank, n_conv))) for n in range(0, n_conv, per_bank)]
    bank = lambda g: k.banks[first_bank + g % n_banks][:, 0:P * len(groups[g])].rearrange("p (n m) -> p n m", m=P)

    with nc.Block() as block:
        @block.sync
        def _(sp):
            sp.dma_start(k.all_w[:, :], k.packed).then_inc(s_w, 16)
            after(sp, s_zero, 1)
            g = by_parity(glob, GP).rearrange("b c q r x -> (b c) q r x")
            border = zeros[:, 0, 0:GP]
            sp.dma_start(g[:, 0, 0, :], border).then_inc(s_rows, 16)
            sp.dma_start(g[:, 1, GPAIRS - 1, :], border).then_inc(s_rows, 16)
            for p in range(2):
                z = by_parity(z2[2 * p:2 * p + 2], ZP).rearrange("b c q r x -> (b c) q r x")
                for pair in (0, ZPAIRS - 1):
                    sp.dma_start(z[:, :, pair, :], zeros[:, :, :]).then_inc(s_rows, 16)
            sp.wait_ge(s_rows, 16 * 6)

        @block.vector
        def _(dve):
            dve.memset(zeros[:, :, :], 0.0).then_inc(s_zero, 1)
            dve.memset(k.v_taps[:, :, :], 0.0).then_inc(s_zero, 1)
            dve.wait_ge(s_w, 16)
            dve.wait_ge(s_zero, 2)
            for dx in range(3):
                for row in range(4):
                    last = dve.tensor_scalar(prod_qk[:, dx, 32 * row:32 * row + 32], w("qk_w"),
                                             w("qk_taps")[:, 4 * dx + row:4 * dx + row + 1], None, ALU.mult)
                for dy in range(3):
                    t = dy * 3 + dx
                    dve.tensor_scalar(k.v_taps[:, dx, 32 * dy + 32:32 * dy + 64], w("v_w", slice(0, 32)),
                                      w("v_dw", slice(0, 32))[:, t:t + 1], None, ALU.mult)
            last.then_inc(s_prod_qk, 1)
            for g, group in enumerate(groups):
                for n in group:
                    for pi in range(2):
                        last = dve.tensor_scalar(prod[:, n, C * pi:C * pi + C], w(f"ffn_in{CONV_MATRICES[n][0]}"),
                                                 w("conv_taps")[:, 2 * n + pi:2 * n + pi + 1], None, ALU.mult)
                last.then_inc(s_prod, 1)
            for g, group in enumerate(groups):
                after(dve, s_hi, g + 1)
                dve.tensor_tensor(k.conv_lo[:, group[0]:group[-1] + 1, :], bank(g),
                                  k.conv_hi[:, group[0]:group[-1] + 1, :].bitcast(F32), ALU.subtract).then_inc(s_split, 1)
            dve.tensor_copy(k.conv_qk[:, :, :], k.banks[0][:, 0:3 * P].rearrange("p (d m) -> p d m", d=3))
            dve.tensor_copy(k.freq_w[:, :], k.banks[7][:, 0:C]).then_inc(s_copy, 1)

        @block.scalar
        def _(act):
            act.wait_ge(s_w, 16)
            act.activation(k.average[:, :], w("average"), ACT.Copy)
            for g, group in enumerate(groups):
                after(act, s_turn, g + 1)
                act.activation(k.conv_hi[:, group[0]:group[-1] + 1, :], bank(g), ACT.Copy).then_inc(s_hi, 1)

        @block.tensor
        def _(pe):
            pe.wait_ge(s_w, 16)
            pe.wait_ge(s_prod_qk, 1)
            for dx in range(3):
                pe.matmul(k.banks[0][:, P * dx:P * dx + P], prod_qk[:, dx, :], w("ident"), start=True, stop=True)
            pe.matmul(k.banks[7][:, 0:C], w("pick_w", slice(0, 40)), w("fftT", slice(0, 40)),
                      start=True, stop=True)
            for g, group in enumerate(groups):
                after(pe, s_prod, g + 1)
                after(pe, s_split, g + 1 - n_banks)
                for n in group:
                    last = pe.matmul(bank(g)[:, n - group[0], :], prod[:, n, :], w("ident"), start=True, stop=True)
                last.then_inc(s_turn, 1)


@phase
def project_in(k, sb):
    nc, w = k.nc, k.w
    n_tiles = 2 * NPIX // TILE
    per_pair = NPIX // TILE
    NX, NZ, NO = 6, 3, 4
    x_sb = sb("x", [P, NX, TILE])
    z_sb = sb("z", [P, NZ, TILE])
    proj_sb = sb("proj", [P, NO, ROWS, GP])
    hid_sb = sb("hid", [32, 2, TILE])
    g_sb = sb("g", [P, 2, TILE])
    neg_b2 = sb("neg_b2", [P, 1])
    x_in = Slots(k.sem, "x", NX)
    stored = Slots(k.sem, "stored", NO, per=3)
    s_pad, s_proj, s_projc, s_hid, s_hidc, s_gate, s_g1, s_g2, s_g3, s_g4 = [
        k.sem(n) for n in ("pad", "proj", "projc", "hid", "hidc", "gate", "g1", "g2", "g3", "g4")]
    ps_proj, ps_hid, ps_gate = k.banks[4], k.banks[5], k.banks[6:8]
    x, local, glob = k.dram["x"], k.dram["local"], k.dram["glob"]

    ln = Norm(sb, k.sem, k.banks[0:4], "ln", w, "ln1_w", "ln1_b", n_center=3, average=k.average[:, :],
              x_at=lambda i: x_sb[:, i % NX, :], x_ready=lambda e, i: x_in.landed(e, i),
              z_at=lambda i: z_sb[:, i % NZ, :], z_free=lambda e, i: after(e, s_proj, i - NZ + 1))

    with nc.Block() as block:
        @block.sync
        def _(sp):
            def load(i):
                after(sp, ln.s_center, i - NX + 1)
                sp.dma_start(x_sb[:, i % NX, :],
                             pixels(x, 2 * (i // per_pair), 2, ROWS * (i % per_pair), ROWS)).then_inc(x_in.sem_of(i), 16)

            def store(i):
                p, r = i // per_pair, ROWS * (i % per_pair)
                after(sp, s_projc, i + 1)
                sp.dma_start(pixels(local, 2 * p, 2, r, ROWS).rearrange("p (r x) -> p r x", x=W),
                             proj_sb[0:64, i % NO, :, 1:1 + W]).then_inc(stored.sem_of(i), 16)
                g = by_parity(glob[2 * p:2 * p + 2], GP).rearrange("b c q r x -> (b c) q r x")
                for row in range(ROWS):
                    sp.dma_start(g[:, 1 - row, r // 2 + row, :], proj_sb[64:128, i % NO, row, :]
                                 ).then_inc(stored.sem_of(i), 16)
            skewed(n_tiles, (0, load), (NX, store))
            stored.all_landed(sp, n_tiles)

        @block.tensor
        def _(pe):
            def proj(i):
                after(pe, ln.s_z, i + 1)
                after(pe, s_projc, i)
                pe.matmul(ps_proj[:, :], w("in_projT"), z_sb[:, i % NZ, :], start=True, stop=True).then_inc(s_proj, 1)

            def hidden(i):
                after(pe, s_projc, i + 1)
                after(pe, s_hidc, i)
                pe.matmul(ps_hid[0:32, :].rearrange("p (r x) -> p r x", x=W), w("gate1T", slice(64, P)),
                          proj_sb[64:P, i % NO, :, 1:1 + W], start=True, stop=True).then_inc(s_hid, 1)

            def gate(i):
                j = i % 64
                after(pe, s_hidc, i + 1)
                if j == 0:
                    after(pe, s_g1, i // 64 - 1)
                pe.matmul(ps_gate[i // 64 % 2][:, :], w("gate2_wide", slice(0, 32))[:, 126 - 2 * j:254 - 2 * j],
                          hid_sb[:, i % 2, :], start=(j == 0), stop=(j == 63)).then_inc(s_gate, 1)
            skewed(n_tiles, (6, gate), (5, hidden), (4, proj), (2, lambda i: ln.variance(pe, i)),
                   (0, lambda i: ln.center(pe, i)))

        @block.scalar
        def _(act):
            act.preload_act_table_set(LOG_EXP)

            def gate_exp(i):
                n = i // 64
                if i % 64 == 63:
                    after(act, s_gate, i + 1)
                    after(act, s_pad, 2)
                    after(act, s_g4, n - 1)
                    act.activation(g_sb[:, n % 2, :], ps_gate[n % 2][:, :], ACT.Exp, bias=neg_b2[:, :],
                                   scale=-1.0).then_inc(s_g1, 1)
            skewed(n_tiles, (2, lambda i: ln.rstd(act, i)), (0, lambda i: ln.square(act, i)), (7, gate_exp))

        @block.gpsimd
        def _(pool):
            skewed(n_tiles, (2, lambda i: ln.affine(pool, i)), (0, lambda i: ln.square_lo(pool, i)))

        @block.vector
        def _(dve):
            dve.memset(proj_sb[:, :, :, :], 0.0).then_inc(s_pad, 1)
            dve.tensor_scalar(neg_b2[:, :], w("gate2_b"), -1.0, None, ALU.mult).then_inc(s_pad, 1)
            dve.wait_ge(s_pad, 2)

            def copy(i):
                p, t = i // per_pair, i % per_pair
                after(dve, s_proj, i + 1)
                if i >= NO:
                    stored.landed(dve, i - NO)
                after(dve, s_hid, i - NO + 1)
                for rows, acc in ((slice(0, 64), k.local_sum[:, p, t:t + 1]), (slice(64, P), None)):
                    src = ps_proj[rows, :].rearrange("p (r x) -> p r x", x=W)
                    dst = proj_sb[rows, i % NO, :, 1:1 + W]
                    if acc is not None:
                        dve.tensor_scalar(dst, src, 0.0, 0.0, ALU.add, ALU.add, accum_out=acc)
                    else:
                        dve.tensor_copy(dst, src).then_inc(s_projc, 1)

            def relu(i):
                after(dve, s_hid, i + 1)
                after(dve, s_gate, i - 1)
                dve.tensor_scalar(hid_sb[:, i % 2, :], ps_hid[0:32, :], w("gate1_b", slice(0, 32)), 0.0,
                                  ALU.add, ALU.max).then_inc(s_hidc, 1)

            def gate_sum(i):
                n = i // 64
                if i % 64 == 63:
                    g = g_sb[:, n % 2, :]
                    after(dve, s_g1, n + 1)
                    dve.tensor_scalar(g, g, 1.0, None, ALU.add).then_inc(s_g2, 1)
                    after(dve, s_g2, n + 1)
                    dve.reciprocal(g, g).then_inc(s_g3, 1)
                    after(dve, s_g3, n + 1)
                    dve.tensor_reduce(k.gate_sum[:, n:n + 1], g, AX.X, ALU.add).then_inc(s_g4, 1)
            skewed(n_tiles, (5, relu), (4, copy), (2, lambda i: ln.scale(dve, i)), (7, gate_sum))


@phase
def gram(k, sb):
    nc = k.nc
    PAIRS = 4
    per_image = H // 2 // PAIRS
    n_groups = B * per_image
    NG, NB, NQ = 3, 5, 3
    n_bank = PAIRS * W // P // 4
    n_units = n_groups * n_bank
    units = per_image * n_bank
    g_sb = sb("g", [P, NG, PAIRS, GP])
    qk_sb = sb("qk", [P, NQ, 4, P])
    odd_sb = sb("odd", [64, B, 64])
    g_in = Slots(k.sem, "g", NG, per=2)
    s_qk, s_qkc, s_gram, s_kept = [k.sem(n) for n in ("qk", "qkc", "gram", "kept")]
    glob = k.dram["glob"]
    ps_gram = k.banks[NB:NB + 2]

    with nc.Block() as block:
        @block.sync
        def _(sp):
            for s in range(n_groups):
                after(sp, s_qk, n_bank * (s - NG + 1))
                for m in range(2):
                    sp.dma_start(g_sb[C * m:C * m + C, s % NG, :, :].rearrange("p r x -> p (r x)"),
                                 row_pairs(glob, s, per_image, PAIRS, GP, m)).then_inc(g_in.sem_of(s), 16)

        @block.tensor
        def _(pe):
            def conv(u):
                s = u // n_bank
                g_in.landed(pe, s)
                after(pe, s_qkc, u - NB + 1)
                for g in range(4):
                    px = (u % n_bank) * 4 + g
                    row, col = px * P // W, px * P % W
                    for dx in range(3):
                        last = pe.matmul(k.banks[u % NB][:, P * g:P * g + P], g_sb[:, s % NG, row, col + dx:col + dx + P],
                                         k.conv_qk[:, dx, :], start=(dx == 0), stop=(dx == 2))
                last.then_inc(s_qk, 1)

            def products(u):
                b, v = u // units, u % units
                after(pe, s_qkc, u + 1)
                if v == 0:
                    after(pe, s_kept, b - 1)
                for g in range(4):
                    last = pe.matmul(ps_gram[b % 2][:, 0:P], qk_sb[:, u % NQ, g, :], qk_sb[:, u % NQ, g, :],
                                     start=(v == 0 and g == 0), stop=(v == units - 1 and g == 3))
                last.then_inc(s_gram, 1)
            skewed(n_units, (2, products), (0, conv))

        @block.vector
        def _(dve):
            def copy(u):
                after(dve, s_qk, u + 1)
                after(dve, s_gram, u - NQ + 1)
                dve.tensor_copy(qk_sb[:, u % NQ, :, :], k.banks[u % NB][:, :].rearrange("p (g c) -> p g c", g=4)
                                ).then_inc(s_qkc, 1)

            def keep(u):
                if (u + 1) % units == 0:
                    b = u // units
                    after(dve, s_gram, u + 1)
                    dve.tensor_copy(k.gram[:, b, :], ps_gram[b % 2][0:64, 0:64])
                    dve.tensor_copy(odd_sb[:, b, :], ps_gram[b % 2][64:P, 64:P]).then_inc(s_kept, 1)
            skewed(n_units, (3, keep), (0, copy))
            after(dve, s_kept, B)
            dve.tensor_tensor(k.gram[:, :, :], k.gram[:, :, :], odd_sb[:, :, :], ALU.add)


@phase
def attention_weights(k, sb):
    nc, w = k.nc, k.w
    s_dve, s_pe, s_act, s_dma = [k.sem(n) for n in ("dve", "pe", "act", "dma")]
    v3 = lambda n, *shape: sb(n, [32, B] + list(shape))
    kdiag = sb("kdiag", [64, B, 32])
    qdiag, kn = v3("qdiag", 32), v3("kn", 32)
    qn, full, scores, bigger, cmp, keep, expo, rowv, prob = (
        v3("qn", 1), v3("full", 32), v3("scores", 8), v3("bigger", 8), v3("cmp", 8), v3("keep", 8),
        v3("expo", 8), v3("rowv", 1), v3("prob", 32))
    gsum, gmean, ssum, rv_sb = sb("gsum", [P, 1]), sb("gmean", [32, 1]), sb("ssum", [32, 1]), sb("rv", [32, B, C])
    m_pair, m_all = sb("m_pair", [64, 2]), sb("m_all", [P, 1])
    pooled, h1, m1 = sb("pooled", [P, 1]), sb("h1", [P, 1]), sb("m1", [P, P])

    steps = []

    def step(engine, fn):
        steps.append((engine, fn))

    def run(eng, name):
        sems = {"dve": s_dve, "pe": s_pe, "act": s_act, "dma": s_dma}
        done = {"dve": 0, "pe": 0, "act": 0, "dma": 0}
        for n, (engine, fn) in enumerate(steps):
            if engine == name:
                if n:
                    before = steps[n - 1][0]
                    eng.wait_ge(sems[before], done[before])
                fn(eng).then_inc(sems[name], 16 if name == "dma" else 1)
            done[engine] += 16 if engine == "dma" else 1

    r32 = slice(0, 32)
    bank = k.banks[0]
    step("dve", lambda e: e.tensor_reduce(m_pair[:, :], k.local_sum[:, :, :], AX.X, ALU.add))
    step("dve", lambda e: e.tensor_copy(m_all[0:64, :], m_pair[:, 0:1]))
    step("dma", lambda e: e.dma_start(m_all[64:P, :], m_pair[:, 1:2]))
    step("pe", lambda e: e.matmul(bank[:, 0:1], w("preT"), m_all[:, :], start=True, stop=True))
    step("dve", lambda e: e.tensor_scalar(pooled[:, :], bank[:, 0:1], 1.0 / NPIX, w("pre_b"), ALU.mult, ALU.add))
    step("dve", lambda e: e.tensor_scalar(m1[:, :], w("group4"), w("m1w"), None, ALU.mult))
    step("pe", lambda e: e.matmul(bank[:, 0:1], m1[:, :], pooled[:, :], start=True, stop=True))
    step("dve", lambda e: e.tensor_scalar(h1[:, :], bank[:, 0:1], w("m1b"), 0.0, ALU.add, ALU.max))
    step("dve", lambda e: e.tensor_tensor(h1[:, :], h1[:, :], w("m2w"), ALU.mult))
    step("act", lambda e: e.activation(k.cw[:, :], h1[:, :], ACT.Sigmoid, bias=w("m2b")))
    step("dve", lambda e: e.tensor_reduce(gsum[:, :], k.gate_sum[:, :], AX.X, ALU.add))
    step("pe", lambda e: e.matmul(bank[0:32, 0:1], w("ones")[:, 0:32], gsum[:, :], start=True, stop=True))
    step("dve", lambda e: e.tensor_scalar(gmean[:, :], bank[0:32, 0:1], 8.0 / (B * NPIX), 1.0, ALU.mult, ALU.max))
    for b in range(B):
        step("dve", lambda e, b=b: e.tensor_tensor(qdiag[:, b, :], k.gram[0:32, b, 0:32], w("ident", r32)[:, 0:32], ALU.mult))
        step("dve", lambda e, b=b: e.tensor_tensor(kdiag[32:64, b, :], k.gram[32:64, b, 32:64],
                                                   w("ident", slice(32, 64))[:, 32:64], ALU.mult))
    step("dve", lambda e: e.tensor_reduce(qn[:, :, :].rearrange("p b o -> p (b o)"), qdiag[:, :, :], AX.X, ALU.add))
    step("pe", lambda e: e.matmul(bank[0:32, 0:128], w("ones", slice(32, 64))[:, 0:32],
                                  kdiag[32:64, :, :].rearrange("p b c -> p (b c)"), start=True, stop=True))
    step("act", lambda e: e.activation(kn[:, :, :].rearrange("p b c -> p (b c)"), bank[0:32, 0:128], ACT.Sqrt))
    step("act", lambda e: e.activation(qn[:, :, :], qn[:, :, :], ACT.Sqrt))
    for t in (kn, qn):
        step("dve", lambda e, t=t: e.tensor_scalar(t[:, :, :], t[:, :, :], 1e-12, None, ALU.max))
        step("dve", lambda e, t=t: e.reciprocal(t[:, :, :], t[:, :, :]))
    for b in range(B):
        step("dve", lambda e, b=b: e.scalar_tensor_tensor(full[:, b, :], k.gram[0:32, b, 32:64], qn[:, b, :],
                                                          kn[:, b, :], ALU.mult, ALU.mult))
        step("dve", lambda e, b=b: e.scalar_tensor_tensor(full[:, b, :], full[:, b, :], w("temp", r32),
                                                          w("head8", r32), ALU.mult, ALU.mult))
        step("dve", lambda e, b=b: e.tensor_reduce(scores[:, b, :], full[:, b, :].rearrange("p (h d) -> p d h", h=HEADS),
                                                   AX.X, ALU.add))
    step("dve", lambda e: e.memset(bigger[:, :, :], 1.0))
    for d in range(8):
        step("dve", lambda e, d=d: e.tensor_tensor(cmp[:, :, :], scores[:, :, d:d + 1].broadcast_to([32, B, 8]),
                                                   scores[:, :, :], ALU.is_gt))
        step("dve", lambda e: e.tensor_tensor(bigger[:, :, :], bigger[:, :, :], cmp[:, :, :], ALU.add))
    step("dve", lambda e: e.tensor_scalar(keep[:, :, :], bigger[:, :, :], gmean[:, :], None, ALU.is_le))
    step("dve", lambda e: e.tensor_reduce(rowv[:, :, :].rearrange("p b o -> p (b o)"), scores[:, :, :], AX.X, ALU.max))
    step("dve", lambda e: e.tensor_tensor(expo[:, :, :], scores[:, :, :], rowv[:, :, :].broadcast_to([32, B, 8]), ALU.subtract))
    step("act", lambda e: e.activation(expo[:, :, :], expo[:, :, :], ACT.Exp))
    step("dve", lambda e: e.tensor_tensor(expo[:, :, :], expo[:, :, :], keep[:, :, :], ALU.mult))
    step("dve", lambda e: e.tensor_reduce(rowv[:, :, :].rearrange("p b o -> p (b o)"), expo[:, :, :], AX.X, ALU.add))
    step("dve", lambda e: e.reciprocal(rowv[:, :, :], rowv[:, :, :]))
    step("dve", lambda e: e.tensor_reduce(ssum[:, :], w("scales", r32), AX.X, ALU.add))
    step("dve", lambda e: e.tensor_scalar(rowv[:, :, :], rowv[:, :, :], ssum[:, :], None, ALU.mult))
    step("dve", lambda e: e.tensor_tensor(expo[:, :, :], expo[:, :, :], rowv[:, :, :].broadcast_to([32, B, 8]), ALU.mult))
    for b in range(B):
        for h in range(HEADS):
            step("dve", lambda e, b=b, h=h: e.tensor_tensor(prob[:, b, 8 * h:8 * h + 8], expo[:, b, :],
                                                            w("head8", r32)[:, 8 * h:8 * h + 8], ALU.mult))
    for b in range(B):
        step("pe", lambda e, b=b: e.matmul(bank[0:32, C * b:C * b + C], prob[:, b, :], w("outA_T", r32), start=True, stop=True))
    step("dve", lambda e: e.tensor_copy(rv_sb[:, :, :], bank[0:32, 0:B * C].rearrange("p (b c) -> p b c", b=B)))
    for b in range(B):
        for dx in range(3):
            for row in range(2):
                step("pe", lambda e, b=b, dx=dx, row=row: e.matmul(
                    k.banks[1 + b][:, P * dx + C * row:P * dx + C * row + C],
                    k.v_taps[:, dx, 32 - 32 * row:160 - 32 * row], rv_sb[:, b, :], start=True, stop=True))
        made = k.banks[1 + b][:, 0:3 * P].rearrange("p (d c) -> p d c", d=3)
        step("act", lambda e, b=b, made=made: e.activation(k.out_hi[:, b, :, :], made, ACT.Copy))
        step("dve", lambda e, b=b, made=made: e.tensor_tensor(k.out_lo[:, b, :, :], made, k.out_hi[:, b, :, :].bitcast(F32),
                                                              ALU.subtract))
    step("act", lambda e: e.activation(k.out_local_hi[:, :], w("outL_T"), ACT.Copy))
    step("dve", lambda e: e.tensor_tensor(m1[:, :], w("outL_T"), k.out_local_hi[:, :].bitcast(F32), ALU.subtract))
    step("dve", lambda e: e.tensor_scalar(k.out_local_lo[:, :], m1[:, :], w("first_half"), None, ALU.mult))

    with nc.Block() as block:
        @block.sync
        def _(sp):
            run(sp, "dma")

        @block.vector
        def _(dve):
            run(dve, "dve")

        @block.tensor
        def _(pe):
            run(pe, "pe")

        @block.scalar
        def _(act):
            run(act, "act")


@phase
def local_branch(k, sb, last):
    nc, w = k.nc, k.w
    n_tiles = NPIX // TILE
    NL, NB, NO = 10, 4, 6
    l_sb = sb("l", [P, NL, TILE])
    xg_sb, xa_sb, m_sb, r_sb, y_sb = [sb(n, [P, NB, TILE]) for n in ("xg", "xa", "m", "r", "y")]
    o_sb = sb("o", [P, NO, TILE])
    spread = sb("spread", [P, P])
    total = sb("total", [P, 1])
    l_in = Slots(k.sem, "l", NL)
    stored = Slots(k.sem, "stored", NO)
    names = ("spread", "pre", "xg", "xa", "sw", "sig", "m", "r", "mask", "y", "post", "o", "thr")
    s_spread, s_pre, s_xg, s_xa, s_sw, s_sig, s_m, s_r, s_mask, s_y, s_post, s_o, s_thr = [k.sem(n) for n in names]
    ps_pre, ps_sw, ps_sig, ps_post = k.banks[0:2], k.banks[2], k.banks[3:5], k.banks[5:7]
    local, gated = k.dram["local"], k.dram["gated"]

    with nc.Block() as block:
        @block.sync
        def _(sp):
            def load(i):
                after(sp, s_o if last else s_pre, i - NL + 1)
                sp.dma_start(l_sb[:, i % NL, :], pixels(local, 0, B, ROWS * i, ROWS)).then_inc(l_in.sem_of(i), 16)

            def store(i):
                after(sp, s_o, i + 1)
                sp.dma_start(by_parity(gated, W).rearrange("b c q r x -> (b c) q r x")[:, :, i, :],
                             o_sb[:, i % NO, :].rearrange("p (q x) -> p q x", q=2)).then_inc(stored.sem_of(i), 16)
            skewed(n_tiles, (0, load), *([(NL - 1, store)] if last else []))
            if last:
                stored.all_landed(sp, n_tiles)

        @block.tensor
        def _(pe):
            after(pe, s_spread, 1)

            def pre(i):
                l_in.landed(pe, i)
                after(pe, s_xa, i - 1)
                if last:
                    after(pe, s_xg, i - 1)
                pe.matmul(ps_pre[i % 2][:, :], w("preT"), l_sb[:, i % NL, :], start=True, stop=True).then_inc(s_pre, 1)

            def sw(i):
                after(pe, s_xa, i + 1)
                after(pe, s_sig, i)
                pe.matmul(ps_sw[:, :], spread[:, :], xa_sb[:, i % NB, :], start=True, stop=True).then_inc(s_sw, 1)

            def post(i):
                after(pe, s_y, i + 1)
                after(pe, s_o, i - 1)
                pe.matmul(ps_post[i % 2][:, :], w("postT"), y_sb[:, i % NB, :], start=True, stop=True).then_inc(s_post, 1)
            skewed(n_tiles, (0, pre), (1, sw), *([(4, post)] if last else []))

            def thr(pe):
                after(pe, s_thr, 1)
                pe.matmul(k.banks[7][:, 0:1], w("group4"), total[:, :], start=True, stop=True).then_inc(s_thr, 1)
            if not last:
                thr(pe)

        @block.scalar
        def _(act):
            def xg(i):
                after(act, s_pre, i + 1)
                after(act, s_xa, i + 1)
                if last:
                    after(act, s_y, i + 1 - NB)
                    act.activation(xg_sb[:, i % NB, :], ps_pre[i % 2][:, :], ACT.Identity, bias=w("pre_b")).then_inc(s_xg, 1)

            def sig(i):
                after(act, s_sw, i + 1)
                after(act, s_m, i - 1)
                act.activation(ps_sig[i % 2][:, :], ps_sw[:, :], ACT.Sigmoid, bias=w("spb")).then_inc(s_sig, 1)

            def resp(i):
                after(act, s_m, i + 1)
                if last:
                    after(act, s_y, i + 1 - NB)
                    act.activation(r_sb[:, i % NB, :], m_sb[:, i % NB, :], ACT.Sigmoid).then_inc(s_r, 1)
                else:
                    act.activation(r_sb[:, i % NB, :], m_sb[:, i % NB, :], ACT.Sigmoid,
                                   accum_out=k.resp_sum[:, i:i + 1]).then_inc(s_r, 1)
            skewed(n_tiles, (2, resp), (1, sig), *([(0, xg)] if last else []))

        @block.vector
        def _(dve):
            dve.tensor_scalar(spread[:, :], w("group4"), w("spw"), None, ALU.mult).then_inc(s_spread, 1)

            def xa(i):
                after(dve, s_pre, i + 1)
                after(dve, s_sw, i + 1 - NB)
                after(dve, s_m, i + 1 - NB)
                dve.tensor_scalar(xa_sb[:, i % NB, :], ps_pre[i % 2][:, :], w("pre_b"), k.cw[:, :],
                                  ALU.add, ALU.mult).then_inc(s_xa, 1)

            def m(i):
                after(dve, s_sig, i + 1)
                after(dve, s_xa, i + 1)
                after(dve, s_r, i + 1 - NB)
                dve.tensor_tensor(m_sb[:, i % NB, :], ps_sig[i % 2][:, :], xa_sb[:, i % NB, :], ALU.mult).then_inc(s_m, 1)

            def mask(i):
                after(dve, s_r, i + 1)
                r = r_sb[:, i % NB, :]
                dve.scalar_tensor_tensor(r, r, k.threshold[:, :], r, ALU.is_gt, ALU.max).then_inc(s_mask, 1)

            def out(i):
                after(dve, s_post, i + 1)
                if i >= NO:
                    stored.landed(dve, i - NO)
                dve.scalar_tensor_tensor(o_sb[:, i % NO, :], ps_post[i % 2][:, :], w("post_b"), l_sb[:, i % NL, :],
                                         ALU.add, ALU.add).then_inc(s_o, 1)
            skewed(n_tiles, (0, xa), (1, m), *([(2, mask), (4, out)] if last else []))
            if not last:
                after(dve, s_r, n_tiles)
                dve.tensor_reduce(total[:, :], k.resp_sum[:, :], AX.X, ALU.add).then_inc(s_thr, 1)
                after(dve, s_thr, 2)
                dve.tensor_scalar(k.threshold[:, :], k.banks[7][:, 0:1], 1.0 / (4 * NPIX), None, ALU.mult)

        @block.gpsimd
        def _(pool):
            def y(i):
                after(pool, s_mask, i + 1)
                after(pool, s_xg, i + 1)
                after(pool, s_post, i + 1 - NB)
                pool.tensor_tensor(y_sb[:, i % NB, :], xg_sb[:, i % NB, :], r_sb[:, i % NB, :], ALU.mult).then_inc(s_y, 1)
            if last:
                skewed(n_tiles, (0, y))


@phase
def project_out(k, sb):
    nc, w = k.nc, k.w
    PAIRS = 4
    per_image = H // 2 // PAIRS
    n_groups = B * per_image
    per_group = PAIRS // ROWS
    n_tiles = n_groups * per_group
    ND, NX, NO = 2, 3, 4
    g_sb = sb("g", [P, ND, PAIRS, GP])
    ghi_sb, glo_sb = sb("ghi", [P, ND, PAIRS, GP], F32R), sb("glo", [P, ND, PAIRS, GP], F32R)
    l_sb = sb("l", [P, ND, PAIRS, W])
    lsplit_sb = sb("lsplit", [P, ND, PAIRS, W], F32R)
    x_sb = sb("x", [P, NX, PAIRS, W])
    x1_sb = sb("x1", [P, NO, PAIRS, W])
    z_sb = sb("z", [P, NO, PAIRS, ZP])
    gl_in, x_in = Slots(k.sem, "gl", ND, per=4), Slots(k.sem, "x", NX, per=2)
    x1_out, z_out = Slots(k.sem, "x1o", NO), Slots(k.sem, "zo", NO)
    s_hi, s_lo, s_local_lo, s_out, s_x1, s_pad = [k.sem(n) for n in ("hi", "lo", "local_lo", "out", "x1", "pad")]
    ps_out = k.banks[5:7]
    glob, gated, x, x1, z2 = [k.dram[n] for n in ("glob", "gated", "x", "x1", "z2")]
    tile = lambda t, n, i: t[:, i // per_group % n, ROWS * (i % per_group):ROWS * (i % per_group) + ROWS, :]
    flat = lambda t: t.rearrange("p r x -> p (r x)")

    pairs = lambda t, s, width, first=0: row_pairs(t, s, per_image, PAIRS, width, first)

    def z_free(e, i):
        after(e, s_pad, 1)
        s = i // per_group
        if i % per_group == 0 and s >= NO:
            z_out.landed(e, s - NO)

    ln = Norm(sb, k.sem, k.banks[0:5], "ln", w, "ln2_w", "ln2_b", n_center=3, average=k.average[:, :],
              x_at=lambda i: flat(tile(x1_sb, NO, i)), x_ready=lambda e, i: after(e, s_x1, i + 1),
              z_at=lambda i: tile(z_sb, NO, i)[:, :, 2:2 + W], z_free=z_free)

    with nc.Block() as block:
        @block.sync
        def _(sp):
            def load(s):
                after(sp, s_lo, s - ND + 1)
                after(sp, s_local_lo, s - ND + 1)
                for m in range(2):
                    half = slice(C * m, C * m + C)
                    sp.dma_start(flat(g_sb[half, s % ND, :, :]), pairs(glob, s, GP, m)).then_inc(gl_in.sem_of(s), 16)
                    sp.dma_start(flat(l_sb[half, s % ND, :, :]), pairs(gated, s, W)).then_inc(gl_in.sem_of(s), 16)
                after(sp, s_x1, per_group * (s - NX + 1))
                rows = pixels(x, s // per_image, 1, 2 * PAIRS * (s % per_image), 2 * PAIRS).rearrange(
                    "c (r q x) -> c q r x", q=2, x=W)
                for q in range(2):
                    sp.dma_start(x_sb[C * q:C * q + C, s % NX, :, :], rows[:, q, :, :]).then_inc(x_in.sem_of(s), 16)

            def store_x(s):
                after(sp, s_x1, per_group * (s + 1))
                sp.dma_start(pairs(x1, s, W), flat(x1_sb[:, s % NO, :, :])).then_inc(x1_out.sem_of(s), 16)

            def store_z(s):
                after(sp, ln.s_z, per_group * (s + 1))
                sp.dma_start(pairs(z2, s, ZP, 1), flat(z_sb[:, s % NO, :, :])).then_inc(z_out.sem_of(s), 16)
            skewed(n_groups, (0, load), (3, store_x), (4, store_z))
            x1_out.all_landed(sp, n_groups)
            z_out.all_landed(sp, n_groups)

        @block.tensor
        def _(pe):
            def out(i):
                s = i // per_group
                b = s // per_image
                after(pe, s_lo, s + 1)
                after(pe, s_local_lo, s + 1)
                after(pe, s_x1, i - 1)
                bank = ps_out[i % 2].rearrange("p (r x) -> p r x", x=W)
                parts = tile(lsplit_sb, ND, i)
                pe.matmul(bank, k.out_local_hi[:, :], parts, start=True, stop=False)
                pe.matmul(bank, k.out_local_lo[:, :], parts, start=False, stop=False)
                for dx in range(3):
                    hi, lo = [tile(t, ND, i)[:, :, dx:dx + W] for t in (ghi_sb, glo_sb)]
                    pe.matmul(bank, k.out_hi[:, b, dx, :], hi, start=False, stop=False)
                    pe.matmul(bank, k.out_hi[:, b, dx, :], lo, start=False, stop=False)
                    last = pe.matmul(bank, k.out_lo[:, b, dx, :], hi, start=False, stop=(dx == 2))
                last.then_inc(s_out, 1)
            skewed(n_tiles, (4, lambda i: ln.variance(pe, i)), (2, lambda i: ln.center(pe, i)), (0, out))

        @block.scalar
        def _(act):
            act.preload_act_table_set(LOG_EXP)

            def split(i):
                s = i // per_group + 1
                if i % per_group == 0 and s < n_groups:
                    hi(s)

            def hi(s):
                gl_in.landed(act, s)
                after(act, s_out, per_group * (s - ND + 1))
                act.activation(ghi_sb[:, s % ND, :, :], g_sb[:, s % ND, :, :], ACT.Copy)
                act.activation(lsplit_sb[:, s % ND, :, :], l_sb[:, s % ND, :, :], ACT.Copy).then_inc(s_hi, 1)
            hi(0)
            skewed(n_tiles, (4, lambda i: ln.rstd(act, i)), (2, lambda i: ln.square(act, i)), (0, split))

        @block.gpsimd
        def _(pool):
            def split(i):
                s = i // per_group + 1
                if i % per_group == 0 and s < n_groups:
                    lo(s)

            def lo(s):
                after(pool, s_hi, s + 1)
                pool.tensor_tensor(glo_sb[:, s % ND, :, :], g_sb[:, s % ND, :, :], ghi_sb[:, s % ND, :, :].bitcast(F32),
                                   ALU.subtract).then_inc(s_lo, 1)
            lo(0)
            skewed(n_tiles, (4, lambda i: ln.affine(pool, i)), (2, lambda i: ln.square_lo(pool, i)), (0, split))

        @block.vector
        def _(dve):
            dve.memset(z_sb[:, :, :, :], 0.0).then_inc(s_pad, 1)

            def x1_tile(i):
                s = i // per_group
                after(dve, s_out, i + 1)
                after(dve, ln.s_center, per_group * (s - NO + 1))
                x_in.landed(dve, s)
                if i % per_group == 0 and s >= NO:
                    x1_out.landed(dve, s - NO)
                dve.tensor_tensor(flat(tile(x1_sb, NO, i)), ps_out[i % 2], flat(tile(x_sb, NX, i)), ALU.add).then_inc(s_x1, 1)

            def split(i):
                s = i // per_group + 1
                if i % per_group == 0 and s < n_groups:
                    local_lo(s)

            def local_lo(s):
                after(dve, s_hi, s + 1)
                part = lsplit_sb[C:P, s % ND, :, :]
                dve.tensor_tensor(part, l_sb[C:P, s % ND, :, :], part.bitcast(F32), ALU.subtract).then_inc(s_local_lo, 1)
            local_lo(0)
            skewed(n_tiles, (4, lambda i: ln.scale(dve, i)), (0, x1_tile), (0, split))


@phase
def conv_ffn(k, sb):
    nc, w = k.nc, k.w
    SR = PATCH
    n_strips = B * H // SR
    per_image = H // SR
    n_sub = STRIP_PAIRS // ROWS
    n_pairs = SHIFTED + STRIP_PAIRS
    NZ, NX, NO = 2, 2, 2
    HW2 = W // 2
    GX = 4 * PATCH
    n_groups = W // GX
    z_sb = sb("z", [P, NZ, n_pairs, ZP])
    hi_sb = sb("hi", [P, NZ, n_pairs, ZP], F32R)
    lo_sb = sb("lo", [P, NZ, n_pairs, ZP], F32R)
    gelu_sb = sb("gelu", [P, 2, TILE])
    h_sb = sb("h", [P, 2, 2, n_groups, STRIP_PAIRS, GX])
    yhi_sb, ylo_sb = [sb(n, [P, 2, n_groups, 2, C], F32R) for n in ("yhi", "ylo")]
    dft_hi, dft_lo = sb("dft_hi", [P, 4 * P], F32R), sb("dft_lo", [P, 4 * P], F32R)
    f_sb = sb("f", [P, 2, n_groups // 2, 2, 2, C])
    x_sb = sb("x", [P, NX, SR, HW2])
    o_sb = sb("o", [P, NO, SR, HW2])
    z_in = Slots(k.sem, "z", NZ, per=3)
    x_in = Slots(k.sem, "x", NX, per=4)
    stored = Slots(k.sem, "stored", NO, per=2)
    s_dft, s_hi, s_lo, s_conv, s_gelu, s_h, s_y, s_yhi, s_ylo, s_f, s_fw, s_back, s_o = [
        k.sem(n) for n in ("dft", "hi", "lo", "conv", "gelu", "h", "y", "yhi", "ylo", "f", "fw", "back", "o")]
    ps_conv, ps_y, ps_f, ps_back = k.banks[0:4], k.banks[4], k.banks[5], k.banks[6:8]
    z2, x1, x2 = k.dram["z2"], k.dram["x1"], k.dram["x2"]
    halves = lambda t, s, m: t[s // per_image].rearrange("c (r x) -> c r x", x=W)[
        :, SR * (s % per_image):SR * (s % per_image) + SR, HW2 * m:HW2 * m + HW2]

    with nc.Block() as block:
        @block.sync
        def _(sp):
            def load_z(s):
                src = by_parity(z2[s // per_image:s // per_image + 1], ZP)[0]
                r = STRIP_PAIRS * (s % per_image)
                after(sp, s_lo, s - NZ + 1)
                sp.dma_start(z_sb[:, s % NZ, 0:SHIFTED, :].rearrange("p r x -> p (r x)"),
                             src[:, :, r:r + SHIFTED, :].rearrange("c q r x -> q c (r x)")).then_inc(z_in.sem_of(s), 16)
                for q in range(2):
                    first = r + 2 - 2 * q
                    sp.dma_start(z_sb[C * q:C * q + C, s % NZ, SHIFTED:n_pairs, :], src[:, q, first:first + STRIP_PAIRS, :]
                                 ).then_inc(z_in.sem_of(s), 16)

            def load_x(s):
                after(sp, s_o, 2 * (s - NX + 1))
                src = by_parity(x1[s // per_image:s // per_image + 1], W)[0]
                r = STRIP_PAIRS * (s % per_image)
                for m in range(2):
                    for q in range(2):
                        sp.dma_start(x_sb[C * m:C * m + C, s % NX, q:SR - 1 + q:2, :],
                                     src[:, q, r:r + STRIP_PAIRS, HW2 * m:HW2 * m + HW2]).then_inc(x_in.sem_of(s), 16)

            def store(s):
                after(sp, s_o, 2 * (s + 1))
                for m in range(2):
                    sp.dma_start(halves(x2, s, m), o_sb[C * m:C * m + C, s % NO, :, :]).then_inc(stored.sem_of(s), 16)
            skewed(n_strips, (0, load_z), (1, load_x), (3, store))
            stored.all_landed(sp, n_strips)

        def rounds(tile_part, filter_piece):
            for s in range(n_strips + 1):
                for m in range(4 * n_sub):
                    if s < n_strips:
                        tile_part(n_sub * s + m // 4, m % 4)
                    if s > 0:
                        filter_piece(s - 1, m)

        @block.tensor
        def _(pe):
            def conv(i, part):
                s, j = i // n_sub, ROWS * (i % n_sub)
                after(pe, s_lo, s + 1)
                if part < 2:
                    after(pe, s_gelu, 2 * (i - 1) + part + 1)
                else:
                    after(pe, s_h, 2 * (i - 1) + part - 1)
                out = ps_conv[part][:, :].rearrange("p (r x) -> p r x", x=W)
                mine = [n for n, c in enumerate(CONV_MATRICES) if c[0] == part]
                for n in mine:
                    _, pair, dx, _ = CONV_MATRICES[n]
                    x0 = dx + (part < 3)
                    z = lambda t: t[:, s % NZ, pair + j:pair + j + ROWS, x0:x0 + W]
                    pe.matmul(out, k.conv_hi[:, n, :], z(hi_sb), start=(n == mine[0]), stop=False)
                    pe.matmul(out, k.conv_hi[:, n, :], z(lo_sb), start=False, stop=False)
                    last = pe.matmul(out, k.conv_lo[:, n, :], z(hi_sb), start=False, stop=(n == mine[-1]))
                last.then_inc(s_conv, 1)

            def project(s, half):
                after(pe, s_h, 2 * n_sub * (s + 1))
                after(pe, s_ylo, 2 * s + half)
                for g in range(4):
                    for part in range(2):
                        last = pe.matmul(ps_y[:, P * g:P * g + P], h_sb[:, s % 2, part, 4 * half + g, :, :],
                                         w(f"ffn_outT{part}"), start=(part == 0), stop=(part == 1))
                last.then_inc(s_y, 1)

            def frequencies(s, q):
                after(pe, s_ylo, 2 * (s + 1))
                after(pe, s_fw, 2 * s + q)
                bank = ps_f[:, :].rearrange("p (g c) -> p g c", c=C)
                for p in range(2):
                    cols = slice(P * (2 * p + q), P * (2 * p + q) + P)
                    hi, lo = yhi_sb[:, s % 2, :, p, :], ylo_sb[:, s % 2, :, p, :]
                    pe.matmul(bank, dft_hi[:, cols], hi, start=(p == 0), stop=False)
                    pe.matmul(bank, dft_hi[:, cols], lo, start=False, stop=False)
                    last = pe.matmul(bank, dft_lo[:, cols], hi, start=False, stop=(p == 1))
                last.then_inc(s_f, 1)

            def back(s, half):
                after(pe, s_fw, 2 * (s + 1))
                after(pe, s_o, 2 * (s - 1) + half + 1)
                for g in range(4):
                    n = 4 * half + g
                    last = pe.matmul(ps_back[half][:, P * g:P * g + P], f_sb[:, s % 2, n // 2, n % 2, :, :],
                                     w("idft"), start=True, stop=True)
                last.then_inc(s_back, 1)

            def piece(s, m):
                if m < 2:
                    project(s, m)
                elif m < 4:
                    frequencies(s, m - 2)
                elif m < 6:
                    back(s, m - 4)
            after(pe, s_dft, 2)
            rounds(conv, piece)

        @block.scalar
        def _(act):
            def split(s):
                z_in.landed(act, s)
                after(act, s_conv, 4 * n_sub * (s - NZ + 1))
                act.activation(hi_sb[:, s % NZ, :, :], z_sb[:, s % NZ, :, :], ACT.Copy).then_inc(s_hi, 1)

            def gelu(i, part):
                if part < 2:
                    after(act, s_conv, 4 * i + part + 1)
                    after(act, s_h, 2 * (i - 1) + part + 1)
                    act.activation(gelu_sb[:, part, :], ps_conv[part][:, :], ACT.Gelu).then_inc(s_gelu, 1)
                elif part == 2 and i % n_sub == 0 and i // n_sub + 1 < n_strips:
                    split(i // n_sub + 1)

            def y_hi(s, half):
                if half < 2:
                    after(act, s_y, 2 * s + half + 1)
                    after(act, s_f, 2 * (s - 1))
                    act.activation(yhi_sb[:, s % 2, 4 * half:4 * half + 4, :, :],
                                   ps_y[:, :].rearrange("p (g q c) -> p g q c", g=4, q=2), ACT.Copy).then_inc(s_yhi, 1)
            act.activation(dft_hi[:, :], w("dft"), ACT.Copy).then_inc(s_dft, 1)
            split(0)
            rounds(gelu, y_hi)

        @block.gpsimd
        def _(pool):
            for s in range(n_strips):
                after(pool, s_hi, s + 1)
                after(pool, s_conv, 4 * n_sub * (s - NZ + 1))
                pool.tensor_tensor(lo_sb[:, s % NZ, :, :], z_sb[:, s % NZ, :, :], hi_sb[:, s % NZ, :, :].bitcast(F32),
                                   ALU.subtract).then_inc(s_lo, 1)

        @block.vector
        def _(dve):
            def hidden(i, part):
                if part < 2:
                    return
                s, j, part = i // n_sub, ROWS * (i % n_sub), part - 2
                after(dve, s_conv, 4 * i + 2 + part + 1)
                after(dve, s_gelu, 2 * i + part + 1)
                after(dve, s_y, 2 * (s - 1))
                grouped = lambda t: t.rearrange("p (r g x) -> p r g x", r=ROWS, x=GX)
                dve.tensor_tensor(h_sb[:, s % 2, part, :, j:j + ROWS, :].rearrange("p g r x -> p r g x"),
                                  grouped(ps_conv[2 + part][:, :]), grouped(gelu_sb[:, part, :]), ALU.mult
                                  ).then_inc(s_h, 1)

            def y_lo(s, half):
                groups = slice(4 * half, 4 * half + 4)
                after(dve, s_yhi, 2 * s + half + 1)
                dve.tensor_tensor(ylo_sb[:, s % 2, groups, :, :], ps_y[:, :].rearrange("p (g q c) -> p g q c", g=4, q=2),
                                  yhi_sb[:, s % 2, groups, :, :].bitcast(F32), ALU.subtract).then_inc(s_ylo, 1)

            def weigh(s, q):
                after(dve, s_f, 2 * s + q + 1)
                after(dve, s_back, 2 * (s - 1))
                weights = k.freq_w[:, :].unsqueeze(1).broadcast_to([P, n_groups // 2, C])
                for half in range(2):
                    cols = slice(half * TILE // 2, (half + 1) * TILE // 2)
                    last = dve.tensor_tensor(f_sb[:, s % 2, :, q, half, :], ps_f[:, cols].rearrange("p (g c) -> p g c", c=C),
                                             weights, ALU.mult)
                last.then_inc(s_fw, 1)

            def out(s, half):
                if half == 0:
                    x_in.landed(dve, s)
                    if s >= NO:
                        stored.landed(dve, s - NO)
                after(dve, s_back, 2 * s + half + 1)
                cols = slice(64 * half, 64 * half + 64)
                view = lambda t: t[:, s % 2, :, cols].rearrange("p y (g x) -> p y g x", x=16)
                dve.tensor_tensor(view(o_sb), ps_back[half][:, :].rearrange("p (g y x) -> p y g x", g=4, y=SR),
                                  view(x_sb), ALU.add).then_inc(s_o, 1)

            def piece(s, m):
                if m < 2:
                    y_lo(s, m)
                elif m < 4:
                    weigh(s, m - 2)
                elif m < 6:
                    out(s, m - 4)
            after(dve, s_dft, 1)
            dve.tensor_tensor(dft_lo[:, :], w("dft"), dft_hi[:, :].bitcast(F32), ALU.subtract).then_inc(s_dft, 1)
            rounds(hidden, piece)


LINES = 8
BLOCK = 16
BLOCKS = H // BLOCK
NCOL = P + 16


@phase
def line_attention(k, sb, name):
    nc, w = k.nc, k.w
    cols = name == "col"
    n_units = 2 * H // LINES
    n_blocks = 2 * BLOCKS
    per_block = BLOCK // LINES
    ln_w, ln_b = (w("cn_g"), w("cn_b")) if cols else (w("rn_g"), w("rn_b"))
    NX, NO, NC, NQ = 4, 2, 3, 3
    HI, LO, HI2, DEPTH = 0, 32, 64, 72
    x_sb = sb("x", [P, NX, BLOCK * W])
    o_sb = sb("o", [P, NO, BLOCK * W])
    into_sb = sb("into", [P, NCOL])
    kqg_sb, kqbias_sb = [sb(n, [P, 16]) for n in ("kqg", "kqbias")]
    bcol_sb, vg_sb, vb_sb = sb("bcol", [P, P]), sb("vg", [P, P]), sb("vb", [P, 1])
    ct_sb = sb("ct", [P, NC, 16, NCOL])
    sq_sb = sb("sq", [P, 2, 8, C])
    ss_sb = sb("ss", [P, 2, 32])
    rstd_sb = sb("rstd", [P, 2, 32])
    mul_sb, lin_sb, low_sb, exp_sb = [sb(n, [P, 256]) for n in ("mul", "lin", "low", "exp")]
    kq_sb = sb("kq", [P, 2, 16, 16])
    kr_sb = sb("kr", [P, 2, 16, 8])
    q_sb = sb("q", [P, NQ, 16, DEPTH])
    s8_sb = sb("s8", [8, 2, TILE])
    st_sb, g1_sb, g2_sb = [sb(n, [P, LINES, 8]) for n in ("st", "g1", "g2")]
    inv_sb = sb("inv", [P, 2, LINES, 16])
    g_sb = sb("gm", [P, LINES, DEPTH])
    u_sb = sb("u", [DEPTH, 2, LINES, P], F32R)
    qt_sb = sb("qt", [DEPTH, 2, TILE], F32R)
    x_in = Slots(k.sem, "x", NX)
    stored = Slots(k.sem, "stored", NO)
    names = ("fold", "folded", "zero", "ct", "ctc", "sq", "ss", "log", "rstd", "mul", "lin", "low", "exp",
             "elu", "kr", "qhi", "qlo", "sum", "inv", "S", "Sc", "ST", "STc", "V", "g1", "g2", "g", "U", "Uhi",
             "Ulo", "qt", "qtc", "app", "h")
    (s_fold, s_folded, s_zero, s_ct, s_ctc, s_sq, s_ss, s_log, s_rstd, s_mul, s_lin, s_low, s_exp,
     s_elu, s_kr, s_qhi, s_qlo, s_sum, s_inv, s_S, s_Sc, s_ST, s_STc, s_V, s_g1, s_g2, s_g, s_U, s_Uhi,
     s_Ulo, s_qt, s_qtc, s_app, s_h) = [k.sem(n) for n in names]
    ps_ct = [k.psum[:, 0:2, 0:2 * NCOL], k.psum[:, 2:4, 0:2 * NCOL]]
    ps_turn, ps_s, ps_app = k.banks[4], k.banks[5], k.banks[6:8]
    ps_sum, ps_st, ps_v = ps_turn[:, 0:P], ps_turn[:, 0:64], ps_turn[:, 0:64]

    def line(l):
        b = x_sb[:, l // BLOCK % NX, :]
        return b.rearrange("p (y x) -> p x y", x=BLOCK)[:, l % BLOCK, :] if cols else b[:, l % BLOCK * W:l % BLOCK * W + W]

    def out_line(l):
        b = o_sb[:, l // BLOCK % NO, :]
        if cols:
            return b.rearrange("p (y x) -> p x y", x=BLOCK)[:, l % BLOCK, :]
        return b.rearrange("p (b y x) -> p y b x", b=BLOCKS, x=BLOCK)[:, l % BLOCK, :, :]

    src = k.dram["h1"] if cols else k.dram["x2"]
    dst = k.dram["h2"] if cols else k.dram["h1"]

    with nc.Block() as block:
        @block.sync
        def _(sp):
            def load(n):
                p, first = n // BLOCKS, n % BLOCKS
                after(sp, s_h, 4 * per_block * (n - NX + 1))
                sp.dma_start(x_sb[:, n % NX, :], pixels(src, 2 * p, 2, BLOCK * first, BLOCK)).then_inc(x_in.sem_of(n), 16)

            def store(n):
                p, first = n // BLOCKS, n % BLOCKS
                after(sp, s_h, 4 * per_block * (n + 1))
                if cols:
                    to, of = pixels(dst, 2 * p, 2, BLOCK * first, BLOCK), o_sb[:, n % NO, :]
                else:
                    to = dst[2 * p:2 * p + 2].rearrange("b c (x n) -> (b c) x n", x=BLOCKS)[
                        :, :, BLOCK * BLOCK * first:BLOCK * BLOCK * (first + 1)]
                    of = o_sb[:, n % NO, :].rearrange("p (b n) -> p b n", b=BLOCKS)
                sp.dma_start(to, of).then_inc(stored.sem_of(n), 16)
            skewed(n_blocks, (0, load), (NX - 1, store))
            stored.all_landed(sp, n_blocks)

        def rounds(*stages):
            for r in range(n_units + 4):
                for j in range(4):
                    for lag, fn in stages:
                        if 0 <= r - lag < n_units:
                            fn(r - lag, j)

        @block.tensor
        def _(pe):
            after(pe, s_fold, 1)
            pe.matmul(ps_turn[:, 0:16], w("center"), kqg_sb[:, :], start=True, stop=True)
            pe.matmul(ps_turn[:, 16:32], bcol_sb[:, :], w(f"{name}_kqT"), start=True, stop=True)
            pe.matmul(ps_turn[:, 32:33], w(f"{name}_vT"), ln_b, start=True, stop=True).then_inc(s_folded, 1)
            after(pe, s_fold, 2)

            def turn_x(u, j):
                t = 4 * u + j
                x_in.landed(pe, u // per_block)
                after(pe, s_ctc, t - 1)
                for l in range(2):
                    for h in range(2):
                        last = pe.matmul(ps_ct[t % 2][:, l, NCOL * h:NCOL * h + NCOL],
                                         line(LINES * u + 2 * j + l)[:, P * h:P * h + P], into_sb[:, :],
                                         start=True, stop=True)
                last.then_inc(s_ct, 1)

            def turn_q(u, j):
                after(pe, s_qlo, u + 1)
                for slot, small, v in ((2, s_inv, u + 2), (3, s_STc, u + 2), (0, s_g1, u + 1)):
                    if j == slot:
                        after(pe, small, min(v + 1, n_units))
                after(pe, s_qtc, 4 * u + j)
                for g in range(4):
                    last = pe.transpose(ps_turn[0:DEPTH, P * g:P * g + P], q_sb[:, u % NQ, 4 * j + g, :], w("ident"))
                last.then_inc(s_qt, 1)

            def small(u, j):
                after(pe, s_qtc, 4 * (u - 2) + j + 1)
                if j == 1:
                    after(pe, s_elu, u + 1)
                    after(pe, s_g1, u)
                    kq = kq_sb[:, u % 2, :, :].rearrange("p (l h) c -> p l h c", h=2)
                    for h in range(2):
                        last = pe.matmul(ps_sum.rearrange("p (l c) -> p l c", c=16), w("ones"), kq[:, :, h, :],
                                         start=(h == 0), stop=(h == 1))
                    last.then_inc(s_sum, 1)
                elif j == 2:
                    after(pe, s_Sc, 2 * u + 2)
                    after(pe, s_inv, u + 1)
                    for l in range(LINES):
                        last = pe.transpose(ps_st[:, 8 * l:8 * l + 8], s8_sb[:, l // 4, P * (l % 4):P * (l % 4) + P],
                                            w("ident", slice(0, 8))[:, 0:8])
                    last.then_inc(s_ST, 1)
                elif j == 3:
                    after(pe, s_STc, u + 1)
                    pe.matmul(ps_v, vg_sb[:, :], st_sb[:, :, :].rearrange("p l c -> p (l c)"),
                              start=True, stop=True).then_inc(s_V, 1)

            def sums(u, j):
                if j < 2:
                    after(pe, s_kr, u + 1)
                    after(pe, s_Ulo, 2 * (u - 1))
                    after(pe, s_Sc, 2 * u + j)
                    for l in range(4):
                        for h in range(2):
                            n = 8 * j + 2 * l + h
                            last = pe.matmul(ps_s[0:8, P * l:P * l + P], kr_sb[:, u % 2, n, :], ct_sb[:, u % NC, n, 0:P],
                                             start=(h == 0), stop=(h == 1))
                    last.then_inc(s_S, 1)

            def matrix(u, j):
                if j >= 2:
                    half = j - 2
                    after(pe, s_g, u + 1)
                    after(pe, s_Sc, min(2 * (u + 2), 2 * n_units))
                    after(pe, s_Ulo, 2 * u + half)
                    for l in range(4):
                        last = pe.matmul(ps_s[0:DEPTH, P * l:P * l + P], g_sb[:, 4 * half + l, :], w(f"{name}_oT"),
                                         start=True, stop=True)
                    last.then_inc(s_U, 1)

            def apply(u, j):
                t = 4 * u + j
                after(pe, s_qtc, t + 1)
                after(pe, s_Ulo, 2 * u + j // 2 + 1)
                after(pe, s_h, t - 1)
                for m in range(2):
                    last = pe.matmul(ps_app[t % 2][:, W * m:W * m + W], u_sb[:, u % 2, 2 * j + m, :],
                                     qt_sb[:, t % 2, W * m:W * m + W], start=True, stop=True)
                last.then_inc(s_app, 1)

            rounds((4, turn_q), (0, turn_x), (2, small), (2, sums), (3, matrix), (4, apply))

        @block.scalar
        def _(act):
            act.preload_act_table_set(LOG_EXP)

            def u_hi(u, j):
                if j >= 2:
                    half = j - 2
                    after(act, s_U, 2 * u + half + 1)
                    after(act, s_app, 4 * (u - 1))
                    act.activation(u_sb[:, u % 2, 4 * half:4 * half + 4, :], ps_s[0:DEPTH, :].rearrange("p (l c) -> p l c", l=4),
                                   ACT.Copy).then_inc(s_Uhi, 1)

            def copy_ct(u, j):
                t = 4 * u + j
                after(act, s_ct, t + 1)
                after(act, s_S, 2 * (u - NC + 1))
                act.activation(ct_sb[:, u % NC, 4 * j:4 * j + 4, :].rearrange("p (l h) c -> p l (h c)", l=2),
                               ps_ct[t % 2], ACT.Copy).then_inc(s_ctc, 1)

            def copy_qt(u, j):
                t = 4 * u + j
                after(act, s_qt, t + 1)
                after(act, s_app, t - 1)
                act.activation(qt_sb[:, t % 2, :], ps_turn[0:DEPTH, :], ACT.Copy).then_inc(s_qtc, 1)

            def kq(u, j):
                if j == 0:
                    r = rstd_sb[:, u % 2, :]
                    after(act, s_ss, 4 * (u + 1))
                    after(act, s_kr, u - 1)
                    act.activation(r, ss_sb[:, u % 2, :], ACT.Ln, scale=1.0 / C, bias=w("eps")).then_inc(s_log, 1)
                    after(act, s_log, u + 1)
                    act.activation(r, r, ACT.Exp, scale=-0.5).then_inc(s_rstd, 1)
                elif j == 2:
                    after(act, s_low, u + 1)
                    after(act, s_elu, u)
                    act.activation(exp_sb[:, :], low_sb[:, :], ACT.Exp).then_inc(s_exp, 1)
                elif j == 3:
                    after(act, s_elu, u + 1)
                    after(act, s_qt, 4 * (u - NQ + 1))
                    for at in (HI, HI2):
                        last = act.activation(q_sb[:, u % NQ, :, at:at + 8].bitcast(F32R), kq_sb[:, u % 2, :, 8:16], ACT.Copy)
                    last.then_inc(s_qhi, 1)

            def copy_s(u, j):
                if j < 2:
                    after(act, s_S, 2 * u + j + 1)
                    after(act, s_ST, u)
                    act.activation(s8_sb[:, j, :], ps_s[0:8, :], ACT.Copy).then_inc(s_Sc, 1)
            after(act, s_zero, 2)
            rounds((4, copy_qt), (0, copy_ct), (1, kq), (2, copy_s), (3, u_hi))

        @block.gpsimd
        def _(pool):
            def squares(u, j):
                t = 4 * u + j
                after(pool, s_ctc, t + 1)
                after(pool, s_ss, t - 1)
                ct = ct_sb[:, u % NC, 4 * j:4 * j + 4, 0:P]
                pool.tensor_tensor(sq_sb[:, t % 2, :, :].rearrange("p (n m) c -> p n (m c)", m=2), ct, ct, ALU.mult
                                   ).then_inc(s_sq, 1)

            def linear(u, j):
                if j == 0:
                    after(pool, s_rstd, u + 1)
                    after(pool, s_lin, u)
                    for kind in range(2):
                        split = lambda t: t.rearrange("p n (m h) -> p n m h", m=2)
                        last = pool.tensor_tensor(
                            split(mul_sb[:, :].rearrange("p (n c) -> p n c", c=16)[:, :, 8 * kind:8 * kind + 8]),
                            split(ct_sb[:, u % NC, :, P + 8 * kind:P + 8 * kind + 8]),
                            rstd_sb[:, u % 2, :].rearrange("p (n m) -> p n m", m=2).unsqueeze(3).broadcast_to([P, 16, 2, HEADS]),
                            ALU.mult)
                        last.then_inc(s_mul, 1)
                    after(pool, s_mul, 2 * (u + 1))
                    after(pool, s_elu, u)
                    pool.tensor_tensor(lin_sb[:, :].rearrange("p (n c) -> p n c", c=16),
                                       mul_sb[:, :].rearrange("p (n c) -> p n c", c=16),
                                       kqbias_sb[:, :].unsqueeze(1).broadcast_to([P, 16, 16]), ALU.add).then_inc(s_lin, 1)
            after(pool, s_fold, 2)
            rounds((0, squares), (1, linear))

        @block.vector
        def _(dve):
            dve.memset(g_sb[:, :, :], 0.0).then_inc(s_zero, 1)
            dve.memset(q_sb[:, :, :, :], 0.0).then_inc(s_zero, 1)
            dve.tensor_copy(into_sb[:, 0:P], w("center"))
            dve.tensor_scalar(kqg_sb[:, :], w(f"{name}_kqT"), ln_w, None, ALU.mult)
            dve.tensor_scalar(vg_sb[:, :], w(f"{name}_vT"), ln_w, None, ALU.mult)
            dve.tensor_scalar(bcol_sb[:, :], w("ones"), ln_b, None, ALU.mult).then_inc(s_fold, 1)
            after(dve, s_folded, 1)
            dve.tensor_copy(into_sb[:, P:NCOL], ps_turn[:, 0:16])
            dve.tensor_tensor(kqbias_sb[:, :], ps_turn[:, 16:32], w(f"{name}_kqb"), ALU.add)
            dve.tensor_tensor(vb_sb[:, :], ps_turn[:, 32:33], w(f"{name}_bv"), ALU.add).then_inc(s_fold, 1)
            after(dve, s_zero, 2)
            after(dve, s_fold, 2)

            def u_lo(u, j):
                if j >= 2:
                    half = j - 2
                    rows = slice(HI2, DEPTH)
                    u_part = u_sb[rows, u % 2, 4 * half:4 * half + 4, :]
                    after(dve, s_Uhi, 2 * u + half + 1)
                    dve.tensor_tensor(u_part, ps_s[rows, :].rearrange("p (l c) -> p l c", l=4), u_part.bitcast(F32),
                                      ALU.subtract).then_inc(s_Ulo, 1)

            def variance(u, j):
                t = 4 * u + j
                after(dve, s_sq, t + 1)
                after(dve, s_log, u - 1)
                dve.tensor_reduce(ss_sb[:, u % 2, 8 * j:8 * j + 8], sq_sb[:, t % 2, :, :], AX.X, ALU.add).then_inc(s_ss, 1)

            def kq(u, j):
                if j == 1:
                    after(dve, s_lin, u + 1)
                    after(dve, s_exp, u)
                    dve.tensor_scalar(low_sb[:, :], lin_sb[:, :], 0.0, None, ALU.min).then_inc(s_low, 1)
                elif j == 2:
                    after(dve, s_exp, u + 1)
                    after(dve, s_sum, u - 1)
                    dve.scalar_tensor_tensor(kq_sb[:, u % 2, :, :].rearrange("p n c -> p (n c)"), lin_sb[:, :], 0.0,
                                             exp_sb[:, :], ALU.max, ALU.add).then_inc(s_elu, 1)
                    after(dve, s_elu, u + 1)
                    after(dve, s_S, 2 * (u - 1))
                    split = lambda t: t.rearrange("p n (m h) -> p n m h", m=2)
                    dve.tensor_tensor(split(kr_sb[:, u % 2, :, :]), split(kq_sb[:, u % 2, :, 0:8]),
                                      rstd_sb[:, u % 2, :].rearrange("p (n m) -> p n m", m=2).unsqueeze(3)
                                      .broadcast_to([P, 16, 2, HEADS]), ALU.mult).then_inc(s_kr, 1)
                elif j == 3:
                    q = q_sb[:, u % NQ, :, :]
                    after(dve, s_qhi, u + 1)
                    dve.tensor_tensor(q[:, :, LO:LO + 8], kq_sb[:, u % 2, :, 8:16], q[:, :, HI:HI + 8], ALU.subtract
                                      ).then_inc(s_qlo, 1)

            def small(u, j):
                if j == 1:
                    after(dve, s_sum, u + 1)
                    dve.reciprocal(inv_sb[:, u % 2, :, :], ps_sum.rearrange("p (l c) -> p l c", c=16)).then_inc(s_inv, 1)
                elif j == 2:
                    after(dve, s_ST, u + 1)
                    dve.tensor_copy(st_sb[:, :, :], ps_st.rearrange("p (l c) -> p l c", c=8)).then_inc(s_STc, 1)
                elif j == 3:
                    after(dve, s_V, u + 1)
                    after(dve, s_inv, u + 1)
                    after(dve, s_g2, u)
                    dve.tensor_tensor(g1_sb[:, :, :], ps_v.rearrange("p (l c) -> p l c", c=8), inv_sb[:, u % 2, :, 0:8],
                                      ALU.mult).then_inc(s_g1, 1)

            def weights(u, j):
                if j == 0:
                    after(dve, s_g1, u + 1)
                    dve.scalar_tensor_tensor(g2_sb[:, :, :], g1_sb[:, :, :], vb_sb[:, :], inv_sb[:, u % 2, :, 8:16], ALU.add,
                                             ALU.mult).then_inc(s_g2, 1)
                    after(dve, s_g2, u + 1)
                    after(dve, s_U, 2 * u)
                    for at in (HI, LO, HI2):
                        last = dve.tensor_tensor(g_sb[:, :, at:at + 8], g2_sb[:, :, :],
                                                 w("head_w").unsqueeze(1).broadcast_to([P, LINES, 8]), ALU.mult)
                    last.then_inc(s_g, 1)

            def result(u, j):
                t, l = 4 * u + j, LINES * u + 2 * j
                if l % BLOCK == 0 and l // BLOCK >= NO:
                    stored.landed(dve, l // BLOCK - NO)
                after(dve, s_app, t + 1)
                form = (lambda v: v) if cols else (lambda v: v.rearrange("p (b x) -> p b x", x=BLOCK))
                for m in range(2):
                    last = dve.scalar_tensor_tensor(out_line(l + m), form(ps_app[t % 2][:, W * m:W * m + W]),
                                                    w(f"{name}_bo"), form(line(l + m)), ALU.add, ALU.add)
                last.then_inc(s_h, 1)

            rounds((3, weights), (2, small), (1, kq), (0, variance), (3, u_lo), (4, result))


@phase
def ffn(k, sb):
    nc, w = k.nc, k.w
    SR = 4 * TILE // W
    n_units = 2 * NPIX // TILE // 4
    per_pair = NPIX // TILE // 4
    NX, NO = 4, OUT_SLOTS
    AHEAD = 2
    x_sb = sb("x", [P, NX, 4 * TILE])
    z_sb = sb("z", [P, 2, 4 * TILE])
    lo_sb = sb("lo", [P, 2, 4 * TILE], F32R)
    stack_sb = sb("stack", [P, 2, 2, 4 * TILE], F32R)
    w1_hi, w1_lo, w1_rest = sb("w1_hi", [P, 256], F32R), sb("w1_lo", [P, 2, 256], F32R), sb("w1_rest", [P, 256])
    hid_sb = sb("hid", [P, 4, TILE])
    o_sb = sb("o", [P, NO, 4 * TILE])
    x_in, stacked, stored = Slots(k.sem, "x", NX), Slots(k.sem, "stacked", 2, per=2), k.out_stored
    s_w1, s_hi, s_lo, s_hid, s_gelu, s_out, s_o = [k.sem(n) for n in ("w1", "hi", "lo", "hid", "gelu", "out", "o")]
    image = lambda m: slice(C * m, C * m + C)
    ps_hid, ps_out = k.banks[4:6], k.banks[6:8]
    h2, out = k.dram["h2"], k.dram["out"]
    at = lambda t, i, n: t[:, i // 4 % n, i % 4 * TILE:i % 4 * TILE + TILE]
    ln = Norm(sb, k.sem, k.banks[0:6], "ln", w, "fn_g", "fn_b",
              x_at=lambda i: at(x_sb, i, NX), x_ready=lambda e, i: x_in.landed(e, i // 4),
              z_at=lambda i: at(z_sb, i, 2), z_free=lambda e, i: after(e, s_lo, 2 * (i // 4)), n_center=4)

    with nc.Block() as block:
        @block.sync
        def _(sp):
            def load(u):
                after(sp, s_o, 4 * (u - NX + 1))
                h = h2[2 * (u // per_pair):2 * (u // per_pair) + 2].rearrange("b c (x n) -> (b c) x n", x=BLOCKS)
                n = SR * BLOCK
                sp.dma_start(x_sb[:, u % NX, :].rearrange("p (b n) -> p b n", b=BLOCKS),
                             h[:, :, n * (u % per_pair):n * (u % per_pair) + n]).then_inc(x_in.sem_of(u), 16)

            def store(u):
                after(sp, s_o, 4 * (u + 1))
                sp.dma_start(pixels(out, 2 * (u // per_pair), 2, SR * (u % per_pair), SR), o_sb[:, u % NO, :]
                             ).then_inc(stored.sem_of(u), 16)

            def stack(u):
                after(sp, s_lo, 2 * (u + 1))
                for m in range(2):
                    sp.dma_start(stack_sb[image(1 - m), u % 2, m, :].bitcast(F32), lo_sb[image(m), u % 2, :].bitcast(F32)).then_inc(stacked.sem_of(u), 16)
            skewed(n_units, (0, load), (NX, store), (2, stack))
            stored.all_landed(sp, n_units)

        def rounds(work, center, rest):
            for u in range(-AHEAD, n_units):
                for j in range(4):
                    if u >= 0:
                        work(4 * u + j)
                    if u + AHEAD < n_units:
                        center(4 * (u + AHEAD) + j)
                rest(u)

        @block.tensor
        def _(pe):
            def first(c):
                i, n = c // 4, c % 4
                m, cols = n % 2, slice(P * (n // 2), P * (n // 2) + P)
                stacked.landed(pe, i // 4)
                after(pe, s_hi, i // 4 + 1)
                after(pe, s_gelu, c - 1)
                if c % 16 < 2:
                    after(pe, ln.s_log, min(4 * (i // 4 + AHEAD) - 1 + c % 2, 4 * n_units))
                z = stack_sb[:, i // 4 % 2, m, i % 4 * TILE:i % 4 * TILE + TILE]
                pe.matmul(ps_hid[c % 2][:, :], w1_hi[:, cols], z, start=True, stop=False)
                pe.matmul(ps_hid[c % 2][:, :], w1_lo[:, m, cols], z, start=False, stop=True).then_inc(s_hid, 1)

            def second(c):
                i, n = c // 4, c % 4
                m = n % 2
                after(pe, s_gelu, c + 1)
                if n == 0:
                    after(pe, s_o, i - 1)
                pe.matmul(ps_out[i % 2][C * m:C * m + C, :], w("w2T")[:, C * (n // 2):C * (n // 2) + C],
                          hid_sb[:, c % 4, :], start=(n // 2 == 0), stop=(n // 2 == 1)).then_inc(s_out, 1)

            def work(i):
                for c in (4 * i, 4 * i + 2):
                    first(c)
                    first(c + 1)
                    if c % 16 >= 2:
                        second(c - 2)
                        second(c - 1)

            def rest(u):
                def variance(j):
                    if u + AHEAD < n_units:
                        after(pe, s_gelu, 16 * u + 15 + j % 2)
                        ln.variance(pe, 4 * (u + AHEAD) + j)
                variance(0)
                variance(1)
                if u >= 0:
                    second(16 * u + 14)
                    second(16 * u + 15)
                variance(2)
                variance(3)
            after(pe, s_w1, 3)
            rounds(work, lambda i: ln.center(pe, i), rest)

        @block.scalar
        def _(act):
            def gelu(c):
                n = c % 4
                after(act, s_hid, c + 1)
                after(act, s_out, c - 3)
                act.activation(hid_sb[:, c % 4, :], ps_hid[c % 2][:, :], ACT.Gelu, bias=w("b1")[:, n // 2:n // 2 + 1]
                               ).then_inc(s_gelu, 1)

            def rest(u):
                if u + AHEAD < n_units:
                    act.preload_act_table_set(LOG_EXP)
                    for j in range(4):
                        ln.rstd(act, 4 * (u + AHEAD) + j)
            rounds(lambda i: [gelu(c) for c in range(4 * i, 4 * i + 4)], lambda i: ln.square(act, i), rest)

        @block.gpsimd
        def _(pool):
            for u in range(n_units):
                for i in range(4 * u, 4 * u + 4):
                    ln.affine(pool, i)
                for m in range(2):
                    after(pool, ln.s_z, 4 * (u + 1))
                    after(pool, s_lo, 2 * u + m)
                    after(pool, s_hi, u + 1)
                    if u >= 2:
                        stacked.landed(pool, u - 2)
                    pool.tensor_tensor(lo_sb[image(m), u % 2, :], z_sb[image(m), u % 2, :],
                                       stack_sb[image(m), u % 2, m, :].bitcast(F32), ALU.subtract).then_inc(s_lo, 1)

        @block.vector
        def _(dve):
            dve.tensor_copy(w1_hi[:, :], w("w1T")).then_inc(s_w1, 1)
            after(dve, s_w1, 1)
            dve.tensor_tensor(w1_rest[:, :], w("w1T"), w1_hi[:, :].bitcast(F32), ALU.subtract).then_inc(s_w1, 1)
            after(dve, s_w1, 2)
            dve.tensor_scalar(w1_lo[:, 0, :], w1_rest[:, :], w("first_half"), None, ALU.mult)
            dve.tensor_scalar(w1_lo[:, 1, :], w1_rest[:, :], w("last_half"), None, ALU.mult).then_inc(s_w1, 1)

            def hi(u):
                after(dve, ln.s_z, 4 * (u + 1))
                after(dve, s_hid, 16 * (u - 1))
                for m in range(2):
                    last = dve.tensor_copy(stack_sb[image(m), u % 2, m, :], z_sb[image(m), u % 2, :])
                last.then_inc(s_hi, 1)

            def work(i):
                if i % 4 == 1 and i // 4 + 1 < n_units:
                    hi(i // 4 + 1)
                if i % 4 == 0 and i // 4 >= NO:
                    stored.landed(dve, i // 4 - NO)
                after(dve, s_out, 4 * (i + 1))
                blocks = lambda t: t.rearrange("p (b y x) -> p b y x", y=SR, x=BLOCK)
                o = o_sb[:, i // 4 % NO, :].rearrange("p (y b x) -> p b y x", y=SR, x=BLOCK)
                for b in range(4):
                    last = dve.scalar_tensor_tensor(o[:, i % 4 * 4 + b, :, :], blocks(ps_out[i % 2][:, :])[:, b, :, :], w("b2"),
                                                    blocks(at(x_sb, i, NX))[:, b, :, :], ALU.add, ALU.add)
                last.then_inc(s_o, 1)

            def rest(u):
                if u + AHEAD < n_units:
                    for j in range(4):
                        ln.scale(dve, 4 * (u + AHEAD) + j)
                if u == -AHEAD:
                    hi(0)
            rounds(work, lambda i: None, rest)


SCRATCH = {
    "local": NPIX, "glob": 2 * GPAIRS * GP, "gated": NPIX, "x1": NPIX, "z2": 2 * ZPAIRS * ZP,
    "x2": NPIX, "h1": NPIX, "h2": NPIX,
}
CHANNELS = {"local": HALF, "glob": HALF, "gated": HALF}
PHASES = [(set_up,), (project_in,), (gram,), (attention_weights,), (local_branch, False), (local_branch, True),
          (project_out,), (conv_ffn,), (line_attention, "row"), (line_attention, "col"), (ffn,)]


def build(nc, x, packed, where, out, phases=PHASES, scratch_kind=None):
    with ExitStack() as ctx:
        dram = {"x": x, "out": out}
        for name, n in SCRATCH.items():
            kind = (scratch_kind or {}).get(name, "Internal")
            dram[name] = nc.dram_tensor(f"scratch_{name}", [B, CHANNELS.get(name, C), n], F32, kind=kind).ap()
        k = Program(nc, ctx, where, packed, dram)
        with ExitStack() as ctx0:
            k.layer0(ctx0)
            layer = 0
            for fn, *args in phases:
                if fn in (line_attention, ffn) and layer == 0:
                    layer = 1
                    ctx0.close()
                    k.reuse_semaphores()
                fn(k, *args)
        return k


def lay_out(inputs):
    pieces = laid_out(inputs)
    where, at = {}, 0
    for name, piece in pieces.items():
        where[name] = (at, at + piece.shape[1])
        at += piece.shape[1]
    return where, np.ascontiguousarray(np.concatenate(list(pieces.values()), 1))


def kernel(**inputs):
    import concourse.bacc as bacc
    from concourse.bass_utils import run_bass_kernel_spmd

    inputs = {name: np.asarray(v) for name, v in inputs.items()}
    x = np.ascontiguousarray(inputs["x"]).reshape(B, C, NPIX)
    where, packed = lay_out(inputs)
    nc = bacc.Bacc("TRN2", target_bir_lowering=False, num_devices=1)
    x_d = nc.dram_tensor("x", x.shape, F32, kind="ExternalInput").ap()
    w_d = nc.dram_tensor("weights", packed.shape, F32, kind="ExternalInput").ap()
    out_d = nc.dram_tensor("out", x.shape, F32, kind="ExternalOutput").ap()
    build(nc, x_d, w_d, where, out_d)
    r = run_bass_kernel_spmd(nc, [{"x": x, "weights": packed}], core_ids=[0])
    return r.results[0]["out"].reshape(B, C, H, W)
```
